# Optimizing a Trainium2 kernel written in Bass

```python
import numpy as np
import jax
import jax.numpy as jnp

def _softmax(x, axis=-1):
    return jax.nn.softmax(x, axis=axis)

def _gelu(x):
    return jax.nn.gelu(x, approximate=True)

def _silu(x):
    return jax.nn.silu(x)

def _sigmoid(x):
    return jax.nn.sigmoid(x)

def _layernorm(x, axis=-1, eps=1e-05):
    m = jnp.mean(x, axis=axis, keepdims=True)
    v = jnp.var(x, axis=axis, keepdims=True)
    return (x - m) / jnp.sqrt(v + eps)

def _scatter_add(tgt, idx, src, axis=0):
    return tgt.at[idx].add(src)

def _segment_sum(src, seg, n):
    return jax.ops.segment_sum(src, seg, n)
kernel_name = 'mk_flamingo_gated_d2_seqx_r8_59600f'

def setup_inputs(seed: int=0):
    np.random.seed(seed)
    _w = jnp.asarray

    def _rec_inputs():
        import jax
        import jax.numpy as jnp
        _rk = jax.random.key(seed)
        x = -0.001547 + 1.001 * jax.random.normal(jax.random.fold_in(_rk, 1), (16, 64, 256), jnp.float32)
        _lenS = 64 - jax.random.randint(jax.random.fold_in(_rk, 7), (16,), 0, max(1, 64 // 4) + 1, jnp.int32)
        _lenS2 = 64 - jax.random.randint(jax.random.fold_in(_rk, 8), (16,), 0, max(1, 64 // 4) + 1, jnp.int32)
        _ctx_2048P = jax.random.normal(jax.random.fold_in(_rk, 12), (16, 16, 256), jnp.float32)
        _ctx_2048c = jax.random.dirichlet(jax.random.fold_in(_rk, 512), 0.3 * jnp.ones((16,), jnp.float32), (16, 64))
        _ctx_2048t = jnp.einsum('bsk,bkd->bsd', _ctx_2048c, _ctx_2048P)
        _ctx_2048t = _ctx_2048t * jax.lax.rsqrt(jnp.mean(jnp.square(_ctx_2048t)) + 1e-12) * 0.953939
        ctx_2048 = -5.72187e-05 + 0.999849 * (_ctx_2048t + 0.3 * jax.random.normal(jax.random.fold_in(_rk, 612), (16, 64, 256), jnp.float32))
        _validS = jnp.arange(64)[None, :] < _lenS[:, None]
        _validS2 = jnp.arange(64)[None, :] < _lenS2[:, None]
        _causal = jnp.tril(jnp.ones((64, 64), dtype=bool))
        mask_BxSxS2_ff0 = jnp.where(jnp.ones((16, 64, 64), dtype=bool), 0.0, -1000000000.0).astype(jnp.float32)
        _g = jax.random.normal(jax.random.fold_in(_rk, 9001), (2, 2), jnp.float32)
        _g = jnp.sign(_g) * jnp.maximum(jnp.abs(_g), 1.0) + (_g == 0) * 1.0
        g_xattn = _g[0]
        g_ffn = _g[1]
        return (x, ctx_2048, mask_BxSxS2_ff0, g_xattn, g_ffn)
    x, ctx_2048, mask_BxSxS2_ff0, g_xattn, g_ffn = _rec_inputs()

    def _L0_xattn_setup():
        import jax, jax.numpy as jnp
        import numpy as np
        B, Q_LEN, E = (8, 16, 256)
        CACHE_LEN = 512
        key = jax.random.key(seed)
        ks = jax.random.split(key, 9)
        s = 1.0 / np.sqrt(E)
        return {'x': jax.random.normal(ks[0], (B, Q_LEN, E), jnp.float32), 'attention_mask': jnp.zeros((B, Q_LEN, CACHE_LEN), jnp.float32), 'k_cache': jax.random.normal(ks[1], (B, CACHE_LEN, E), jnp.float32), 'v_cache': jax.random.normal(ks[2], (B, CACHE_LEN, E), jnp.float32), 'Wq': jax.random.normal(ks[3], (E, E), jnp.float32) * s, 'bq': jax.random.normal(ks[4], (E,), jnp.float32) * s, 'Wk': jax.random.normal(ks[5], (E, E), jnp.float32) * s, 'bk': jax.random.normal(ks[6], (E,), jnp.float32) * s, 'Wv': jax.random.normal(ks[7], (E, E), jnp.float32) * s, 'bv': jax.random.normal(ks[8], (E,), jnp.float32) * s}
    _L0_xattn_all = _L0_xattn_setup()
    _L0_xattn_in = {k: v for k, v in _L0_xattn_all.items() if k in ('Wq', 'bq', 'Wk', 'bk', 'Wv', 'bv')}
    del _L0_xattn_all

    def _L0_ffn_setup():
        import jax, jax.numpy as jnp
        import numpy as np
        EPS = 1e-05
        RMS_EPS = 1e-06

        def activation_quant(x, num_bits=8):
            qn = -2 ** (num_bits - 1)
            qp = 2 ** (num_bits - 1) - 1
            xf = x.astype(jnp.float32)
            s = qp / jnp.clip(jnp.max(jnp.abs(xf), axis=-1, keepdims=True), EPS, None)
            return (jnp.clip(jnp.round(xf * s), qn, qp) / s).astype(x.dtype)

        def weight_quant(w):
            wf = w.astype(jnp.float32)
            s = 1.0 / jnp.clip(jnp.mean(jnp.abs(wf)), EPS, None)
            return (jnp.clip(jnp.round(wf * s), -1.0, 1.0) / s).astype(w.dtype)

        def bit_linear(x, w):
            qx = x + jax.lax.stop_gradient(activation_quant(x) - x)
            qw = w + jax.lax.stop_gradient(weight_quant(w) - w)
            return jnp.einsum('bsh,oh->bso', qx, qw)

        def rms_norm(x, weight, eps=RMS_EPS):
            xf = x.astype(jnp.float32)
            var = jnp.mean(xf * xf, axis=-1, keepdims=True)
            return weight * (xf * jax.lax.rsqrt(var + eps)).astype(x.dtype)
        key = jax.random.key(seed)
        k1, k2, k3, k4 = jax.random.split(key, 4)
        B, S, H, I = (2, 256, 256, 1024)
        scale = 1.0 / np.sqrt(H)
        return {'x': jax.random.normal(k1, (B, S, H), dtype=jnp.float32), 'w_gate': jax.random.normal(k2, (I, H), dtype=jnp.float32) * scale, 'w_up': jax.random.normal(k3, (I, H), dtype=jnp.float32) * scale, 'w_down': jax.random.normal(k4, (H, I), dtype=jnp.float32) * (1.0 / np.sqrt(I)), 'ln_weight': jnp.ones((I,), dtype=jnp.float32)}
    _L0_ffn_all = _L0_ffn_setup()
    _L0_ffn_in = {k: v for k, v in _L0_ffn_all.items() if k in ('w_gate', 'w_up', 'w_down', 'ln_weight')}
    del _L0_ffn_all

    def _L1_xattn_setup():
        import jax, jax.numpy as jnp
        import numpy as np
        FP8_MAX = 448.0
        EPS = 1e-05

        def _fp8_roundtrip(x):
            return x.astype(jnp.float8_e4m3fn).astype(jnp.float32)

        def _div_clamp_fp8(x, scale):
            y = jnp.clip(x.astype(jnp.float32) / scale, -FP8_MAX, FP8_MAX)
            y = y.astype(jnp.bfloat16).astype(jnp.float32)
            return _fp8_roundtrip(y)

        def _ln(x, w, b):
            mu = jnp.mean(x, axis=-1, keepdims=True)
            var = jnp.mean(jnp.square(x - mu), axis=-1, keepdims=True)
            return (x - mu) * jax.lax.rsqrt(var + EPS) * w + b

        def _fp8_linear_pertensor(x, wq, w_scale, in_scale):
            xq = _div_clamp_fp8(x, in_scale)
            return jnp.einsum('bsi,oi->bso', xq * in_scale, wq) * w_scale

        def _gqa(q, k, v):
            scale = 1.0 / np.sqrt(q.shape[-1])
            scores = jnp.einsum('bsghd,btgd->bghst', q, k) * scale
            p = jax.nn.softmax(scores, axis=-1)
            return jnp.einsum('bghst,btgd->bsghd', p, v)
        key = jax.random.key(seed)
        ks = jax.random.split(key, 8)
        B, S, SC, H, NH, G, D = (2, 256, 64, 256, 16, 8, 128)

        def qw(k, out_f, in_f):
            w = jax.random.normal(k, (out_f, in_f), jnp.float32) * 0.02
            sc = jnp.max(jnp.abs(w)) / FP8_MAX
            return (_fp8_roundtrip(w / sc), sc.astype(jnp.float32))
        wq, wq_s = qw(ks[0], NH * D, H)
        wqx, wqx_s = qw(ks[1], NH * D, H)
        wk, wk_s = qw(ks[2], G * D, H)
        wv, wv_s = qw(ks[3], G * D, H)
        wproj, wp_s = qw(ks[4], H, 2 * NH * D)
        return {'hidden_states': jax.random.normal(ks[5], (B, S, H), jnp.float32), 'cond': jax.random.normal(ks[6], (B, SC, H), jnp.float32), 'ln_w': jnp.ones((H,), jnp.float32), 'ln_b': jnp.zeros((H,), jnp.float32), 'wq': wq, 'wq_scale': wq_s, 'q_in_scale': jnp.full((H,), 0.05, jnp.float32), 'wqx': wqx, 'wqx_scale': wqx_s, 'qx_in_scale': jnp.full((H,), 0.05, jnp.float32), 'wk': wk, 'wk_scale': wk_s, 'k_in_scale': jnp.full((H,), 0.05, jnp.float32), 'wv': wv, 'wv_scale': wv_s, 'v_in_scale': jnp.full((H,), 0.05, jnp.float32), 'w_kv_x': jax.random.normal(ks[7], (2 * G * D, H), jnp.float32) * 0.02, 'qln_w': jnp.ones((D,), jnp.float32), 'qln_b': jnp.zeros((D,), jnp.float32), 'kln_w': jnp.ones((D,), jnp.float32), 'kln_b': jnp.zeros((D,), jnp.float32), 'qxln_w': jnp.ones((D,), jnp.float32), 'qxln_b': jnp.zeros((D,), jnp.float32), 'kxln_w': jnp.ones((D,), jnp.float32), 'kxln_b': jnp.zeros((D,), jnp.float32), 'wproj': wproj, 'proj_w_scale': wp_s, 'proj_in_scale': jnp.asarray(0.05, jnp.float32), 'proj_smooth': jnp.full((2 * NH * D,), 0.05, jnp.float32)}
    _L1_xattn_all = _L1_xattn_setup()
    _L1_xattn_in = {k: v for k, v in _L1_xattn_all.items() if k in ('ln_w', 'ln_b', 'wq', 'wq_scale', 'q_in_scale', 'wqx', 'wqx_scale', 'qx_in_scale', 'wk', 'wk_scale', 'k_in_scale', 'wv', 'wv_scale', 'v_in_scale', 'w_kv_x', 'qln_w', 'qln_b', 'kln_w', 'kln_b', 'qxln_w', 'qxln_b', 'kxln_w', 'kxln_b', 'wproj', 'proj_w_scale', 'proj_in_scale', 'proj_smooth')}
    del _L1_xattn_all

    def _L1_ffn_setup():
        import jax, jax.numpy as jnp
        import numpy as np
        NUM_ROUTED = 7
        TOP_K = 3
        D = 256
        H = 256
        B, S = (4, 256)

        def _expert_ffn(x, w1, wg, w2):
            return jax.nn.silu(x @ w1) * (x @ wg) @ w2
        key = jax.random.key(seed)
        ks = jax.random.split(key, 8)
        s = 0.02
        return {'x': jax.random.normal(ks[0], (B, S, D), jnp.float32), 'W1': jax.random.normal(ks[1], (NUM_ROUTED, D, H), jnp.float32) * s, 'Wg': jax.random.normal(ks[2], (NUM_ROUTED, D, H), jnp.float32) * s, 'W2': jax.random.normal(ks[3], (NUM_ROUTED, H, D), jnp.float32) * s, 'Ws1': jax.random.normal(ks[4], (D, H), jnp.float32) * s, 'Wsg': jax.random.normal(ks[5], (D, H), jnp.float32) * s, 'Ws2': jax.random.normal(ks[6], (H, D), jnp.float32) * s, 'gate_w': jax.random.normal(ks[7], (D, NUM_ROUTED), jnp.float32) * s, 'gate_b': jnp.zeros((NUM_ROUTED,), jnp.float32), 'biases': jnp.zeros((NUM_ROUTED,), jnp.float32)}
    _L1_ffn_all = _L1_ffn_setup()
    _L1_ffn_in = {k: v for k, v in _L1_ffn_all.items() if k in ('W1', 'Wg', 'W2', 'Ws1', 'Wsg', 'Ws2', 'gate_w', 'gate_b', 'biases')}
    del _L1_ffn_all
    return {'x': x, 'ctx_2048': ctx_2048, 'mask_BxSxS2_ff0': mask_BxSxS2_ff0, 'g_xattn': g_xattn, 'g_ffn': g_ffn, 'L0_xattn_Wq': _L0_xattn_in['Wq'], 'L0_xattn_bq': _L0_xattn_in['bq'], 'L0_xattn_Wk': _L0_xattn_in['Wk'], 'L0_xattn_bk': _L0_xattn_in['bk'], 'L0_xattn_Wv': _L0_xattn_in['Wv'], 'L0_xattn_bv': _L0_xattn_in['bv'], 'L0_ffn_w_gate': _L0_ffn_in['w_gate'], 'L0_ffn_w_up': _L0_ffn_in['w_up'], 'L0_ffn_w_down': _L0_ffn_in['w_down'], 'L0_ffn_ln_weight': _L0_ffn_in['ln_weight'], 'L1_xattn_ln_w': _L1_xattn_in['ln_w'], 'L1_xattn_ln_b': _L1_xattn_in['ln_b'], 'L1_xattn_wq': _L1_xattn_in['wq'], 'L1_xattn_wq_scale': _L1_xattn_in['wq_scale'], 'L1_xattn_q_in_scale': _L1_xattn_in['q_in_scale'], 'L1_xattn_wqx': _L1_xattn_in['wqx'], 'L1_xattn_wqx_scale': _L1_xattn_in['wqx_scale'], 'L1_xattn_qx_in_scale': _L1_xattn_in['qx_in_scale'], 'L1_xattn_wk': _L1_xattn_in['wk'], 'L1_xattn_wk_scale': _L1_xattn_in['wk_scale'], 'L1_xattn_k_in_scale': _L1_xattn_in['k_in_scale'], 'L1_xattn_wv': _L1_xattn_in['wv'], 'L1_xattn_wv_scale': _L1_xattn_in['wv_scale'], 'L1_xattn_v_in_scale': _L1_xattn_in['v_in_scale'], 'L1_xattn_w_kv_x': _L1_xattn_in['w_kv_x'], 'L1_xattn_qln_w': _L1_xattn_in['qln_w'], 'L1_xattn_qln_b': _L1_xattn_in['qln_b'], 'L1_xattn_kln_w': _L1_xattn_in['kln_w'], 'L1_xattn_kln_b': _L1_xattn_in['kln_b'], 'L1_xattn_qxln_w': _L1_xattn_in['qxln_w'], 'L1_xattn_qxln_b': _L1_xattn_in['qxln_b'], 'L1_xattn_kxln_w': _L1_xattn_in['kxln_w'], 'L1_xattn_kxln_b': _L1_xattn_in['kxln_b'], 'L1_xattn_wproj': _L1_xattn_in['wproj'], 'L1_xattn_proj_w_scale': _L1_xattn_in['proj_w_scale'], 'L1_xattn_proj_in_scale': _L1_xattn_in['proj_in_scale'], 'L1_xattn_proj_smooth': _L1_xattn_in['proj_smooth'], 'L1_ffn_W1': _L1_ffn_in['W1'], 'L1_ffn_Wg': _L1_ffn_in['Wg'], 'L1_ffn_W2': _L1_ffn_in['W2'], 'L1_ffn_Ws1': _L1_ffn_in['Ws1'], 'L1_ffn_Wsg': _L1_ffn_in['Wsg'], 'L1_ffn_Ws2': _L1_ffn_in['Ws2'], 'L1_ffn_gate_w': _L1_ffn_in['gate_w'], 'L1_ffn_gate_b': _L1_ffn_in['gate_b'], 'L1_ffn_biases': _L1_ffn_in['biases']}

def reference(x, ctx_2048, mask_BxSxS2_ff0, g_xattn, g_ffn, L0_xattn_Wq, L0_xattn_bq, L0_xattn_Wk, L0_xattn_bk, L0_xattn_Wv, L0_xattn_bv, L0_ffn_w_gate, L0_ffn_w_up, L0_ffn_w_down, L0_ffn_ln_weight, L1_xattn_ln_w, L1_xattn_ln_b, L1_xattn_wq, L1_xattn_wq_scale, L1_xattn_q_in_scale, L1_xattn_wqx, L1_xattn_wqx_scale, L1_xattn_qx_in_scale, L1_xattn_wk, L1_xattn_wk_scale, L1_xattn_k_in_scale, L1_xattn_wv, L1_xattn_wv_scale, L1_xattn_v_in_scale, L1_xattn_w_kv_x, L1_xattn_qln_w, L1_xattn_qln_b, L1_xattn_kln_w, L1_xattn_kln_b, L1_xattn_qxln_w, L1_xattn_qxln_b, L1_xattn_kxln_w, L1_xattn_kxln_b, L1_xattn_wproj, L1_xattn_proj_w_scale, L1_xattn_proj_in_scale, L1_xattn_proj_smooth, L1_ffn_W1, L1_ffn_Wg, L1_ffn_W2, L1_ffn_Ws1, L1_ffn_Wsg, L1_ffn_Ws2, L1_ffn_gate_w, L1_ffn_gate_b, L1_ffn_biases):
    import jax
    import jax.numpy as jnp

    def _L0_xattn_ref(x, attention_mask, k_cache, v_cache, Wq, bq, Wk, bk, Wv, bv):
        import jax, jax.numpy as jnp
        import numpy as np
        B, Q_LEN, E = (8, 16, 256)
        CACHE_LEN = 512
        Q = jnp.einsum('bqe,fe->bqf', x, Wq) + bq
        K_new = jnp.einsum('bqe,fe->bqf', x, Wk) + bk
        V_new = jnp.einsum('bqe,fe->bqf', x, Wv) + bv
        q_len = x.shape[1]
        end_step = attention_mask.shape[-1]
        past_kv_len = end_step - q_len
        k_cache = jax.lax.dynamic_update_slice(k_cache, K_new, (0, past_kv_len, 0))
        v_cache = jax.lax.dynamic_update_slice(v_cache, V_new, (0, past_kv_len, 0))
        K = k_cache[:, :end_step, :]
        V = v_cache[:, :end_step, :]
        scale = 1.0 / jnp.sqrt(jnp.asarray(Q.shape[-1], Q.dtype))
        scores = jnp.einsum('bqe,bke->bqk', Q, K) * scale + attention_mask
        attn = jax.nn.softmax(scores, axis=-1)
        return jnp.einsum('bqk,bke->bqe', attn, V)

    def _L0_ffn_ref(x, w_gate, w_up, w_down, ln_weight):
        import jax, jax.numpy as jnp
        import numpy as np
        EPS = 1e-05
        RMS_EPS = 1e-06

        def activation_quant(x, num_bits=8):
            qn = -2 ** (num_bits - 1)
            qp = 2 ** (num_bits - 1) - 1
            xf = x.astype(jnp.float32)
            s = qp / jnp.clip(jnp.max(jnp.abs(xf), axis=-1, keepdims=True), EPS, None)
            return (jnp.clip(jnp.round(xf * s), qn, qp) / s).astype(x.dtype)

        def weight_quant(w):
            wf = w.astype(jnp.float32)
            s = 1.0 / jnp.clip(jnp.mean(jnp.abs(wf)), EPS, None)
            return (jnp.clip(jnp.round(wf * s), -1.0, 1.0) / s).astype(w.dtype)

        def bit_linear(x, w):
            qx = x + jax.lax.stop_gradient(activation_quant(x) - x)
            qw = w + jax.lax.stop_gradient(weight_quant(w) - w)
            return jnp.einsum('bsh,oh->bso', qx, qw)

        def rms_norm(x, weight, eps=RMS_EPS):
            xf = x.astype(jnp.float32)
            var = jnp.mean(xf * xf, axis=-1, keepdims=True)
            return weight * (xf * jax.lax.rsqrt(var + eps)).astype(x.dtype)
        h = jax.nn.silu(bit_linear(x, w_gate)) * bit_linear(x, w_up)
        h = rms_norm(h, ln_weight)
        return bit_linear(h, w_down)

    def _L1_xattn_ref(hidden_states, cond, ln_w, ln_b, wq, wq_scale, q_in_scale, wqx, wqx_scale, qx_in_scale, wk, wk_scale, k_in_scale, wv, wv_scale, v_in_scale, w_kv_x, qln_w, qln_b, kln_w, kln_b, qxln_w, qxln_b, kxln_w, kxln_b, wproj, proj_w_scale, proj_in_scale, proj_smooth):
        import jax, jax.numpy as jnp
        import numpy as np
        FP8_MAX = 448.0
        EPS = 1e-05

        def _fp8_roundtrip(x):
            return x.astype(jnp.float8_e4m3fn).astype(jnp.float32)

        def _div_clamp_fp8(x, scale):
            y = jnp.clip(x.astype(jnp.float32) / scale, -FP8_MAX, FP8_MAX)
            y = y.astype(jnp.bfloat16).astype(jnp.float32)
            return _fp8_roundtrip(y)

        def _ln(x, w, b):
            mu = jnp.mean(x, axis=-1, keepdims=True)
            var = jnp.mean(jnp.square(x - mu), axis=-1, keepdims=True)
            return (x - mu) * jax.lax.rsqrt(var + EPS) * w + b

        def _fp8_linear_pertensor(x, wq, w_scale, in_scale):
            xq = _div_clamp_fp8(x, in_scale)
            return jnp.einsum('bsi,oi->bso', xq * in_scale, wq) * w_scale

        def _gqa(q, k, v):
            scale = 1.0 / np.sqrt(q.shape[-1])
            scores = jnp.einsum('bsghd,btgd->bghst', q, k) * scale
            p = jax.nn.softmax(scores, axis=-1)
            return jnp.einsum('bghst,btgd->bsghd', p, v)
        b, s, _ = hidden_states.shape
        sc = cond.shape[1]
        d = qln_w.shape[0]
        nh = wq.shape[0] // d
        g = wk.shape[0] // d
        hpg = nh // g
        ln_out = _ln(hidden_states, ln_w, ln_b)
        q = _fp8_linear_pertensor(ln_out, wq, wq_scale, q_in_scale).reshape(b, s, g, hpg, d)
        q = _ln(q, qln_w, qln_b)
        k = _fp8_linear_pertensor(ln_out, wk, wk_scale, k_in_scale).reshape(b, s, g, d)
        k = _ln(k, kln_w, kln_b)
        v = _fp8_linear_pertensor(ln_out, wv, wv_scale, v_in_scale).reshape(b, s, g, d)
        core = _gqa(q, k, v).reshape(b, s, nh * d)
        qx = _fp8_linear_pertensor(ln_out, wqx, wqx_scale, qx_in_scale).reshape(b, s, g, hpg, d)
        qx = _ln(qx, qxln_w, qxln_b)
        kvx = jnp.einsum('bsi,oi->bso', cond, w_kv_x)
        kx, vx = jnp.split(kvx, 2, axis=-1)
        kx = _ln(kx.reshape(b, sc, g, d), kxln_w, kxln_b)
        vx = vx.reshape(b, sc, g, d)
        xout = _gqa(qx, kx, vx).reshape(b, s, nh * d)
        cat = jnp.concatenate([core, xout], axis=-1)
        catq = _div_clamp_fp8(cat, proj_smooth)
        return jnp.einsum('bsi,oi->bso', catq, wproj) * (proj_in_scale * proj_w_scale)

    def _L1_ffn_ref(x, W1, Wg, W2, Ws1, Wsg, Ws2, gate_w, gate_b, biases):
        import jax, jax.numpy as jnp
        import numpy as np
        NUM_ROUTED = 7
        TOP_K = 3
        D = 256
        H = 256
        B, S = (4, 256)

        def _expert_ffn(x, w1, wg, w2):
            return jax.nn.silu(x @ w1) * (x @ wg) @ w2
        output = _expert_ffn(x, Ws1, Wsg, Ws2)
        gate_logits = x @ gate_w + gate_b
        gate_probas = jax.nn.softmax(gate_logits, axis=-1)
        biased_probas = gate_probas + biases
        _, topk_idxs = jax.lax.top_k(biased_probas, TOP_K)
        topk_probas = jnp.take_along_axis(gate_probas, topk_idxs, axis=-1)
        topk_probas = topk_probas / jnp.sum(topk_probas, axis=-1, keepdims=True)
        for e in range(NUM_ROUTED):
            w_e = jnp.sum(topk_probas * (topk_idxs == e), axis=-1)
            output = output + _expert_ffn(x, W1[e], Wg[e], W2[e]) * w_e[..., None]
        return output
    x = x + jnp.tanh(g_xattn[0]) * _L0_xattn_ref(_layernorm(x, axis=-1), mask_BxSxS2_ff0, ctx_2048, ctx_2048, L0_xattn_Wq, L0_xattn_bq, L0_xattn_Wk, L0_xattn_bk, L0_xattn_Wv, L0_xattn_bv)
    x = x + jnp.tanh(g_ffn[0]) * _L0_ffn_ref(_layernorm(x, axis=-1), L0_ffn_w_gate, L0_ffn_w_up, L0_ffn_w_down, L0_ffn_ln_weight)
    x = x + jnp.tanh(g_xattn[1]) * _L1_xattn_ref(_layernorm(x, axis=-1), ctx_2048, L1_xattn_ln_w, L1_xattn_ln_b, L1_xattn_wq, L1_xattn_wq_scale, L1_xattn_q_in_scale, L1_xattn_wqx, L1_xattn_wqx_scale, L1_xattn_qx_in_scale, L1_xattn_wk, L1_xattn_wk_scale, L1_xattn_k_in_scale, L1_xattn_wv, L1_xattn_wv_scale, L1_xattn_v_in_scale, L1_xattn_w_kv_x, L1_xattn_qln_w, L1_xattn_qln_b, L1_xattn_kln_w, L1_xattn_kln_b, L1_xattn_qxln_w, L1_xattn_qxln_b, L1_xattn_kxln_w, L1_xattn_kxln_b, L1_xattn_wproj, L1_xattn_proj_w_scale, L1_xattn_proj_in_scale, L1_xattn_proj_smooth)
    x = x + jnp.tanh(g_ffn[1]) * _L1_ffn_ref(_layernorm(x, axis=-1), L1_ffn_W1, L1_ffn_Wg, L1_ffn_W2, L1_ffn_Ws1, L1_ffn_Wsg, L1_ffn_Ws2, L1_ffn_gate_w, L1_ffn_gate_b, L1_ffn_biases)
    return x

_drawn_inputs = setup_inputs


def setup_inputs(seed=0):
    import zlib

    import numpy as np

    out = dict(_drawn_inputs(seed))
    spreads = {'g_ffn': (-1.0, 0.6),
     'L0_ffn_ln_weight': (1.0, 0.2),
     'L1_xattn_ln_w': (1.0, 0.6),
     'L1_xattn_ln_b': (0.0, 0.309),
     'L1_xattn_q_in_scale': (0.05000000074505806, 0.6),
     'L1_xattn_qx_in_scale': (0.05000000074505806, 0.6),
     'L1_xattn_k_in_scale': (0.05000000074505806, 0.6),
     'L1_xattn_v_in_scale': (0.05000000074505806, 0.6),
     'L1_xattn_qln_w': (1.0, 0.6),
     'L1_xattn_qln_b': (0.0, 0.8),
     'L1_xattn_kln_w': (1.0, 0.6),
     'L1_xattn_kln_b': (0.0, 0.8),
     'L1_xattn_qxln_w': (1.0, 0.6),
     'L1_xattn_qxln_b': (0.0, 0.8),
     'L1_xattn_kxln_w': (1.0, 0.6),
     'L1_xattn_kxln_b': (0.0, 0.8),
     'L1_xattn_proj_smooth': (0.05000000074505806, 0.2),
     'L1_ffn_gate_b': (0.0, 0.8),
     'L1_ffn_biases': (0.0, 0.8)}
    factors = {'L0_xattn_bq': 3.619,
     'L0_xattn_bk': 8.0,
     'L1_ffn_W1': 7.87,
     'L1_ffn_Wg': 7.777,
     'L1_ffn_W2': 7.775,
     'L1_ffn_Ws1': 4.659,
     'L1_ffn_Wsg': 4.589,
     'L1_ffn_Ws2': 4.596,
     'L1_ffn_gate_w': 8.0}
    for name, (base, spread) in spreads.items():
        noise = np.random.default_rng([zlib.crc32(name.encode()), seed]).standard_normal(out[name].shape)
        drawn = base * np.exp(spread * noise) if base else spread * noise
        out[name] = jnp.asarray(drawn.astype(out[name].dtype))
    for name, factor in factors.items():
        out[name] = (out[name] * factor).astype(out[name].dtype)
    return out
```

```python
from contextlib import ExitStack, contextmanager

import concourse.bass as bass
from concourse import mybir

F32 = mybir.dt.float32
F32R = mybir.dt.float32r
BF16 = mybir.dt.bfloat16
U16 = mybir.dt.uint16
ALU = mybir.AluOpType
ACT = mybir.ActivationFunctionType
AX = mybir.AxisListType

P = 128
BATCH, SEQ, E = 16, 64, 256
TOK = BATCH * SEQ
TILES = TOK // P
KT = E // P
ST = 4
GROUPS = TILES // ST
INNER = 1024
HEADS, KV, D = 16, 8, 128
EXPERTS, TOP_K = 7, 3
MAGIC = 1.5 * 2.0 ** 23
FP8_MAX = 448.0
FP8_LEAST = 1.5 * 2.0 ** -6
FP8_SHIFT = 2.0 ** 20
LN_EPS, RMS_EPS, QUANT_EPS = 1e-5, 1e-6, 1e-5


def bcast(ap, axis, n):
    shape = list(ap.shape)
    shape.insert(axis, n)
    return ap.unsqueeze(axis).broadcast_to(shape)


@contextmanager
def phase_semaphores(nc):
    taken = []

    def take(name):
        taken.append(nc.alloc_semaphore(name=name))
        return taken[-1]

    yield take
    nc.clear_and_free_semaphores(taken)
    nc.all_engine_barrier()


def flamingo_program(nc, t):
    ctx = ExitStack()
    with ctx:
        def sb(name, shape, dt=F32):
            return ctx.enter_context(nc.sbuf_tensor(name, shape, dt))

        k = {
            "x": sb("x_res", [P, TILES, E]),
            "ident": sb("ident", [P, P]),
            "identb": sb("identb", [P, P], BF16),
            "ones": sb("ones", [P, P]),
            "half": sb("neg_half", [P, 32]),
            "gate": sb("gate", [P, 4]),
        }
        setup(nc, t, k)
        attention0(nc, t, k)
        bitnet(nc, t, k)
        with nc.sbuf_tensor("xq_all", [P, 4, KT, TOK], BF16) as xq:
            k["xq"] = xq
            quantize_tokens(nc, t, k)
            gqa_pass(nc, t, k, cross=False)
            gqa_pass(nc, t, k, cross=True)
        moe(nc, t, k)
        with nc.semaphore("stored") as stored, nc.Block() as block:
            @block.sync
            def _(sp):
                sp.dma_start(t["out"].rearrange("(n p) e -> p n e", p=P), k["x"][:]).then_inc(stored, 16)
                sp.wait_ge(stored, 16)


def setup(nc, t, k):
    with phase_semaphores(nc) as take, ExitStack() as c:
        loaded = take("setup_loaded")
        filled = take("setup_filled")
        made = take("setup_made")
        raw = c.enter_context(nc.sbuf_tensor("gate_raw", [P, 4], F32))
        block = c.enter_context(nc.Block())

        @block.sync
        def _(sp):
            sp.dma_start(k["x"][:], t["x"].rearrange("(n p) e -> p n e", p=P)).then_inc(loaded, 16)
            sp.dma_start(raw[:, 0:2], t["g_xattn"].rearrange("(o n) -> o n", o=1).broadcast_to([P, 2])).then_inc(loaded, 16)
            sp.dma_start(raw[:, 2:4], t["g_ffn"].rearrange("(o n) -> o n", o=1).broadcast_to([P, 2])).then_inc(loaded, 16)

        @block.gpsimd
        def _(pool):
            nc.gpsimd.memset(k["ident"][:], 0.0).then_inc(filled, 1)
            nc.gpsimd.memset(k["ones"][:], 1.0)
            nc.gpsimd.memset(k["half"][:], -0.5)
            pool.wait_ge(filled, 1)
            nc.gpsimd.affine_select(out=k["ident"][:], in_=k["ident"][:], compare_op=ALU.not_equal, fill=1.0,
                                    base=0, pattern=[[-1, P]], channel_multiplier=1).then_inc(made, 1)
            pool.wait_ge(made, 1)
            nc.gpsimd.tensor_copy(k["identb"][:], k["ident"][:]).then_inc(made, 1)
            pool.wait_ge(made, 2)

        @block.scalar
        def _(act):
            act.wait_ge(loaded, 48)
            nc.scalar.activation(k["gate"][:], raw[:], ACT.Tanh)


class LayerNorm:

    def __init__(self, nc, c, take, name, k):
        self.nc, self.k = nc, k
        self.stats = c.enter_context(nc.sbuf_tensor(name + "_stats", [P, ST, 6], F32))
        self.mv = c.enter_context(nc.sbuf_tensor(name + "_mv", [P, ST, 2], F32))
        self.ve = c.enter_context(nc.sbuf_tensor(name + "_ve", [P, ST], F32))
        self.rstd = c.enter_context(nc.sbuf_tensor(name + "_rstd", [P, ST], F32))
        self.stats_done = take(name + "_stats_done")
        self.mv_done = take(name + "_mv_done")
        self.ve_done = take(name + "_ve_done")
        self.rstd_done = take(name + "_rstd_done")

    def on_vector(self, dve, s, source, out, normed):
        for j in range(ST):
            self.nc.vector.bn_stats(self.stats[:, j, :], source(j)).then_inc(self.stats_done, 1)
        dve.wait_ge(self.stats_done, (s + 1) * ST)
        self.nc.vector.memset(self.ve[:, 0:1], 0.0)
        for j in range(ST):
            self.nc.vector.bn_aggr(self.mv[:, j, :], self.stats[:, j, :]).then_inc(self.mv_done, 1)
        dve.wait_ge(self.mv_done, (s + 1) * ST)
        self.nc.vector.tensor_scalar(self.ve[:], self.mv[:, :, 1], 1.0, LN_EPS, ALU.mult, ALU.add).then_inc(self.ve_done, 1)
        dve.wait_ge(self.rstd_done, s + 1)
        for j in range(ST):
            self.nc.vector.tensor_scalar(out(j), source(j), self.mv[:, j, 0:1], self.rstd[:, j:j + 1],
                                         ALU.subtract, ALU.mult).then_inc(normed, 1)

    def on_pool(self, pool, s):
        pool.wait_ge(self.ve_done, s + 1)
        self.nc.gpsimd.tensor_tensor(self.rstd[:], self.ve[:], self.k["half"][:, 0:ST], ALU.pow).then_inc(self.rstd_done, 1)


def attention0(nc, t, k):
    with phase_semaphores(nc) as take, ExitStack() as c:
        def sb(name, shape, dt=F32):
            return c.enter_context(nc.sbuf_tensor("a_" + name, shape, dt))

        def ps(name):
            return c.enter_context(nc.psum_tensor("a_" + name, [P, 512], F32))

        def sem(name):
            return take("a_" + name)

        wq, wk, wv = sb("wq", [P, KT, E]), sb("wk", [P, KT, E]), sb("wv", [P, KT, E])
        bq, bk, bv = sb("bq", [P, KT]), sb("bk", [P, KT]), sb("bv", [P, E])
        mask = sb("mask", [P, TILES, SEQ])
        xn, xnT = sb("xn", [P, ST, E]), sb("xnT", [P, KT, ST * P])
        qT, kT = sb("qT", [P, KT, ST * P]), sb("kT", [P, KT, ST * P])
        v = sb("v", [P, ST, E])
        s_ = sb("s", [P, ST, SEQ])
        mx, sm, rc = sb("mx", [P, ST]), sb("sm", [P, ST]), sb("rc", [P, ST])
        probs = sb("probs", [P, ST, P])
        pT = sb("pT", [P, ST, P])
        ln = LayerNorm(nc, c, take, "a_ln", k)
        tp = [ps("tp0"), ps("tp1")]
        qk = [ps("qk0"), ps("qk1")]
        vo = [ps("vo0"), ps("vo1")]
        sp_ = ps("scores")
        loaded, normed, turned, xnT_done = sem("loaded"), sem("normed"), sem("turned"), sem("xnT_done")
        qk_done, qk_kept, v_done, v_kept = sem("qk_done"), sem("qk_kept"), sem("v_done"), sem("v_kept")
        sc_done, masked, max_done, sub_done = sem("sc_done"), sem("masked"), sem("max_done"), sem("sub_done")
        exp_done, sum_done, rec_done, probs_done = sem("exp_done"), sem("sum_done"), sem("rec_done"), sem("probs_done")
        pT_turned, pT_kept, o_done, x_done, zeroed = (sem("pT_turned"), sem("pT_kept"), sem("o_done"), sem("x_done"),
                                                      sem("zeroed"))
        block = c.enter_context(nc.Block())

        @block.sync
        def _(sp):
            for dst, src in ((wq, "L0_WqT"), (wk, "L0_WkT"), (wv, "L0_WvT")):
                sp.dma_start(dst[:], t[src].rearrange("(c p) f -> p c f", p=P)).then_inc(loaded, 16)
            for dst, src in ((bq, "L0_bq"), (bk, "L0_bk")):
                sp.dma_start(dst[:], t[src]).then_inc(loaded, 16)
            sp.dma_start(bv[:], t["L0_bv"].rearrange("(o n) -> o n", o=1).broadcast_to([P, E])).then_inc(loaded, 16)
            sp.dma_start(mask[:], t["mask"].rearrange("(n p) s -> p n s", p=P)).then_inc(loaded, 16)

        @block.gpsimd
        def _(pool):
            nc.gpsimd.memset(probs[:], 0.0).then_inc(zeroed, 1)
            with pool.Fori(0, GROUPS) as s:
                ln.on_pool(pool, s)

        @block.vector
        def _(dve):
            dve.wait_ge(loaded, 7 * 16)
            dve.wait_ge(zeroed, 1)
            with dve.Fori(0, GROUPS) as s:
                def tile(j):
                    return k["x"][:].rearrange("p n e -> p (n e)")[:, bass.ds(s * (ST * E) + j * E, E)]

                ln.on_vector(dve, s, tile, lambda j: xn[:, j, :], normed)
                for h in range(2):
                    dve.wait_ge(v_done, s * 2 + h + 1)
                    nc.vector.tensor_tensor(v[:, 2 * h:2 * h + 2, :], vo[h][:].rearrange("p (n e) -> p n e", n=2),
                                            bcast(bv[:], 1, 2), ALU.add).then_inc(v_kept, 1)
                dve.wait_ge(sc_done, s + 1)
                for b in range(2):
                    rows = slice(b * SEQ, (b + 1) * SEQ)
                    nc.vector.scalar_tensor_tensor(
                        s_[rows], sp_[rows].rearrange("p (n m) -> p n m", n=ST)[:, :, b * SEQ:(b + 1) * SEQ], E ** -0.5,
                        mask[rows].rearrange("p n s -> p (n s)")[:, bass.ds(s * (ST * SEQ), ST * SEQ)].rearrange("p (n s) -> p n s", n=ST),
                        ALU.mult, ALU.add).then_inc(masked, 1)
                dve.wait_ge(masked, s * 2 + 2)
                nc.vector.tensor_reduce(mx[:], s_[:], AX.X, ALU.max).then_inc(max_done, 1)
                dve.wait_ge(max_done, s + 1)
                nc.vector.tensor_tensor(s_[:], s_[:], bcast(mx[:], 2, SEQ), ALU.subtract).then_inc(sub_done, 1)
                dve.wait_ge(exp_done, s + 1)
                nc.vector.tensor_reduce(sm[:], s_[:], AX.X, ALU.add).then_inc(sum_done, 1)
                dve.wait_ge(sum_done, s + 1)
                nc.vector.reciprocal(rc[:], sm[:]).then_inc(rec_done, 1)
                dve.wait_ge(rec_done, s + 1)
                for b in range(2):
                    rows = slice(b * SEQ, (b + 1) * SEQ)
                    nc.vector.tensor_tensor(probs[rows, :, b * SEQ:(b + 1) * SEQ], s_[rows], bcast(rc[rows], 2, SEQ),
                                            ALU.mult).then_inc(probs_done, 1)
                for j in range(ST):
                    dve.wait_ge(o_done, s * 2 + j // 2 + 1)
                    nc.vector.scalar_tensor_tensor(tile(j), vo[j // 2][:, (j % 2) * E:(j % 2 + 1) * E], k["gate"][:, 0:1], tile(j),
                                                   ALU.mult, ALU.add).then_inc(x_done, 1)

        @block.scalar
        def _(act):
            act.wait_ge(loaded, 7 * 16)
            with act.Fori(0, GROUPS) as s:
                for c_ in range(KT):
                    act.wait_ge(turned, s * ST + ST)
                    nc.scalar.activation(xnT[:, c_, :], tp[c_][:], ACT.Copy).then_inc(xnT_done, 1)
                for n, (dst, bias) in enumerate(((qT, bq), (kT, bk))):
                    for f in range(KT):
                        act.wait_ge(qk_done, s * 4 + n * 2 + f + 1)
                        nc.scalar.activation(dst[:, f, :], qk[f][:], ACT.Identity, bias=bias[:, f:f + 1]).then_inc(qk_kept, 1)
                act.wait_ge(sub_done, s + 1)
                nc.scalar.activation(s_[:], s_[:], ACT.Exp).then_inc(exp_done, 1)
                act.wait_ge(pT_turned, s + 1)
                nc.scalar.activation(pT[:], tp[0][:].rearrange("p (n m) -> p n m", n=ST), ACT.Copy).then_inc(pT_kept, 1)

        @block.tensor
        def _(pe):
            pe.wait_ge(loaded, 7 * 16)
            with pe.Fori(0, GROUPS) as s:
                for j in range(ST):
                    pe.wait_ge(normed, s * ST + j + 1)
                    for c_ in range(KT):
                        last = nc.tensor.transpose(tp[c_][:, j * P:(j + 1) * P], xn[:, j, c_ * P:(c_ + 1) * P], k["ident"][:])
                    last.then_inc(turned, 1)
                pe.wait_ge(xnT_done, s * KT + KT)
                for n, w in enumerate((wq, wk)):
                    for f in range(KT):
                        if n == 1:
                            pe.wait_ge(qk_kept, s * 4 + f + 1)
                        for c_ in range(KT):
                            last = nc.tensor.matmul(qk[f][:], w[:, c_, f * P:(f + 1) * P], xnT[:, c_, :],
                                                    start=c_ == 0, stop=c_ == KT - 1)
                        last.then_inc(qk_done, 1)
                pe.wait_ge(x_done, s * ST)
                for j in range(ST):
                    for c_ in range(KT):
                        last = nc.tensor.matmul(vo[j // 2][:, (j % 2) * E:(j % 2 + 1) * E], xnT[:, c_, j * P:(j + 1) * P],
                                                wv[:, c_, :], start=c_ == 0, stop=c_ == KT - 1)
                    if j % 2 == 1:
                        last.then_inc(v_done, 1)
                pe.wait_ge(qk_kept, s * 4 + 4)
                for j in range(ST):
                    for c_ in range(KT):
                        last = nc.tensor.matmul(sp_[:, j * P:(j + 1) * P], qT[:, c_, j * P:(j + 1) * P], kT[:, c_, j * P:(j + 1) * P],
                                                start=c_ == 0, stop=c_ == KT - 1)
                last.then_inc(sc_done, 1)
                pe.wait_ge(probs_done, s * 2 + 2)
                for j in range(ST):
                    last = nc.tensor.transpose(tp[0][:, j * P:(j + 1) * P], probs[:, j, :], k["ident"][:])
                last.then_inc(pT_turned, 1)
                pe.wait_ge(pT_kept, s + 1)
                pe.wait_ge(v_kept, s * 2 + 2)
                for j in range(ST):
                    last = nc.tensor.matmul(vo[j // 2][:, (j % 2) * E:(j % 2 + 1) * E], pT[:, j, :], v[:, j, :],
                                            start=True, stop=True)
                    if j % 2 == 1:
                        last.then_inc(o_done, 1)


def bitnet(nc, t, k):
    with phase_semaphores(nc) as take, ExitStack() as c:
        def sb(name, shape, dt=F32):
            return c.enter_context(nc.sbuf_tensor("b_" + name, shape, dt))

        def ps(name, dt=F32):
            return c.enter_context(nc.psum_tensor("b_" + name, [P, 512 if dt == F32 else 1024], dt))

        def sem(name):
            return take("b_" + name)

        FC = INNER // P
        raw = [sb("raw_gate", [P, KT * INNER]), sb("raw_up", [P, KT * INNER]), sb("raw_down", [P, FC * E])]
        tern = [sb("gate", [P, KT * INNER], BF16), sb("up", [P, KT * INNER], BF16), sb("down", [P, FC * E], BF16)]
        wg, wu = (w[:].rearrange("p (c f) -> p c f", c=KT) for w in tern[:2])
        wd = tern[2][:].rearrange("p (c f) -> p c f", c=FC)
        colsum, mean, winv = sb("colsum", [P, 3]), sb("mean", [P, 3]), sb("winv", [P, 3])
        lnw = sb("lnw", [P, INNER])
        xn, rnd, xq = sb("xn", [P, ST, E]), sb("rnd", [P, ST, E]), sb("xq", [P, ST, E], BF16)
        am, inv, sx, dg, du = (sb(n, [P, ST]) for n in ("am", "inv", "sx", "dg", "du"))
        xqT = sb("xqT", [P, KT, ST * P], BF16)
        silu = sb("silu", [P, 2, 512])
        h = sb("h", [P, ST, INNER])
        junk = sb("junk", [P, INNER])
        ssq, ms, r, ah, hm, hinv, hs, od, one = (sb(n, [P, ST]) for n in ("ssq", "ms", "r", "ah", "hm", "hinv", "hs", "od", "rr"))
        hr = sb("hr", [P, 2, INNER])
        hq = sb("hq", [P, ST, INNER], BF16)
        hT = sb("hT", [P, 2, FC, P], BF16)
        ln = LayerNorm(nc, c, take, "b_ln", k)
        tpx = ps("tpx", BF16)
        gp = [ps("g0"), ps("g1")]
        up = [ps("u0"), ps("u1")]
        tph = ps("tph", BF16)
        yp = [ps("y0"), ps("y1")]
        wsum = yp[1]
        names = ("loaded", "colsum_done", "wsum_done", "mean_done", "winv_done", "scaled", "clipped", "tern_done", "normed",
                 "am_done", "inv_done", "sx_done", "rnd_done", "xq_done", "turned", "xqT_done", "gu_done", "silu_done",
                 "h_done", "ssq_done", "ms_done", "r_done", "hw_done", "ah_done", "hm_done", "hinv_done", "hs_done",
                 "hr_done", "hq_done", "hturned", "hT_done", "y_done", "x_done", "d_done")
        q = {n: sem(n) for n in names}
        block = c.enter_context(nc.Block())

        @block.sync
        def _(sp):
            for dst, src, n in ((raw[0], "L0_gateT", KT), (raw[1], "L0_upT", KT), (raw[2], "L0_downT", FC)):
                sp.dma_start(dst[:].rearrange("p (c f) -> p c f", c=n), t[src].rearrange("(c p) f -> p c f", p=P)).then_inc(q["loaded"], 16)
            sp.dma_start(lnw[:], t["L0_lnw"].rearrange("(o n) -> o n", o=1).broadcast_to([P, INNER])).then_inc(q["loaded"], 16)

        @block.gpsimd
        def _(pool):
            with pool.Fori(0, GROUPS) as s:
                ln.on_pool(pool, s)
                pool.wait_ge(q["ms_done"], s + 1)
                nc.gpsimd.tensor_tensor(r[:], ms[:], k["half"][:, 0:ST], ALU.pow).then_inc(q["r_done"], 1)

        @block.vector
        def _(dve):
            V = nc.vector
            dve.wait_ge(q["loaded"], 64)
            for n in range(3):
                V.tensor_reduce(colsum[:, n:n + 1], raw[n][:], AX.X, ALU.add, apply_absolute_value=True).then_inc(q["colsum_done"], 1)
            dve.wait_ge(q["wsum_done"], 1)
            V.tensor_scalar(mean[:], wsum[:, 0:3], 1.0 / (E * INNER), QUANT_EPS, ALU.mult, ALU.max).then_inc(q["mean_done"], 1)
            dve.wait_ge(q["mean_done"], 1)
            V.reciprocal(winv[:], mean[:]).then_inc(q["winv_done"], 1)
            dve.wait_ge(q["winv_done"], 1)
            for n in range(3):
                V.tensor_scalar(raw[n][:], raw[n][:], winv[:, n:n + 1], 1.0, ALU.mult, ALU.min).then_inc(q["scaled"], 1)
                dve.wait_ge(q["scaled"], n + 1)
                V.tensor_scalar(raw[n][:], raw[n][:], -1.0, MAGIC, ALU.max, ALU.add).then_inc(q["clipped"], 1)
                dve.wait_ge(q["clipped"], n + 1)
                V.tensor_scalar(tern[n][:], raw[n][:], MAGIC, None, ALU.subtract).then_inc(q["tern_done"], 1)
            with dve.Fori(0, GROUPS) as s:
                def tile(j):
                    return k["x"][:].rearrange("p n e -> p (n e)")[:, bass.ds(s * (ST * E) + j * E, E)]

                ln.on_vector(dve, s, tile, lambda j: xn[:, j, :], q["normed"])
                dve.wait_ge(q["normed"], s * ST + ST)
                V.tensor_reduce(am[:], xn[:], AX.X, ALU.max, apply_absolute_value=True).then_inc(q["am_done"], 1)
                dve.wait_ge(q["am_done"], s + 1)
                V.tensor_scalar(am[:], am[:], QUANT_EPS, 1.0 / 127.0, ALU.max, ALU.mult).then_inc(q["inv_done"], 1)
                dve.wait_ge(q["inv_done"], s + 1)
                V.reciprocal(sx[:], am[:]).then_inc(q["sx_done"], 1)
                V.tensor_scalar(dg[:], am[:], mean[:, 0:1], None, ALU.mult).then_inc(q["d_done"], 1)
                V.tensor_scalar(du[:], am[:], mean[:, 1:2], None, ALU.mult).then_inc(q["d_done"], 1)
                dve.wait_ge(q["sx_done"], s + 1)
                for j in range(ST):
                    V.tensor_scalar(rnd[:, j, :], xn[:, j, :], sx[:, j:j + 1], MAGIC, ALU.mult, ALU.add).then_inc(q["rnd_done"], 1)
                dve.wait_ge(q["rnd_done"], s * ST + ST)
                V.tensor_scalar(xq[:], rnd[:], MAGIC, None, ALU.subtract).then_inc(q["xq_done"], 1)
                dve.wait_ge(q["d_done"], s * 2 + 2)
                for n in range(2 * ST):
                    j, f = n // 2, n % 2
                    dve.wait_ge(q["silu_done"], s * 2 * ST + n + 1)
                    V.scalar_tensor_tensor(h[:, j, f * 512:(f + 1) * 512], up[n % 2][:], du[:, j:j + 1], silu[:, n % 2, :],
                                           ALU.mult, ALU.mult).then_inc(q["h_done"], 1)
                for j in range(ST):
                    dve.wait_ge(q["ssq_done"], s * ST + j + 1)
                    V.tensor_tensor(h[:, j, :], h[:, j, :], lnw[:], ALU.mult).then_inc(q["hw_done"], 1)
                V.tensor_scalar(ms[:], ssq[:], 1.0 / INNER, RMS_EPS, ALU.mult, ALU.add).then_inc(q["ms_done"], 1)
                dve.wait_ge(q["hw_done"], s * ST + ST)
                V.tensor_reduce(ah[:], h[:], AX.X, ALU.max, apply_absolute_value=True).then_inc(q["ah_done"], 1)
                dve.wait_ge(q["ah_done"], s + 1)
                dve.wait_ge(q["r_done"], s + 1)
                V.tensor_tensor(hm[:], ah[:], r[:], ALU.mult).then_inc(q["hm_done"], 1)
                dve.wait_ge(q["hm_done"], s * 2 + 1)
                V.tensor_scalar(hm[:], hm[:], QUANT_EPS, 1.0 / 127.0, ALU.max, ALU.mult).then_inc(q["hm_done"], 1)
                dve.wait_ge(q["hm_done"], s * 2 + 2)
                V.reciprocal(hinv[:], hm[:]).then_inc(q["hinv_done"], 1)
                V.tensor_scalar(od[:], hm[:], mean[:, 2:3], k["gate"][:, 2:3], ALU.mult, ALU.mult).then_inc(q["hinv_done"], 1)
                dve.wait_ge(q["hinv_done"], s * 2 + 2)
                V.tensor_tensor(hs[:], hinv[:], r[:], ALU.mult).then_inc(q["hs_done"], 1)
                dve.wait_ge(q["hs_done"], s + 1)
                for j in range(ST):
                    V.tensor_scalar(hr[:, j % 2, :], h[:, j, :], hs[:, j:j + 1], MAGIC, ALU.mult, ALU.add).then_inc(q["hr_done"], 1)
                    dve.wait_ge(q["hr_done"], s * ST + j + 1)
                    V.tensor_scalar(hq[:, j, :], hr[:, j % 2, :], MAGIC, None, ALU.subtract).then_inc(q["hq_done"], 1)
                for j in range(ST):
                    dve.wait_ge(q["y_done"], s * ST + j + 1)
                    V.scalar_tensor_tensor(tile(j), yp[j % 2][:, 0:E], od[:, j:j + 1], tile(j),
                                           ALU.mult, ALU.add).then_inc(q["x_done"], 1)

        @block.scalar
        def _(act):
            with act.Fori(0, GROUPS) as s:
                act.wait_ge(q["turned"], s + 1)
                nc.scalar.activation(xqT[:].rearrange("p c m -> p (c m)"), tpx[:], ACT.Copy).then_inc(q["xqT_done"], 1)
                act.wait_ge(q["d_done"], s * 2 + 2)
                for n in range(2 * ST):
                    j, f = n // 2, n % 2
                    act.wait_ge(q["gu_done"], s * 2 * ST + n + 1)
                    if n >= 2:
                        act.wait_ge(q["h_done"], s * 2 * ST + n - 1)
                    nc.scalar.activation(silu[:, n % 2, :], gp[n % 2][:], ACT.Silu, scale=dg[:, j:j + 1]).then_inc(q["silu_done"], 1)
                for j in range(ST):
                    act.wait_ge(q["h_done"], s * 2 * ST + 2 * j + 2)
                    if j > 0:
                        act.wait_ge(q["ssq_done"], s * ST + j)
                    nc.scalar.activation(junk[:], h[:, j, :], ACT.Square, accum_out=ssq[:, j:j + 1]).then_inc(q["ssq_done"], 1)
                for j in range(ST):
                    act.wait_ge(q["hturned"], s * ST + j + 1)
                    if j >= 2:
                        act.wait_ge(q["y_done"], s * ST + j - 1)
                    nc.scalar.activation(hT[:, j % 2].rearrange("p c m -> p (c m)"), tph[:], ACT.Copy).then_inc(q["hT_done"], 1)

        @block.tensor
        def _(pe):
            pe.wait_ge(q["colsum_done"], 3)
            nc.tensor.matmul(wsum[:, 0:3], k["ones"][:], colsum[:], start=True, stop=True).then_inc(q["wsum_done"], 1)
            pe.wait_ge(q["tern_done"], 3)
            with pe.Fori(0, GROUPS) as s:
                pe.wait_ge(q["xq_done"], s + 1)
                for j in range(ST):
                    for c_ in range(KT):
                        last = nc.tensor.transpose(tpx[:, (c_ * ST + j) * P:(c_ * ST + j + 1) * P], xq[:, j, c_ * P:(c_ + 1) * P], k["identb"][:])
                last.then_inc(q["turned"], 1)
                pe.wait_ge(q["xqT_done"], s + 1)
                for n in range(2 * ST):
                    j, f = n // 2, n % 2
                    if n >= 2:
                        pe.wait_ge(q["h_done"], s * 2 * ST + n - 1)
                    for w, dst in ((wg, gp[n % 2]), (wu, up[n % 2])):
                        for c_ in range(KT):
                            last = nc.tensor.matmul(dst[:], xqT[:, c_, j * P:(j + 1) * P], w[:, c_, f * 512:(f + 1) * 512],
                                                    start=c_ == 0, stop=c_ == KT - 1)
                    last.then_inc(q["gu_done"], 1)

                def turn(j):
                    pe.wait_ge(q["hq_done"], s * ST + j + 1)
                    if j > 0:
                        pe.wait_ge(q["hT_done"], s * ST + j)
                    for c_ in range(FC):
                        last = nc.tensor.transpose(tph[:, c_ * P:(c_ + 1) * P], hq[:, j, c_ * P:(c_ + 1) * P], k["identb"][:])
                    last.then_inc(q["hturned"], 1)

                def down(j):
                    pe.wait_ge(q["hT_done"], s * ST + j + 1)
                    if j >= 2:
                        pe.wait_ge(q["x_done"], s * ST + j - 1)
                    for c_ in range(FC):
                        last = nc.tensor.matmul(yp[j % 2][:, 0:E], hT[:, j % 2, c_, :], wd[:, c_, :],
                                                start=c_ == 0, stop=c_ == FC - 1)
                    last.then_inc(q["y_done"], 1)

                turn(0)
                for j in range(1, ST):
                    turn(j)
                    down(j - 1)
                down(ST - 1)


def quantize_tokens(nc, t, k):
    with phase_semaphores(nc) as take, ExitStack() as c:
        def sb(name, shape, dt=F32):
            return c.enter_context(nc.sbuf_tensor("n_" + name, shape, dt))

        def sem(name):
            return take("n_" + name)

        N = ST * P
        lw, lb, ins, inv = sb("lw", [P, KT]), sb("lb", [P, KT]), sb("ins", [P, 4 * KT]), sb("inv", [P, 4 * KT])
        xn, xm, lnT = sb("xn", [P, ST, E]), sb("xm", [P, ST, E]), sb("lnT", [P, KT, N])
        yb, kb, big = sb("yb", [P, 2, N], BF16), sb("kb", [P, 2, N], BF16), sb("big", [P, 2, N])
        ln1, ln2 = LayerNorm(nc, c, take, "n_ln1", k), LayerNorm(nc, c, take, "n_ln2", k)
        tp = [c.enter_context(nc.psum_tensor(f"n_tp{i}", [P, N], F32)) for i in range(KT)]
        q = {n: sem(n) for n in ("loaded", "inv_done", "normed", "normed2", "turned", "lnT_done", "y_done", "clipped", "abs_done",
                                 "k_done", "big_done", "xq_done")}
        W = 4 * KT
        block = c.enter_context(nc.Block())

        @block.sync
        def _(sp):
            for dst, src in ((lw, "L1_ln_w"), (lb, "L1_ln_b")):
                sp.dma_start(dst[:], t[src]).then_inc(q["loaded"], 16)
            for n, src in enumerate(("L1_q_in_scale", "L1_k_in_scale", "L1_v_in_scale", "L1_qx_in_scale")):
                sp.dma_start(ins[:, n * KT:(n + 1) * KT], t[src]).then_inc(q["loaded"], 16)

        @block.gpsimd
        def _(pool):
            with pool.Fori(0, GROUPS) as s:
                ln1.on_pool(pool, s)
                ln2.on_pool(pool, s)
                for w in range(W):
                    pool.wait_ge(q["big_done"], s * W + w + 1)
                    out = k["xq"][:].rearrange("p v c n -> p (v c n)")[:, bass.ds(s * N + w * TOK, N)]
                    nc.gpsimd.tensor_tensor(out, big[:, w % 2, :], kb[:, w % 2, :], ALU.subtract).then_inc(q["xq_done"], 1)

        @block.vector
        def _(dve):
            V = nc.vector
            dve.wait_ge(q["loaded"], 96)
            V.reciprocal(inv[:], ins[:]).then_inc(q["inv_done"], 1)
            with dve.Fori(0, GROUPS) as s:
                def tile(j):
                    return k["x"][:].rearrange("p n e -> p (n e)")[:, bass.ds(s * (ST * E) + j * E, E)]

                ln1.on_vector(dve, s, tile, lambda j: xn[:, j, :], q["normed"])
                dve.wait_ge(q["normed"], s * ST + ST)
                ln2.on_vector(dve, s, lambda j: xn[:, j, :], lambda j: xm[:, j, :], q["normed2"])
                for w in range(W):
                    u = w % 2
                    dve.wait_ge(q["y_done"], s * W + w + 1)
                    V.tensor_scalar(yb[:, u, :], yb[:, u, :], FP8_MAX, -FP8_MAX, ALU.min, ALU.max).then_inc(q["clipped"], 1)
                    dve.wait_ge(q["clipped"], s * W + w + 1)
                    if w >= 2:
                        dve.wait_ge(q["xq_done"], s * W + w - 1)
                    V.tensor_scalar(kb[:, u, :].bitcast(U16), yb[:, u, :].bitcast(U16), 0x7FFF, None, ALU.bitwise_and).then_inc(q["abs_done"], 1)
                    dve.wait_ge(q["abs_done"], s * W + w + 1)
                    V.tensor_scalar(kb[:, u, :], kb[:, u, :], FP8_LEAST, FP8_SHIFT, ALU.max, ALU.mult).then_inc(q["k_done"], 1)
                    dve.wait_ge(q["k_done"], s * W + w + 1)
                    V.tensor_tensor(big[:, u, :], yb[:, u, :], kb[:, u, :], ALU.add).then_inc(q["big_done"], 1)
                dve.wait_ge(q["xq_done"], s * W + W)

        @block.scalar
        def _(act):
            act.wait_ge(q["loaded"], 96)
            act.wait_ge(q["inv_done"], 1)
            with act.Fori(0, GROUPS) as s:
                act.wait_ge(q["turned"], s + 1)
                for c_ in range(KT):
                    nc.scalar.activation(lnT[:, c_, :], tp[c_][:], ACT.Identity, bias=lb[:, c_:c_ + 1],
                                         scale=lw[:, c_:c_ + 1]).then_inc(q["lnT_done"], 1)
                act.wait_ge(q["lnT_done"], s * KT + KT)
                for w in range(W):
                    if w >= 2:
                        act.wait_ge(q["big_done"], s * W + w - 1)
                    nc.scalar.activation(yb[:, w % 2, :], lnT[:, w % KT, :], ACT.Copy, scale=inv[:, w:w + 1]).then_inc(q["y_done"], 1)

        @block.tensor
        def _(pe):
            with pe.Fori(0, GROUPS) as s:
                for j in range(ST):
                    pe.wait_ge(q["normed2"], s * ST + j + 1)
                    for c_ in range(KT):
                        last = nc.tensor.transpose(tp[c_][:, j * P:(j + 1) * P], xm[:, j, c_ * P:(c_ + 1) * P], k["ident"][:])
                last.then_inc(q["turned"], 1)


def gqa_pass(nc, t, k, cross):
    L = "x" if cross else "c"
    with phase_semaphores(nc) as take, ExitStack() as c:
        def sb(name, shape, dt=F32):
            return c.enter_context(nc.sbuf_tensor(f"{L}_{name}", shape, dt))

        def ps(name):
            return c.enter_context(nc.psum_tensor(f"{L}_{name}", [P, 512], F32))

        def sem(name):
            return take(f"{L}_{name}")

        CH = 512
        NQ, NK = HEADS * D // CH, KV * D // CH
        NN = NQ + NK
        NC = NN + NK
        SPLIT = NQ if cross else NC
        NV = 1 if cross else 3
        GH = KV // 2
        w_hi, w_lo = sb("w_hi", [P, SPLIT, KT, CH], F32R), sb("w_lo", [P, SPLIT, KT, CH], F32R)
        w_ctx = sb("w_ctx", [P, NC - SPLIT, KT, CH]) if cross else None
        p_hi, p_lo = sb("p_hi", [P, HEADS, E], F32R), sb("p_lo", [P, HEADS, E], F32R)
        qkT = sb("qkT", [P, 2, HEADS + KV, P])
        v = sb("v", [P, 2, KV * D])
        stage = [qkT[:, 0, 0:8, :].rearrange("p h d -> p (h d)"), qkT[:, 0, 8:16, :].rearrange("p h d -> p (h d)"),
                 qkT[:, 1, 0:8, :].rearrange("p h d -> p (h d)")]
        NS = len(stage)
        wsum = sb("wsum", [P, 2, 8])
        xqc = sb("xqc", [P, NV, KT, P], F32R)
        ctxT = sb("ctxT", [P, KT, TOK]) if cross else None
        ctxc = sb("ctxc", [P, KT, P]) if cross else None
        sq, ss = sb("sq", [P, 2, CH]), sb("ss", [P, 2, 4])
        ve, rs, qn = sb("ve", [P, 2, 4]), sb("rs", [P, 2, 4]), sb("qn", [P, 2, CH])
        ex = sb("ex", [P, 2, CH])
        mx, sm, rc = sb("mx", [P, 2, 8]), sb("sm", [P, 2, 8]), sb("rc", [P, 2, 8])
        pT = sb("pT", [P, 2, GH, P])
        yb, kb, big = sb("yb", [P, 2, CH], BF16), sb("kb", [P, 2, CH], BF16), sb("big", [P, 2, CH])
        cat = sb("cat", [P, 2, 2 * GH, P], F32R)
        smooth, ismooth = sb("smooth", [P, HEADS]), sb("ismooth", [P, HEADS])
        insc = sb("insc", [P, 3, KT])
        wsc = sb("wsc", [P, 3])
        sc = sb("sc", [P, 3, KT])
        lnp = sb("lnp", [P, 4])
        pscale, coef = sb("pscale", [P, 2]), sb("coef", [P, 2])

        qp = [ps("qp0"), ps("qp1")]
        tq, sp_, pp, yp = ps("tq"), ps("scores"), ps("pp"), ps("yp")
        op = [ps("op0"), ps("op1")]

        names = ("small", "w_loaded0", "w_loaded1", "w_loaded2", "ctx_loaded", "prep", "wsum_done", "mean_done", "centred", "hi_done", "lo_done",
                 "xqc_done", "qkv_done", "turned", "sc_done", "pt_done", "pv_done", "y_done", "sq_done", "tev_done",
                 "vev_done", "exp_done", "ptev_done", "ss_done", "qn_done", "max_done", "sub_done", "sum_done", "rec_done",
                 "pn_done", "q1_done", "clipped", "abs_done", "k_done", "big_done", "cat_done", "x_done", "ve_done", "rs_done")
        q = {n: sem(n) for n in names}

        w_loaded = [q[f"w_loaded{i}"] for i in range(NS)]

        kinds = [("q", i) for i in range(NQ)] + [("k", i) for i in range(NK)] + [("v", i) for i in range(NK)]
        kinds = [x for x in kinds if not (cross and x[0] == "v")] + [("p", i) for i in range(4)]
        source = {"q": "L1_wqxT" if cross else "L1_wqT", "k": "L1_wkvxT" if cross else "L1_wkT", "v": "L1_wvT"}
        variant = {"q": 0, "k": 1, "v": 2}
        half = HEADS * D if cross else 0
        centre_count = [sum(x[0] in "qk" for x in kinds[:n + 1]) for n in range(len(kinds))]
        split_kinds = [x[0] in "qvp" or not cross for x in kinds]
        split_count = [sum(split_kinds[:n + 1]) for n in range(len(kinds))]
        hi_parts = [0 if not s else (1 if x[0] == "p" else KT) for x, s in zip(kinds, split_kinds)]
        hi_count = [sum(hi_parts[:n + 1]) for n in range(len(kinds))]

        with nc.Block() as block:
            @block.sync
            def _(sp):
                if not cross:
                    small = [(insc[:, n, :], t[f"L1_{m}_in_scale"]) for n, m in enumerate("qkv")]
                    small += [(wsc[:, n:n + 1], t[f"L1_w{m}_scale"].rearrange("(o n) -> o n", o=1).broadcast_to([P, 1])) for n, m in enumerate("qkv")]
                else:
                    small = [(insc[:, 0, :], t["L1_qx_in_scale"]),
                             (wsc[:, 0:1], t["L1_wqx_scale"].rearrange("(o n) -> o n", o=1).broadcast_to([P, 1]))]
                small += [(smooth[:], t["L1_smoothT"][:, HEADS * cross:HEADS * (cross + 1)])]
                x_ = "x" if cross else ""
                small += [(lnp[:, n:n + 1], t[f"L1_{m}"].rearrange("(d o) -> d o", o=1))
                          for n, m in enumerate((f"q{x_}ln_w", f"q{x_}ln_b", f"k{x_}ln_w", f"k{x_}ln_b"))]
                small += [(pscale[:, n:n + 1], t[m].rearrange("(o n) -> o n", o=1).broadcast_to([P, 1]))
                          for n, m in enumerate(("L1_proj_in_scale", "L1_proj_w_scale"))]
                for dst, src in small:
                    sp.dma_start(dst, src).then_inc(q["small"], 16)
                k["small"] = 16 * len(small)
                for n, (kind, i) in enumerate(kinds):
                    if n >= NS:
                        if split_kinds[n - NS]:
                            sp.wait_ge(q["lo_done"], split_count[n - NS])
                        else:
                            sp.wait_ge(q["centred"], centre_count[n - NS])
                    if kind == "p":
                        dst = stage[n % NS].rearrange("p (h f) -> p h f", h=4)
                        src = t["L1_wprojT"][half + i * CH:half + (i + 1) * CH, :].rearrange("(h d) f -> d h f", d=D)
                    else:
                        dst = stage[n % NS].rearrange("p (c f) -> p c f", c=KT)
                        src = t[source[kind]][:, i * CH:(i + 1) * CH].rearrange("(c p) f -> p c f", p=P)
                    sp.dma_start(dst, src).then_inc(w_loaded[n % NS], 16)
                if cross:
                    for i in range(NK):
                        lo = KV * D + i * CH
                        sp.dma_start(w_ctx[:, NK + i], t["L1_wkvxT"][:, lo:lo + CH].rearrange("(c p) f -> p c f", p=P)).then_inc(q["ctx_loaded"], 16)
                    sp.dma_start(ctxT[:], t["ctxT"].rearrange("(c p) n -> p c n", p=P)).then_inc(q["ctx_loaded"], 16)
                    sp.wait_ge(q["ctx_loaded"], 16 * (NK + 1))

            @block.scalar
            def _(act):
                act.wait_ge(q["prep"], 3 if not cross else 1)
                for n, (kind, i) in enumerate(kinds):
                    if not split_kinds[n]:
                        continue
                    if kind in "qk":
                        act.wait_ge(q["centred"], centre_count[n])
                    act.wait_ge(w_loaded[n % NS], 16 * (n // NS + 1))
                    if kind == "p":
                        nc.scalar.activation(p_hi[:, 4 * i:4 * i + 4, :], stage[n % NS].rearrange("p (h f) -> p h f", h=4), ACT.Copy).then_inc(q["hi_done"], 1)
                    else:
                        at = i + {"q": 0, "k": NQ, "v": NN}[kind]
                        for c_ in range(KT):
                            nc.scalar.activation(w_hi[:, at, c_, :], stage[n % NS][:, c_ * CH:(c_ + 1) * CH], ACT.Copy,
                                                 scale=sc[:, variant[kind], c_:c_ + 1]).then_inc(q["hi_done"], 1)

            @block.vector
            def _(dve):
                V = nc.vector
                dve.wait_ge(q["small"], k["small"])
                for n in range(1 if cross else 3):
                    V.tensor_scalar(sc[:, n, :], insc[:, n, :], wsc[:, n:n + 1], None, ALU.mult).then_inc(q["prep"], 1)
                V.reciprocal(ismooth[:], smooth[:])
                V.tensor_tensor(coef[:, 0:1], pscale[:, 0:1], pscale[:, 1:2], ALU.mult).then_inc(q["prep"], 1)
                dve.wait_ge(q["prep"], 2 if cross else 4)
                V.tensor_tensor(coef[:, 1:2], coef[:, 0:1], k["gate"][:, 1:2], ALU.mult)
                for n, (kind, i) in enumerate(kinds):
                    dve.wait_ge(w_loaded[n % NS], 16 * (n // NS + 1))
                    st = stage[n % NS]
                    if kind in "qk":
                        m = centre_count[n]
                        heads = st.rearrange("p (h d) -> p h d", d=D)
                        V.tensor_reduce(wsum[:, m % 2, :], heads, AX.X, ALU.add).then_inc(q["wsum_done"], 1)
                        dve.wait_ge(q["wsum_done"], m)
                        V.tensor_scalar(wsum[:, m % 2, :], wsum[:, m % 2, :], 1.0 / D, None, ALU.mult).then_inc(q["mean_done"], 1)
                        dve.wait_ge(q["mean_done"], m)
                        out = heads if split_kinds[n] else w_ctx[:, i].rearrange("p c (h d) -> p (c h) d", d=D)
                        V.tensor_tensor(out, heads, bcast(wsum[:, m % 2, :], 2, D), ALU.subtract).then_inc(q["centred"], 1)
                    if split_kinds[n]:
                        dve.wait_ge(q["hi_done"], hi_count[n])
                        if kind == "p":
                            V.tensor_tensor(p_lo[:, 4 * i:4 * i + 4, :], st.rearrange("p (h f) -> p h f", h=4),
                                            p_hi[:, 4 * i:4 * i + 4, :].bitcast(F32), ALU.subtract).then_inc(q["lo_done"], 1)
                        else:
                            at = i + {"q": 0, "k": NQ, "v": NN}[kind]
                            for c_ in range(KT):
                                last = V.scalar_tensor_tensor(w_lo[:, at, c_, :], st[:, c_ * CH:(c_ + 1) * CH], sc[:, variant[kind], c_:c_ + 1],
                                                              w_hi[:, at, c_, :].bitcast(F32), ALU.mult, ALU.subtract)
                            last.then_inc(q["lo_done"], 1)

        def run(eng, ahead, both, alone):
            ahead(0, 0, True)
            both(0, 0, True)
            both(1, 1, False)
            with eng.Fori(1, TILES // 2 - 1) as i:
                both(i * 2, 0, False)
                both(i * 2 + 1, 1, False)
            both(TILES - 2, 0, False)
            alone(TILES - 1, 1, False)

        with nc.Block() as block:
            @block.gpsimd
            def _(pool):
                G = nc.gpsimd

                def copy_tile(n, first):
                    if not first:
                        pool.wait_ge(q["qkv_done"], n * NC)
                    for v_ in range(NV):
                        base = (3 if cross else v_) * KT * TOK
                        src = k["xq"][:].rearrange("p v c n -> p (v c n)")
                        for c_ in range(KT):
                            at = n * P + (base + c_ * TOK)
                            last = G.tensor_copy(xqc[:, v_, c_, :], src[:, bass.ds(at, P)])
                            if cross:
                                last = G.tensor_copy(ctxc[:, c_, :], ctxT[:].rearrange("p c n -> p (c n)")[:, bass.ds(n * P + c_ * TOK, P)])
                    last.then_inc(q["xqc_done"], 1)

                def rstd(n, i, first):
                    u = i % 2
                    if not (first and i < 2):
                        pool.wait_ge(q["qn_done"], n * NN + i - 1)
                    pool.wait_ge(q["ve_done"], n * NN + i + 1)
                    G.tensor_tensor(rs[:, u, :], ve[:, u, :], k["half"][:, 0:4], ALU.pow).then_inc(q["rs_done"], 1)

                def fp8(n, m, first):
                    pool.wait_ge(q["big_done"], n * 4 + m + 1)
                    if not first:
                        pool.wait_ge(q["y_done"], n)
                    h, b = m // 2, m % 2
                    G.tensor_tensor(cat[:, h, :, b * SEQ:(b + 1) * SEQ], big[:, b, :].rearrange("p (h s) -> p h s", s=SEQ),
                                    kb[:, b, :].rearrange("p (h s) -> p h s", s=SEQ), ALU.subtract).then_inc(q["cat_done"], 1)

                def ahead(n, par, first):
                    copy_tile(n, first)
                    for i in range(NN):
                        rstd(n, i, first)

                def both(n, par, first):
                    copy_tile(n + 1, False)
                    rstd(n + 1, 0, False)
                    rstd(n + 1, 1, False)
                    for m in range(4):
                        rstd(n + 1, m + 2, False)
                        fp8(n, m, first)

                def alone(n, par, first):
                    for m in range(4):
                        fp8(n, m, first)

                run(pool, ahead, both, alone)

            @block.vector
            def _(dve):
                V = nc.vector

                def sums(n, i):
                    dve.wait_ge(q["sq_done"], n * NN + i + 1)
                    V.tensor_reduce(ss[:, i % 2, :], sq[:, i % 2, :].rearrange("p (h d) -> p h d", d=D), AX.X, ALU.add).then_inc(q["ss_done"], 1)
                    dve.wait_ge(q["ss_done"], n * NN + i + 1)
                    V.tensor_scalar(ve[:, i % 2, :], ss[:, i % 2, :], 1.0 / D, LN_EPS, ALU.mult, ALU.add).then_inc(q["ve_done"], 1)

                def scale(n, i, first):
                    dve.wait_ge(q["rs_done"], n * NN + i + 1)
                    if not (first and i < 2):
                        dve.wait_ge(q["turned"], n * NN + i - 1)
                    V.tensor_tensor(qn[:, i % 2, :].rearrange("p (h d) -> p h d", d=D), qp[i % 2][:].rearrange("p (h d) -> p h d", d=D),
                                    bcast(rs[:, i % 2, :], 2, D), ALU.mult).then_inc(q["qn_done"], 1)

                def less_max(n, h, first):
                    dve.wait_ge(q["sc_done"], n * 2 + h + 1)
                    s3 = sp_[:].rearrange("p (g s) -> p g s", s=SEQ)
                    V.tensor_reduce(mx[:, h, :], s3, AX.X, ALU.max).then_inc(q["max_done"], 1)
                    dve.wait_ge(q["max_done"], n * 2 + h + 1)
                    if not first:
                        dve.wait_ge(q["pt_done"], n * 2 + h - 1)
                    V.tensor_tensor(ex[:, h, :].rearrange("p (g s) -> p g s", s=SEQ), s3, bcast(mx[:, h, :], 2, SEQ),
                                    ALU.subtract).then_inc(q["sub_done"], 1)

                def normalise(n, h):
                    e3 = ex[:, h, :].rearrange("p (g s) -> p g s", s=SEQ)
                    dve.wait_ge(q["exp_done"], n * 2 + h + 1)
                    V.tensor_reduce(sm[:, h, :], e3, AX.X, ALU.add).then_inc(q["sum_done"], 1)
                    dve.wait_ge(q["sum_done"], n * 2 + h + 1)
                    V.reciprocal(rc[:, h, :], sm[:, h, :]).then_inc(q["rec_done"], 1)
                    dve.wait_ge(q["rec_done"], n * 2 + h + 1)
                    V.tensor_tensor(e3, e3, bcast(rc[:, h, :], 2, SEQ), ALU.mult).then_inc(q["pn_done"], 1)

                def fp8(n, m, first):
                    h, u = m // 2, m % 2
                    dve.wait_ge(q["pv_done"], n * 2 + h + 1)
                    V.tensor_tensor(yb[:, u, :].rearrange("p (h s) -> p h s", s=SEQ), op[u][:].rearrange("p (h s) -> p h s", s=SEQ),
                                    bcast(ismooth[:, 2 * GH * h:2 * GH * (h + 1)], 2, SEQ), ALU.mult).then_inc(q["q1_done"], 1)
                    dve.wait_ge(q["q1_done"], n * 4 + m + 1)
                    V.tensor_scalar(yb[:, u, :], yb[:, u, :], FP8_MAX, -FP8_MAX, ALU.min, ALU.max).then_inc(q["clipped"], 1)
                    dve.wait_ge(q["clipped"], n * 4 + m + 1)
                    if not (first and m < 2):
                        dve.wait_ge(q["cat_done"], n * 4 + m - 1)
                    V.tensor_scalar(kb[:, u, :].bitcast(U16), yb[:, u, :].bitcast(U16), 0x7FFF, None, ALU.bitwise_and).then_inc(q["abs_done"], 1)
                    dve.wait_ge(q["abs_done"], n * 4 + m + 1)
                    V.tensor_scalar(kb[:, u, :], kb[:, u, :], FP8_LEAST, FP8_SHIFT, ALU.max, ALU.mult).then_inc(q["k_done"], 1)
                    dve.wait_ge(q["k_done"], n * 4 + m + 1)
                    V.tensor_tensor(big[:, u, :], yb[:, u, :], kb[:, u, :], ALU.add).then_inc(q["big_done"], 1)

                def add_x(n):
                    tile = k["x"][:].rearrange("p n e -> p (n e)")[:, bass.ds(n * E, E)]
                    dve.wait_ge(q["y_done"], n + 1)
                    V.scalar_tensor_tensor(tile, yp[:, 0:E], coef[:, 1:2], tile, ALU.mult, ALU.add).then_inc(q["x_done"], 1)

                def ahead(n, par, first):
                    sums(n, 0)
                    for i in range(1, NN):
                        sums(n, i)
                        scale(n, i - 1, first)
                    scale(n, NN - 1, first)

                def both(n, par, first):
                    m = n + 1
                    less_max(n, 0, first)
                    sums(m, 0)
                    sums(m, 1)
                    scale(m, 0, False)
                    less_max(n, 1, first)
                    normalise(n, 0)
                    sums(m, 2)
                    scale(m, 1, False)
                    normalise(n, 1)
                    sums(m, 3)
                    scale(m, 2, False)
                    fp8(n, 0, first)
                    sums(m, 4)
                    scale(m, 3, False)
                    fp8(n, 1, first)
                    sums(m, 5)
                    scale(m, 4, False)
                    fp8(n, 2, first)
                    scale(m, 5, False)
                    fp8(n, 3, first)
                    add_x(n)

                def alone(n, par, first):
                    less_max(n, 0, first)
                    less_max(n, 1, first)
                    normalise(n, 0)
                    normalise(n, 1)
                    for m in range(4):
                        fp8(n, m, first)
                    add_x(n)

                run(dve, ahead, both, alone)

            @block.scalar
            def _(act):
                A = nc.scalar

                def square(n, i, first):
                    act.wait_ge(q["qkv_done"], n * NC + i + 1)
                    if not (first and i < 2):
                        act.wait_ge(q["ss_done"], n * NN + i - 1)
                    A.activation(sq[:, i % 2, :], qp[i % 2][:], ACT.Square).then_inc(q["sq_done"], 1)

                def keep_qk(n, i, par):
                    act.wait_ge(q["turned"], n * NN + i + 1)
                    w = 0 if i < NQ else 2
                    A.activation(qkT[:, par, 4 * i:4 * i + 4, :], tq[:].rearrange("p (h m) -> p h m", h=4), ACT.Identity,
                                 bias=lnp[:, w + 1:w + 2], scale=lnp[:, w:w + 1]).then_inc(q["tev_done"], 1)

                def keep_v(n, i, par):
                    act.wait_ge(q["qkv_done"], n * NC + NN + i + 1)
                    A.activation(v[:, par, i * CH:(i + 1) * CH], qp[(NN + i) % 2][:], ACT.Copy).then_inc(q["vev_done"], 1)

                def exponent(n, h):
                    act.wait_ge(q["sub_done"], n * 2 + h + 1)
                    A.activation(ex[:, h, :], ex[:, h, :], ACT.Exp, scale=D ** -0.5).then_inc(q["exp_done"], 1)

                def keep_pT(n, h):
                    act.wait_ge(q["pt_done"], n * 2 + h + 1)
                    A.activation(pT[:, h], pp[:].rearrange("p (g m) -> p g m", g=GH), ACT.Copy).then_inc(q["ptev_done"], 1)

                def ahead(n, par, first):
                    square(n, 0, first)
                    square(n, 1, first)
                    for i in range(2, NN):
                        keep_qk(n, i - 2, par)
                        square(n, i, first)
                    keep_v(n, 0, par)
                    keep_qk(n, NN - 2, par)
                    keep_v(n, 1, par)
                    keep_qk(n, NN - 1, par)

                def both(n, par, first):
                    m, mp = n + 1, 1 - par
                    square(m, 0, False)
                    square(m, 1, False)
                    exponent(n, 0)
                    keep_qk(m, 0, mp)
                    square(m, 2, False)
                    exponent(n, 1)
                    keep_pT(n, 0)
                    keep_qk(m, 1, mp)
                    square(m, 3, False)
                    keep_pT(n, 1)
                    keep_qk(m, 2, mp)
                    square(m, 4, False)
                    keep_qk(m, 3, mp)
                    square(m, 5, False)
                    keep_v(m, 0, mp)
                    keep_qk(m, 4, mp)
                    keep_v(m, 1, mp)
                    keep_qk(m, 5, mp)

                def alone(n, par, first):
                    exponent(n, 0)
                    exponent(n, 1)
                    keep_pT(n, 0)
                    keep_pT(n, 1)

                run(act, ahead, both, alone)

            @block.tensor
            def _(pe):
                T = nc.tensor

                def project(n, i, first):
                    if i == 0:
                        pe.wait_ge(q["xqc_done"], n + 1)
                    if i >= 2:
                        if i - 2 < NN:
                            pe.wait_ge(q["qn_done"], n * NN + i - 1)
                        else:
                            pe.wait_ge(q["vev_done"], n * NK + i - 1 - NN)
                    elif not first:
                        pe.wait_ge(q["vev_done"], n * NK - 1 + i)
                    bank = qp[i % 2][:]
                    if i < SPLIT:
                        v_ = 0 if i < NQ else 1 if i < NN else 2
                        for c_ in range(KT):
                            for part in range(2):
                                last = T.matmul(bank, xqc[:, v_, c_, :], (w_hi, w_lo)[part][:, i, c_, :],
                                                start=c_ == 0 and part == 0, stop=c_ == KT - 1 and part == 1)
                    else:
                        for c_ in range(KT):
                            last = T.matmul(bank, ctxc[:, c_, :], w_ctx[:, i - SPLIT, c_, :], start=c_ == 0, stop=c_ == KT - 1)
                    last.then_inc(q["qkv_done"], 1)

                def turn(n, i, first):
                    pe.wait_ge(q["qn_done"], n * NN + i + 1)
                    if not (first and i == 0):
                        pe.wait_ge(q["tev_done"], n * NN + i)
                    for h in range(4):
                        out = tq[:, h * P:(h + 1) * P]
                        if i < NQ:
                            out = tq[:].rearrange("p (g b h s) -> p g h b s", g=2, b=2, h=2)[:, h // 2, h % 2]
                        last = T.transpose(out, qn[:, i % 2, h * D:(h + 1) * D], k["ident"][:])
                    last.then_inc(q["turned"], 1)

                def scores(n, h, par, first):
                    pe.wait_ge(q["tev_done"], n * NN + NN)
                    if not (first and h == 0):
                        pe.wait_ge(q["sub_done"], n * 2 + h)
                    for g in range(GH):
                        kv = h * GH + g
                        for b in range(2):
                            rows = slice(b * SEQ, (b + 1) * SEQ)
                            last = T.matmul(sp_[:, (g * 2 + b) * SEQ:(g * 2 + b + 1) * SEQ], qkT[:, par, 2 * kv + b, :],
                                            qkT[:, par, HEADS + kv, rows], start=True, stop=True)
                    last.then_inc(q["sc_done"], 1)

                def turn_p(n, h, first):
                    pe.wait_ge(q["pn_done"], n * 2 + h + 1)
                    if not (first and h == 0):
                        pe.wait_ge(q["ptev_done"], n * 2 + h)
                    for g in range(GH):
                        last = T.transpose(pp[:, g * P:(g + 1) * P], ex[:, h, g * P:(g + 1) * P], k["ident"][:])
                    last.then_inc(q["pt_done"], 1)

                def attend(n, h, par, first):
                    pe.wait_ge(q["ptev_done"], n * 2 + h + 1)
                    pe.wait_ge(q["vev_done"], n * NK + NK)
                    if not (first and h == 0):
                        pe.wait_ge(q["q1_done"], n * 4 + h * 2)
                    for g in range(GH):
                        kv = h * GH + g
                        for b in range(2):
                            rows = slice(b * SEQ, (b + 1) * SEQ)
                            last = T.matmul(op[b][:, g * P:(g + 1) * P], v[rows, par, kv * D:(kv + 1) * D], pT[rows, h, g, :],
                                            start=True, stop=True)
                    last.then_inc(q["pv_done"], 1)

                def output(n, h, first):
                    pe.wait_ge(q["cat_done"], n * 4 + h * 2 + 2)
                    if h == 0 and not first:
                        pe.wait_ge(q["x_done"], n)
                    for i in range(2 * GH):
                        hd = 2 * GH * h + i
                        for part in range(2):
                            last = T.matmul(yp[:, 0:E], cat[:, h, i, :], (p_hi, p_lo)[part][:, hd, :],
                                            start=hd == 0 and part == 0, stop=hd == HEADS - 1 and part == 1)
                    if h == 1:
                        last.then_inc(q["y_done"], 1)

                def ahead(n, par, first):
                    project(n, 0, first)
                    project(n, 1, first)
                    for i in range(2, NC):
                        turn(n, i - 2, first)
                        project(n, i, first)

                def both(n, par, first):
                    m = n + 1
                    scores(n, 0, par, first)
                    project(m, 0, False)
                    project(m, 1, False)
                    scores(n, 1, par, first)
                    turn(m, 0, False)
                    project(m, 2, False)
                    turn_p(n, 0, first)
                    turn(m, 1, False)
                    project(m, 3, False)
                    attend(n, 0, par, first)
                    turn_p(n, 1, first)
                    turn(m, 2, False)
                    project(m, 4, False)
                    turn(m, 3, False)
                    attend(n, 1, par, first)
                    project(m, 5, False)
                    output(n, 0, first)
                    turn(m, 4, False)
                    project(m, 6, False)
                    turn(m, 5, False)
                    project(m, 7, False)
                    output(n, 1, first)

                def alone(n, par, first):
                    scores(n, 0, par, first)
                    scores(n, 1, par, first)
                    turn_p(n, 0, first)
                    turn_p(n, 1, first)
                    attend(n, 0, par, first)
                    attend(n, 1, par, first)
                    output(n, 0, first)
                    output(n, 1, first)

                run(pe, ahead, both, alone)


def moe(nc, t, k):
    with phase_semaphores(nc) as take, ExitStack() as c:
        def sb(name, shape, dt=F32):
            return c.enter_context(nc.sbuf_tensor("m_" + name, shape, dt))

        def ps(name):
            return c.enter_context(nc.psum_tensor("m_" + name, [P, 512], F32))

        def sem(name):
            return take("m_" + name)

        N, NE, X = ST * P, EXPERTS + 1, EXPERTS
        w1, wg, w2 = sb("w1", [P, 2, KT, E]), sb("wg", [P, 2, KT, E]), sb("w2", [P, 2, KT, E])
        gw, gb, eb = sb("gw", [P, KT, X]), sb("gb", [P, X]), sb("eb", [P, X])
        earlier = sb("earlier", [P, X, X])
        xn, xnT = sb("xn", [P, ST, E]), sb("xnT", [P, KT, TOK])
        lg, pr, bp = sb("lg", [P, ST, X]), sb("pr", [P, ST, X]), sb("bp", [P, ST, X])
        mx, sm = sb("mx", [P, ST]), sb("sm", [P, ST])
        gt, eq = sb("gt", [P, ST, X * X]), sb("eq", [P, ST, X * X])
        rank = sb("rank", [P, ST, X])
        we = sb("we", [P, GROUPS * ST, NE])
        silu, h = sb("silu", [P, 2, N]), sb("h", [P, 2, KT, N])
        ln = LayerNorm(nc, c, take, "m_ln", k)
        ap_, gp = [ps("a0"), ps("a1")], [ps("g0"), ps("g1")]
        yp = [ps("y0"), ps("y1")]
        tp = ap_
        lp = gp[0]
        names = ("loaded", "w_loaded0", "w_loaded1", "normed", "turned", "xnT_done", "lg_done", "lb_done", "mx_done", "sub_done",
                 "exp_done", "sm_done", "rec_done", "pr_done", "bp_done", "gt_done", "eq_done", "eqm_done", "sum_done", "rank_done",
                 "sel_done", "ws_done", "wr_done", "wg_done", "we_done", "ag_done", "silu_done", "h_done", "y_done", "x_done", "ones_done",
                 "earlier_done")
        q = {n: sem(n) for n in names}
        w_loaded = [q["w_loaded0"], q["w_loaded1"]]
        UNITS = NE * GROUPS

        with nc.Block() as block:
            @block.sync
            def _(sp):
                sp.dma_start(gw[:], t["L1_gate_w"].rearrange("(c p) x -> p c x", p=P)).then_inc(q["loaded"], 16)
                for dst, src in ((gb, "L1_gate_b"), (eb, "L1_biases")):
                    sp.dma_start(dst[:], t[src].rearrange("(o n) -> o n", o=1).broadcast_to([P, X])).then_inc(q["loaded"], 16)

            @block.gpsimd
            def _(pool):
                nc.gpsimd.memset(earlier[:], 1.0).then_inc(q["ones_done"], 1)
                pool.wait_ge(q["ones_done"], 1)
                nc.gpsimd.affine_select(out=earlier[:], in_=earlier[:], compare_op=ALU.is_gt, fill=0.0, base=0,
                                        pattern=[[1, X], [-1, X]], channel_multiplier=0).then_inc(q["earlier_done"], 1)
                with pool.Fori(0, GROUPS) as s:
                    ln.on_pool(pool, s)

            @block.vector
            def _(dve):
                V = nc.vector
                dve.wait_ge(q["loaded"], 48)
                dve.wait_ge(q["earlier_done"], 1)
                with dve.Fori(0, GROUPS) as s:
                    def tile(j):
                        return k["x"][:].rearrange("p n e -> p (n e)")[:, bass.ds(s * (ST * E) + j * E, E)]

                    ln.on_vector(dve, s, tile, lambda j: xn[:, j, :], q["normed"])
                    dve.wait_ge(q["lg_done"], s + 1)
                    V.tensor_tensor(lg[:], lp[:, 0:ST * X].rearrange("p (j x) -> p j x", x=X), bcast(gb[:], 1, ST), ALU.add).then_inc(q["lb_done"], 1)
                    dve.wait_ge(q["lb_done"], s + 1)
                    V.tensor_reduce(mx[:], lg[:], AX.X, ALU.max).then_inc(q["mx_done"], 1)
                    dve.wait_ge(q["mx_done"], s + 1)
                    V.tensor_tensor(lg[:], lg[:], bcast(mx[:], 2, X), ALU.subtract).then_inc(q["sub_done"], 1)
                    dve.wait_ge(q["exp_done"], s + 1)
                    V.tensor_reduce(sm[:], lg[:], AX.X, ALU.add).then_inc(q["sm_done"], 1)
                    dve.wait_ge(q["sm_done"], s + 1)
                    V.reciprocal(sm[:], sm[:]).then_inc(q["rec_done"], 1)
                    dve.wait_ge(q["rec_done"], s + 1)
                    V.tensor_tensor(pr[:], lg[:], bcast(sm[:], 2, X), ALU.mult).then_inc(q["pr_done"], 1)
                    dve.wait_ge(q["pr_done"], s + 1)
                    V.tensor_tensor(bp[:], pr[:], bcast(eb[:], 1, ST), ALU.add).then_inc(q["bp_done"], 1)
                    dve.wait_ge(q["bp_done"], s + 1)
                    for j in range(ST):
                        other, own = bcast(bp[:, j, :], 1, X), bcast(bp[:, j, :], 2, X)
                        V.tensor_tensor(gt[:, j, :].rearrange("p (e o) -> p e o", o=X), other, own, ALU.is_gt).then_inc(q["gt_done"], 1)
                        V.tensor_tensor(eq[:, j, :].rearrange("p (e o) -> p e o", o=X), other, own, ALU.is_equal).then_inc(q["eq_done"], 1)
                    dve.wait_ge(q["eq_done"], s * ST + ST)
                    V.tensor_tensor(eq[:], eq[:], bcast(earlier[:].rearrange("p e o -> p (e o)"), 1, ST), ALU.mult).then_inc(q["eqm_done"], 1)
                    dve.wait_ge(q["eqm_done"], s + 1)
                    dve.wait_ge(q["gt_done"], s * ST + ST)
                    V.tensor_tensor(gt[:], gt[:], eq[:], ALU.add).then_inc(q["sum_done"], 1)
                    dve.wait_ge(q["sum_done"], s + 1)
                    V.tensor_reduce(rank[:].rearrange("p j x -> p (j x)"), gt[:].rearrange("p j (e o) -> p (j e) o", o=X), AX.X, ALU.add).then_inc(q["rank_done"], 1)
                    dve.wait_ge(q["rank_done"], s + 1)
                    V.scalar_tensor_tensor(rank[:], rank[:], TOP_K - 0.5, pr[:], ALU.is_lt, ALU.mult).then_inc(q["sel_done"], 1)
                    dve.wait_ge(q["sel_done"], s + 1)
                    V.tensor_reduce(sm[:], rank[:], AX.X, ALU.add).then_inc(q["ws_done"], 1)
                    dve.wait_ge(q["ws_done"], s + 1)
                    V.reciprocal(sm[:], sm[:]).then_inc(q["wr_done"], 1)
                    dve.wait_ge(q["wr_done"], s + 1)
                    V.tensor_scalar(sm[:], sm[:], k["gate"][:, 3:4], None, ALU.mult).then_inc(q["wg_done"], 1)
                    dve.wait_ge(q["wg_done"], s + 1)
                    table = we[:].rearrange("p n x -> p (n x)")[:, bass.ds(s * (ST * NE), ST * NE)].rearrange("p (n x) -> p n x", x=NE)
                    V.tensor_tensor(table[:, :, 1:NE], rank[:], bcast(sm[:], 2, X), ALU.mult).then_inc(q["we_done"], 1)
                V.tensor_scalar(we[:, :, 0], k["ones"][:, 0:GROUPS * ST], k["gate"][:, 3:4], None, ALU.mult)

            @block.scalar
            def _(act):
                with act.Fori(0, GROUPS) as s:
                    act.wait_ge(q["turned"], s + 1)
                    for c_ in range(KT):
                        nc.scalar.activation(xnT[:].rearrange("p c n -> p (c n)")[:, bass.ds(s * N + c_ * TOK, N)], tp[c_][:],
                                             ACT.Copy).then_inc(q["xnT_done"], 1)
                    act.wait_ge(q["sub_done"], s + 1)
                    nc.scalar.activation(lg[:], lg[:], ACT.Exp).then_inc(q["exp_done"], 1)

            @block.tensor
            def _(pe):
                for s in range(GROUPS):
                    if s > 0:
                        pe.wait_ge(q["xnT_done"], s * KT)
                    for j in range(ST):
                        pe.wait_ge(q["normed"], s * ST + j + 1)
                        for c_ in range(KT):
                            last = nc.tensor.transpose(tp[c_][:, j * P:(j + 1) * P], xn[:, j, c_ * P:(c_ + 1) * P], k["ident"][:])
                    last.then_inc(q["turned"], 1)
                    pe.wait_ge(q["xnT_done"], (s + 1) * KT)
                    if s > 0:
                        pe.wait_ge(q["lb_done"], s)
                    for j in range(ST):
                        for c_ in range(KT):
                            at = s * N + j * P
                            last = nc.tensor.matmul(lp[:, j * X:(j + 1) * X], xnT[:, c_, at:at + P], gw[:, c_, :],
                                                    start=c_ == 0, stop=c_ == KT - 1)
                    last.then_inc(q["lg_done"], 1)

        def run(eng, first_product, second_product):
            first_product(0, 0, True)
            for n in range(1, 4):
                first_product(n, n, True)
                second_product(n - 1, n - 1, True)
            with eng.Fori(1, UNITS // 4) as i:
                for u in range(4):
                    first_product(i * 4 + u, u, False)
                    second_product(i * 4 + (u - 1), (u - 1) % 4, u == 0 and None)
            second_product(UNITS - 1, 3, False)

        with nc.Block() as block:
            @block.sync
            def _(sp):
                def load(e, par):
                    for w, src in ((w1, "L1_W1"), (wg, "L1_Wg"), (w2, "L1_W2")):
                        flat = t[src].rearrange("x k f -> (x k) f")[bass.ds(e * E, E), :]
                        sp.dma_start(w[:, par], flat.rearrange("(c p) f -> p c f", p=P)).then_inc(w_loaded[par], 16)

                load(0, 0)
                load(1, 1)
                with sp.Fori(1, NE // 2) as i:
                    sp.wait_ge(q["y_done"], i * 4 - 2)
                    load(i * 2, 0)
                    sp.wait_ge(q["y_done"], i * 4)
                    load(i * 2 + 1, 1)

            @block.scalar
            def _(act):
                def silus(n, u, first):
                    for f in range(KT):
                        act.wait_ge(q["ag_done"], n * KT + f + 1)
                        if not (first and u == 0):
                            act.wait_ge(q["h_done"], n * KT + f - 1)
                        nc.scalar.activation(silu[:, f, :], ap_[f][:], ACT.Silu).then_inc(q["silu_done"], 1)

                run(act, silus, lambda n, u, first: None)

            @block.vector
            def _(dve):
                def product(n, u, first):
                    for f in range(KT):
                        dve.wait_ge(q["silu_done"], n * KT + f + 1)
                        nc.vector.tensor_tensor(h[:, u % 2, f, :], silu[:, f, :], gp[f][:], ALU.mult).then_inc(q["h_done"], 1)

                def add_x(n, u, first):
                    e_off = n // 2 if isinstance(n, int) else None
                    for j in range(ST):
                        dve.wait_ge(q["y_done"], n + 1) if j == 0 else None
                        row = (u % 2) * ST + j
                        tile = k["x"][:, row, :]
                        if e_off is None:
                            at = we[:].rearrange("p n x -> p (n x)")[:, bass.ds((n - u % 2) // 2 + row * NE, 1)]
                        else:
                            at = we[:, row, e_off:e_off + 1]
                        nc.vector.scalar_tensor_tensor(tile, yp[j // 2][:, (j % 2) * E:(j % 2 + 1) * E], at, tile,
                                                       ALU.mult, ALU.add).then_inc(q["x_done"], 1)

                run(dve, product, add_x)

            @block.tensor
            def _(pe):
                def first_products(n, u, first):
                    s, par = u % 2, u // 2
                    if s == 0:
                        e3 = (n // 4 + 1) if isinstance(n, int) else (n - u) // 4 + 1
                        pe.wait_ge(w_loaded[par], e3 * 48)
                    for f in range(KT):
                        if not (first and u == 0):
                            pe.wait_ge(q["h_done"], n * KT + f - 1)
                        for w, dst in ((w1, ap_[f]), (wg, gp[f])):
                            for c_ in range(KT):
                                last = nc.tensor.matmul(dst[:], w[:, par, c_, f * P:(f + 1) * P], xnT[:, c_, s * N:(s + 1) * N],
                                                        start=c_ == 0, stop=c_ == KT - 1)
                        last.then_inc(q["ag_done"], 1)

                def second_product(n, u, first):
                    par = u // 2
                    pe.wait_ge(q["h_done"], n * KT + KT)
                    if not (isinstance(n, int) and n == 0):
                        pe.wait_ge(q["x_done"], n * ST)
                    for j in range(ST):
                        for f in range(KT):
                            last = nc.tensor.matmul(yp[j // 2][:, (j % 2) * E:(j % 2 + 1) * E], h[:, u % 2, f, j * P:(j + 1) * P],
                                                    w2[:, par, f, :], start=f == 0, stop=f == KT - 1)
                    last.then_inc(q["y_done"], 1)

                run(pe, first_products, second_product)


def kernel(**a):
    import numpy as np
    import concourse.bacc as bacc
    from concourse.bass_utils import run_bass_kernel_spmd

    def arr(name):
        return np.ascontiguousarray(a[name])

    def columns(name):
        return np.ascontiguousarray(np.asarray(a[name]).reshape(-1, P).T)

    def turned(name):
        return np.ascontiguousarray(np.asarray(a[name]).T)

    ins = {
        "x": arr("x").reshape(TOK, E),
        "ctxT": np.ascontiguousarray(arr("ctx_2048").reshape(TOK, E).T),
        "mask": arr("mask_BxSxS2_ff0").reshape(TOK, SEQ),
        "g_xattn": arr("g_xattn"), "g_ffn": arr("g_ffn"),
        "L0_WqT": turned("L0_xattn_Wq"), "L0_WkT": turned("L0_xattn_Wk"), "L0_WvT": turned("L0_xattn_Wv"),
        "L0_bq": columns("L0_xattn_bq"), "L0_bk": columns("L0_xattn_bk"), "L0_bv": arr("L0_xattn_bv"),
        "L0_gateT": turned("L0_ffn_w_gate"), "L0_upT": turned("L0_ffn_w_up"), "L0_downT": turned("L0_ffn_w_down"),
        "L0_lnw": arr("L0_ffn_ln_weight"),
        "L1_wqT": turned("L1_xattn_wq"), "L1_wkT": turned("L1_xattn_wk"), "L1_wvT": turned("L1_xattn_wv"),
        "L1_wqxT": turned("L1_xattn_wqx"), "L1_wkvxT": turned("L1_xattn_w_kv_x"), "L1_wprojT": turned("L1_xattn_wproj"),
        "L1_smoothT": np.ascontiguousarray(arr("L1_xattn_proj_smooth").reshape(2 * HEADS, D).T),
        "L1_gate_w": arr("L1_ffn_gate_w"), "L1_gate_b": arr("L1_ffn_gate_b"), "L1_biases": arr("L1_ffn_biases"),
        "L1_W1": np.concatenate([arr("L1_ffn_Ws1")[None], arr("L1_ffn_W1")]),
        "L1_Wg": np.concatenate([arr("L1_ffn_Wsg")[None], arr("L1_ffn_Wg")]),
        "L1_W2": np.concatenate([arr("L1_ffn_Ws2")[None], arr("L1_ffn_W2")]),
    }
    for n in ("ln_w", "ln_b", "q_in_scale", "k_in_scale", "v_in_scale", "qx_in_scale"):
        ins["L1_" + n] = columns("L1_xattn_" + n)
    for n in ("qln_w", "qln_b", "kln_w", "kln_b",
              "qxln_w", "qxln_b", "kxln_w", "kxln_b"):
        ins["L1_" + n] = arr("L1_xattn_" + n)
    for n in ("wq_scale", "wk_scale", "wv_scale", "wqx_scale", "proj_in_scale", "proj_w_scale"):
        ins["L1_" + n] = arr("L1_xattn_" + n).reshape(1)

    nc = bacc.Bacc("TRN2", target_bir_lowering=False, num_devices=1)
    t = {n: nc.dram_tensor("in_" + n, v.shape, mybir.dt.from_np(v.dtype), kind="ExternalInput").ap() for n, v in ins.items()}
    t["out"] = nc.dram_tensor("out_x", (TOK, E), F32, kind="ExternalOutput").ap()
    flamingo_program(nc, t)
    r = run_bass_kernel_spmd(nc, [{"in_" + n: v for n, v in ins.items()}], core_ids=[0])
    return np.asarray(r.results[0]["out_x"]).reshape(BATCH, SEQ, E)
```

```python
from contextlib import ExitStack, contextmanager
from itertools import islice

import concourse.bass as bass
from concourse import mybir

F32 = mybir.dt.float32
F32R = mybir.dt.float32r
BF16 = mybir.dt.bfloat16
U16 = mybir.dt.uint16
ALU = mybir.AluOpType
ACT = mybir.ActivationFunctionType
AX = mybir.AxisListType

P = 128
BATCH, SEQ, E = 16, 64, 256
TOK = BATCH * SEQ
TILES = TOK // P
KT = E // P
ST = 4
GROUPS = TILES // ST
INNER = 1024
HEADS, KV, D = 16, 8, 128
EXPERTS, TOP_K = 7, 3
MAGIC = 1.5 * 2.0 ** 23
FP8_MAX = 448.0
FP8_LEAST = 1.5 * 2.0 ** -6
FP8_SHIFT = 2.0 ** 20
LN_EPS, RMS_EPS, QUANT_EPS = 1e-5, 1e-6, 1e-5


def bcast(ap, axis, n):
    shape = list(ap.shape)
    shape.insert(axis, n)
    return ap.unsqueeze(axis).broadcast_to(shape)


@contextmanager
def phase_semaphores(nc):
    taken = []

    def take(name):
        taken.append(nc.alloc_semaphore(name=name))
        return taken[-1]

    yield take
    nc.clear_and_free_semaphores(taken)
    nc.all_engine_barrier()


def flamingo_program(nc, t):
    ctx = ExitStack()
    with ctx:
        def sb(name, shape, dt=F32):
            return ctx.enter_context(nc.sbuf_tensor(name, shape, dt))

        k = {
            "x": sb("x_res", [P, TILES, E]),
            "ident": sb("ident", [P, P]),
            "identb": sb("identb", [P, P], BF16),
            "ones": sb("ones", [P, P]),
            "half": sb("neg_half", [P, 32]),
            "gate": sb("gate", [P, 4]),
        }
        setup(nc, t, k)
        with ExitStack() as right, ExitStack() as left:
            over_tokens = PassWeights(nc, left, k, cross=False)
            with ExitStack() as c:
                tern = Ternary(nc, c)
                attention0(nc, t, k, tern)
                bitnet(nc, t, k, tern, over_tokens)
            k["xq"] = right.enter_context(nc.sbuf_tensor("xq_all", [P, 4, KT, TOK], BF16, side="right"))
            quantize_tokens(nc, t, k)
            gqa_pass(nc, t, k, over_tokens)
            left.close()
            over_context = PassWeights(nc, left, k, cross=True)
            prepare_pass(nc, t, over_context)
            gqa_pass(nc, t, k, over_context)
        moe(nc, t, k)
        with nc.semaphore("stored") as stored, nc.Block() as block:
            @block.sync
            def _(sp):
                sp.dma_start(t["out"].rearrange("(n p) e -> p n e", p=P), k["x"][:]).then_inc(stored, 16)
                sp.wait_ge(stored, 16)


def setup(nc, t, k):
    with phase_semaphores(nc) as take, ExitStack() as c:
        loaded = take("setup_loaded")
        filled = take("setup_filled")
        made = take("setup_made")
        raw = c.enter_context(nc.sbuf_tensor("gate_raw", [P, 4], F32))
        block = c.enter_context(nc.Block())

        @block.sync
        def _(sp):
            sp.dma_start(k["x"][:], t["x"].rearrange("(n p) e -> p n e", p=P)).then_inc(loaded, 16)
            sp.dma_start(raw[:, 0:2], t["g_xattn"].rearrange("(o n) -> o n", o=1).broadcast_to([P, 2])).then_inc(loaded, 16)
            sp.dma_start(raw[:, 2:4], t["g_ffn"].rearrange("(o n) -> o n", o=1).broadcast_to([P, 2])).then_inc(loaded, 16)

        @block.gpsimd
        def _(pool):
            nc.gpsimd.memset(k["ident"][:], 0.0).then_inc(filled, 1)
            nc.gpsimd.memset(k["ones"][:], 1.0)
            nc.gpsimd.memset(k["half"][:], -0.5)
            pool.wait_ge(filled, 1)
            nc.gpsimd.affine_select(out=k["ident"][:], in_=k["ident"][:], compare_op=ALU.not_equal, fill=1.0,
                                    base=0, pattern=[[-1, P]], channel_multiplier=1).then_inc(made, 1)
            pool.wait_ge(made, 1)
            nc.gpsimd.tensor_copy(k["identb"][:], k["ident"][:]).then_inc(made, 1)
            pool.wait_ge(made, 2)

        @block.scalar
        def _(act):
            act.wait_ge(loaded, 48)
            nc.scalar.activation(k["gate"][:], raw[:], ACT.Tanh)


class LayerNorm:

    def __init__(self, nc, c, take, name, k):
        self.nc, self.k = nc, k
        self.stats = c.enter_context(nc.sbuf_tensor(name + "_stats", [P, ST, 6], F32))
        self.mv = c.enter_context(nc.sbuf_tensor(name + "_mv", [P, ST, 2], F32))
        self.ve = c.enter_context(nc.sbuf_tensor(name + "_ve", [P, ST], F32))
        self.rstd = c.enter_context(nc.sbuf_tensor(name + "_rstd", [P, ST], F32))
        self.stats_done = take(name + "_stats_done")
        self.mv_done = take(name + "_mv_done")
        self.ve_done = take(name + "_ve_done")
        self.rstd_done = take(name + "_rstd_done")

    def on_vector(self, dve, s, source, out, normed):
        for j in range(ST):
            self.nc.vector.bn_stats(self.stats[:, j, :], source(j)).then_inc(self.stats_done, 1)
        dve.wait_ge(self.stats_done, (s + 1) * ST)
        self.nc.vector.memset(self.ve[:, 0:1], 0.0)
        for j in range(ST):
            self.nc.vector.bn_aggr(self.mv[:, j, :], self.stats[:, j, :]).then_inc(self.mv_done, 1)
        dve.wait_ge(self.mv_done, (s + 1) * ST)
        self.nc.vector.tensor_scalar(self.ve[:], self.mv[:, :, 1], 1.0, LN_EPS, ALU.mult, ALU.add).then_inc(self.ve_done, 1)
        dve.wait_ge(self.rstd_done, s + 1)
        for j in range(ST):
            self.nc.vector.tensor_scalar(out(j), source(j), self.mv[:, j, 0:1], self.rstd[:, j:j + 1],
                                         ALU.subtract, ALU.mult).then_inc(normed, 1)

    def on_pool(self, pool, s):
        pool.wait_ge(self.ve_done, s + 1)
        self.nc.gpsimd.tensor_tensor(self.rstd[:], self.ve[:], self.k["half"][:, 0:ST], ALU.pow).then_inc(self.rstd_done, 1)


def take_steps(eng, steps, n):
    for step in islice(steps, n):
        step(eng)


class Ternary:

    def __init__(self, nc, c):
        def sb(name, shape, dt=F32):
            return c.enter_context(nc.sbuf_tensor("tern_" + name, shape, dt, side="right"))

        self.nc = nc
        self.values = [sb(n, [P, KT * INNER], BF16) for n in ("gate", "up", "down")]
        self.mean = sb("mean", [P, 3])

    def begin(self, c, take):
        self.raw = [c.enter_context(self.nc.sbuf_tensor("tern_raw_" + n, [P, KT * INNER], F32)) for n in ("gate", "up", "down")]
        self.colsum = c.enter_context(self.nc.sbuf_tensor("tern_colsum", [P, 3], F32))
        self.inverse = c.enter_context(self.nc.sbuf_tensor("tern_inverse", [P, 3], F32))
        self.wsum = c.enter_context(self.nc.psum_tensor("tern_wsum", [P, 512], F32))
        self.loaded = [take(f"tern_loaded{n}") for n in range(3)]
        self.colsum_done, self.wsum_done, self.mean_done = take("tern_colsum_done"), take("tern_wsum_done"), take("tern_mean_done")
        self.inverse_done, self.scaled, self.clipped = take("tern_inverse_done"), take("tern_scaled"), take("tern_clipped")

    def on_sync(self, sp, t):
        for n, (src, slices) in enumerate((("L0_gateT", KT), ("L0_upT", KT), ("L0_downT", INNER // P))):
            sp.dma_start(self.raw[n][:].rearrange("p (c f) -> p c f", c=slices),
                         t[src].rearrange("(c p) f -> p c f", p=P)).then_inc(self.loaded[n], 16)

    def on_scalar(self, act, n):
        act.wait_ge(self.loaded[n], 16)
        self.nc.scalar.activation(self.values[n][:], self.raw[n][:], ACT.Abs, accum_out=self.colsum[:, n:n + 1]).then_inc(self.colsum_done, 1)

    def on_tensor(self, pe, k):
        pe.wait_ge(self.colsum_done, 3)
        self.nc.tensor.matmul(self.wsum[:, 0:3], k["ones"][:], self.colsum[:], start=True, stop=True).then_inc(self.wsum_done, 1)

    def means(self, dve):
        dve.wait_ge(self.wsum_done, 1)
        self.nc.vector.tensor_scalar(self.mean[:], self.wsum[:, 0:3], 1.0 / (E * INNER), QUANT_EPS, ALU.mult, ALU.max).then_inc(self.mean_done, 1)
        dve.wait_ge(self.mean_done, 1)
        self.nc.vector.reciprocal(self.inverse[:], self.mean[:]).then_inc(self.inverse_done, 1)
        dve.wait_ge(self.inverse_done, 1)

    def scaling(self, dve, n):
        self.nc.vector.tensor_scalar(self.raw[n][:], self.raw[n][:], self.inverse[:, n:n + 1], 1.0, ALU.mult, ALU.min).then_inc(self.scaled, 1)

    def clipping(self, dve, n):
        dve.wait_ge(self.scaled, n + 1)
        self.nc.vector.tensor_scalar(self.raw[n][:], self.raw[n][:], -1.0, MAGIC, ALU.max, ALU.add).then_inc(self.clipped, 1)

    def rounding(self, dve, n):
        dve.wait_ge(self.clipped, n + 1)
        self.nc.vector.tensor_scalar(self.values[n][:], self.raw[n][:], MAGIC, None, ALU.subtract)

    def on_vector(self):
        yield self.means
        for step in (self.scaling, self.clipping, self.rounding):
            for n in range(3):
                yield lambda dve, step=step, n=n: step(dve, n)


class PassWeights:

    CH = 512
    NQ, NK = HEADS * D // 512, KV * D // 512
    STAGES = 3

    def __init__(self, nc, c, k, cross):
        L = "x" if cross else "c"

        def sb(name, shape, dt=F32):
            return c.enter_context(nc.sbuf_tensor(f"{L}_{name}", shape, dt))

        self.nc, self.k, self.cross, self.L = nc, k, cross, L
        split = self.NQ if cross else self.NQ + 2 * self.NK
        self.w_hi, self.w_lo = sb("w_hi", [P, split, KT, self.CH], F32R), sb("w_lo", [P, split, KT, self.CH], F32R)
        self.w_ctx = sb("w_ctx", [P, 2 * self.NK, KT, self.CH]) if cross else None
        self.p_hi, self.p_lo = sb("p_hi", [P, HEADS, E], F32R), sb("p_lo", [P, HEADS, E], F32R)
        self.smooth, self.ismooth = sb("smooth", [P, HEADS]), sb("ismooth", [P, HEADS])
        self.insc, self.wsc, self.sc = sb("insc", [P, 3, KT]), sb("wsc", [P, 3]), sb("sc", [P, 3, KT])
        self.lnp, self.pscale, self.coef = sb("lnp", [P, 4]), sb("pscale", [P, 2]), sb("coef", [P, 2])
        self.kinds = [("q", i) for i in range(self.NQ)] + [("k", i) for i in range(self.NK)]
        self.kinds += [] if cross else [("v", i) for i in range(self.NK)]
        self.kinds += [("p", i) for i in range(4)]
        self.split = [not cross or kind in "qp" for kind, _ in self.kinds]

    def count(self, n, what):
        return sum(what(m) for m in range(n + 1))

    def centred_count(self, n):
        return self.count(n, lambda m: self.kinds[m][0] in "qk")

    def hi_count(self, n):
        return self.count(n, lambda m: self.split[m])

    def vector_lo_count(self, n):
        return self.count(n, lambda m: self.split[m] and self.kinds[m][0] != "p")

    def pool_lo_count(self, n):
        return self.count(n, lambda m: self.kinds[m][0] == "p")

    def begin(self, c, take):
        L, nc = self.L, self.nc
        self.stage = [c.enter_context(nc.sbuf_tensor(f"{L}_stage{i}", [P, KT * self.CH], F32)) for i in range(self.STAGES)]
        self.sums = c.enter_context(nc.sbuf_tensor(f"{L}_sums", [P, self.STAGES, 8], F32))
        self.small, self.scales = take(f"{L}_small"), take(f"{L}_scales")
        self.loaded = [take(f"{L}_loaded{i}") for i in range(self.STAGES)]
        self.sum_done, self.mean_done, self.centred = take(f"{L}_wsum_done"), take(f"{L}_wmean_done"), take(f"{L}_centred")
        self.hi_done, self.lo_done, self.plo_done = take(f"{L}_hi_done"), take(f"{L}_lo_done"), take(f"{L}_plo_done")
        self.rest_loaded = take(f"{L}_rest_loaded")

    def slot(self, n):
        kind, i = self.kinds[n]
        return i + {"q": 0, "k": self.NQ, "v": self.NQ + self.NK, "p": 0}[kind]

    def on_sync(self, sp, t):
        x_ = "x" if self.cross else ""
        kinds = ("q",) if self.cross else ("q", "k", "v")
        small = [(self.insc[:, n, :], t[f"L1_{m}{x_}_in_scale"]) for n, m in enumerate(kinds)]
        small += [(self.wsc[:, n:n + 1], t[f"L1_w{m}{x_}_scale"].rearrange("(o n) -> o n", o=1).broadcast_to([P, 1])) for n, m in enumerate(kinds)]
        small += [(self.smooth[:], t["L1_smoothT"][:, HEADS * self.cross:HEADS * (self.cross + 1)])]
        small += [(self.lnp[:, n:n + 1], t[f"L1_{m}"].rearrange("(d o) -> d o", o=1))
                  for n, m in enumerate((f"q{x_}ln_w", f"q{x_}ln_b", f"k{x_}ln_w", f"k{x_}ln_b"))]
        small += [(self.pscale[:, n:n + 1], t[m].rearrange("(o n) -> o n", o=1).broadcast_to([P, 1]))
                  for n, m in enumerate(("L1_proj_in_scale", "L1_proj_w_scale"))]
        self.small_count = 16 * len(small)
        for dst, src in small:
            sp.dma_start(dst, src).then_inc(self.small, 16)
        source = {"q": "L1_wqxT" if self.cross else "L1_wqT", "k": "L1_wkvxT" if self.cross else "L1_wkT", "v": "L1_wvT"}
        half = HEADS * D if self.cross else 0
        for n, (kind, i) in enumerate(self.kinds):
            stage = self.stage[n % self.STAGES]
            if n >= self.STAGES:
                m = n - self.STAGES
                if self.kinds[m][0] == "p":
                    sp.wait_ge(self.plo_done, self.pool_lo_count(m))
                elif self.split[m]:
                    sp.wait_ge(self.lo_done, self.vector_lo_count(m))
                else:
                    sp.wait_ge(self.centred, self.centred_count(m))
            if kind == "p":
                dst = stage[:].rearrange("p (h f) -> p h f", h=4)
                src = t["L1_wprojT"][half + i * self.CH:half + (i + 1) * self.CH, :].rearrange("(h d) f -> d h f", d=D)
            else:
                dst = stage[:].rearrange("p (c f) -> p c f", c=KT)
                src = t[source[kind]][:, i * self.CH:(i + 1) * self.CH].rearrange("(c p) f -> p c f", p=P)
            sp.dma_start(dst, src).then_inc(self.loaded[n % self.STAGES], 16)
        if self.cross:
            for i in range(self.NK):
                lo = KV * D + i * self.CH
                sp.dma_start(self.w_ctx[:, self.NK + i], t["L1_wkvxT"][:, lo:lo + self.CH].rearrange("(c p) f -> p c f", p=P)).then_inc(self.rest_loaded, 16)
            sp.wait_ge(self.rest_loaded, 16 * self.NK)

    def arrived(self, eng, n):
        eng.wait_ge(self.loaded[n % self.STAGES], 16 * (n // self.STAGES + 1))

    def scale(self, dve):
        V = self.nc.vector
        dve.wait_ge(self.small, self.small_count)
        for n in range(1 if self.cross else 3):
            V.tensor_scalar(self.sc[:, n, :], self.insc[:, n, :], self.wsc[:, n:n + 1], None, ALU.mult).then_inc(self.scales, 1)
        V.reciprocal(self.ismooth[:], self.smooth[:]).then_inc(self.scales, 1)
        V.tensor_tensor(self.coef[:, 0:1], self.pscale[:, 0:1], self.pscale[:, 1:2], ALU.mult).then_inc(self.scales, 1)
        dve.wait_ge(self.scales, 3 if self.cross else 5)
        V.tensor_tensor(self.coef[:, 1:2], self.coef[:, 0:1], self.k["gate"][:, 1:2], ALU.mult).then_inc(self.scales, 1)

    def mean(self, dve, n):
        V, s = self.nc.vector, self.sums[:, n % self.STAGES, :]
        self.arrived(dve, n)
        V.tensor_reduce(s, self.stage[n % self.STAGES][:].rearrange("p (h d) -> p h d", d=D), AX.X, ALU.add).then_inc(self.sum_done, 1)
        dve.wait_ge(self.sum_done, self.centred_count(n))
        V.tensor_scalar(s, s, 1.0 / D, None, ALU.mult).then_inc(self.mean_done, 1)

    def low(self, dve, n):
        dve.wait_ge(self.hi_done, self.hi_count(n))
        kind, at = self.kinds[n][0], self.slot(n)
        for c_ in range(KT):
            last = self.nc.vector.scalar_tensor_tensor(
                self.w_lo[:, at, c_, :], self.stage[n % self.STAGES][:, c_ * self.CH:(c_ + 1) * self.CH],
                self.sc[:, "qkv".index(kind), c_:c_ + 1], self.w_hi[:, at, c_, :].bitcast(F32), ALU.mult, ALU.subtract)
        last.then_inc(self.lo_done, 1)

    def on_vector(self):
        yield self.scale
        for n in range(len(self.kinds) + 1):
            if n < len(self.kinds) and self.kinds[n][0] in "qk":
                yield lambda dve, n=n: self.mean(dve, n)
            if n > 0 and self.split[n - 1] and self.kinds[n - 1][0] != "p":
                yield lambda dve, n=n: self.low(dve, n - 1)

    def high(self, act, n):
        kind, at = self.kinds[n][0], self.slot(n)
        if kind in "qk":
            act.wait_ge(self.centred, self.centred_count(n))
        self.arrived(act, n)
        if kind == "p":
            last = self.nc.scalar.activation(self.p_hi[:, 4 * at:4 * at + 4, :].rearrange("p h f -> p (h f)"), self.stage[n % self.STAGES][:], ACT.Copy)
        else:
            for c_ in range(KT):
                last = self.nc.scalar.activation(self.w_hi[:, at, c_, :], self.stage[n % self.STAGES][:, c_ * self.CH:(c_ + 1) * self.CH],
                                                 ACT.Copy, scale=self.sc[:, "qkv".index(kind), c_:c_ + 1])
        last.then_inc(self.hi_done, 1)

    def on_scalar(self):
        yield lambda act: act.wait_ge(self.scales, 4 if self.cross else 6)
        for n in range(len(self.kinds)):
            if self.split[n]:
                yield lambda act, n=n: self.high(act, n)

    def centre(self, pool, n):
        pool.wait_ge(self.mean_done, self.centred_count(n))
        heads = self.stage[n % self.STAGES][:].rearrange("p (h d) -> p h d", d=D)
        out = heads if self.split[n] else self.w_ctx[:, self.kinds[n][1]].rearrange("p c (h d) -> p (c h) d", d=D)
        self.nc.gpsimd.tensor_tensor(out, heads, bcast(self.sums[:, n % self.STAGES, :], 2, D), ALU.subtract).then_inc(self.centred, 1)

    def low_output(self, pool, n):
        at = slice(4 * self.kinds[n][1], 4 * self.kinds[n][1] + 4)
        pool.wait_ge(self.hi_done, self.hi_count(n))
        self.nc.gpsimd.tensor_tensor(self.p_lo[:, at, :].rearrange("p h f -> p (h f)"), self.stage[n % self.STAGES][:],
                                     self.p_hi[:, at, :].rearrange("p h f -> p (h f)").bitcast(F32), ALU.subtract).then_inc(self.plo_done, 1)

    def on_pool(self):
        for n, (kind, _) in enumerate(self.kinds):
            if kind in "qk":
                yield lambda pool, n=n: self.centre(pool, n)
            if kind == "p":
                yield lambda pool, n=n: self.low_output(pool, n)


def prepare_pass(nc, t, weights):
    with phase_semaphores(nc) as take, ExitStack() as c:
        weights.begin(c, take)
        block = c.enter_context(nc.Block())

        @block.sync
        def _(sp):
            weights.on_sync(sp, t)

        @block.vector
        def _(dve):
            for step in weights.on_vector():
                step(dve)

        @block.scalar
        def _(act):
            for step in weights.on_scalar():
                step(act)

        @block.gpsimd
        def _(pool):
            for step in weights.on_pool():
                step(pool)


def attention0(nc, t, k, tern):
    with phase_semaphores(nc) as take, ExitStack() as c:
        def sb(name, shape, dt=F32):
            return c.enter_context(nc.sbuf_tensor("a_" + name, shape, dt))

        def ps(name):
            return c.enter_context(nc.psum_tensor("a_" + name, [P, 512], F32))

        def sem(name):
            return take("a_" + name)

        wq, wk, wv = sb("wq", [P, KT, E]), sb("wk", [P, KT, E]), sb("wv", [P, KT, E])
        bq, bk, bv = sb("bq", [P, KT]), sb("bk", [P, KT]), sb("bv", [P, E])
        mask = sb("mask", [P, TILES, SEQ])
        xn, xnT = sb("xn", [P, ST, E]), sb("xnT", [P, KT, ST * P])
        qT, kT = sb("qT", [P, KT, ST * P]), sb("kT", [P, KT, ST * P])
        v = sb("v", [P, ST, E])
        s_ = sb("s", [P, ST, SEQ])
        mx, sm, rc = sb("mx", [P, ST]), sb("sm", [P, ST]), sb("rc", [P, ST])
        probs = sb("probs", [P, ST, P])
        pT = sb("pT", [P, ST, P])
        ln = LayerNorm(nc, c, take, "a_ln", k)
        tp = [ps("tp0"), ps("tp1")]
        qk = [ps("qk0"), ps("qk1")]
        vo = [ps("vo0"), ps("vo1")]
        sp_ = ps("scores")
        loaded, normed, turned, xnT_done = sem("loaded"), sem("normed"), sem("turned"), sem("xnT_done")
        qk_done, qk_kept, v_done, v_kept = sem("qk_done"), sem("qk_kept"), sem("v_done"), sem("v_kept")
        sc_done, masked, max_done, sub_done = sem("sc_done"), sem("masked"), sem("max_done"), sem("sub_done")
        exp_done, sum_done, rec_done, probs_done = sem("exp_done"), sem("sum_done"), sem("rec_done"), sem("probs_done")
        pT_turned, pT_kept, o_done, x_done, zeroed = (sem("pT_turned"), sem("pT_kept"), sem("o_done"), sem("x_done"),
                                                      sem("zeroed"))
        tern.begin(c, take)
        block = c.enter_context(nc.Block())

        @block.sync
        def _(sp):
            for dst, src in ((wq, "L0_WqT"), (wk, "L0_WkT"), (wv, "L0_WvT")):
                sp.dma_start(dst[:], t[src].rearrange("(c p) f -> p c f", p=P)).then_inc(loaded, 16)
            for dst, src in ((bq, "L0_bq"), (bk, "L0_bk")):
                sp.dma_start(dst[:], t[src]).then_inc(loaded, 16)
            sp.dma_start(bv[:], t["L0_bv"].rearrange("(o n) -> o n", o=1).broadcast_to([P, E])).then_inc(loaded, 16)
            sp.dma_start(mask[:], t["mask"].rearrange("(n p) s -> p n s", p=P)).then_inc(loaded, 16)
            tern.on_sync(sp, t)

        @block.gpsimd
        def _(pool):
            nc.gpsimd.memset(probs[:], 0.0).then_inc(zeroed, 1)
            for s in range(GROUPS):
                ln.on_pool(pool, s)

        @block.vector
        def _(dve):
            dve.wait_ge(loaded, 7 * 16)
            dve.wait_ge(zeroed, 1)
            steps = tern.on_vector()
            for s in range(GROUPS):
                def tile(j):
                    return k["x"][:].rearrange("p n e -> p (n e)")[:, bass.ds(s * (ST * E) + j * E, E)]

                ln.on_vector(dve, s, tile, lambda j: xn[:, j, :], normed)
                take_steps(dve, steps, 4 if s > 0 else 0)
                for h in range(2):
                    dve.wait_ge(v_done, s * 2 + h + 1)
                    nc.vector.tensor_tensor(v[:, 2 * h:2 * h + 2, :], vo[h][:].rearrange("p (n e) -> p n e", n=2),
                                            bcast(bv[:], 1, 2), ALU.add).then_inc(v_kept, 1)
                take_steps(dve, steps, 3 if s > 0 else 0)
                dve.wait_ge(sc_done, s + 1)
                for b in range(2):
                    rows = slice(b * SEQ, (b + 1) * SEQ)
                    nc.vector.scalar_tensor_tensor(
                        s_[rows], sp_[rows].rearrange("p (n m) -> p n m", n=ST)[:, :, b * SEQ:(b + 1) * SEQ], E ** -0.5,
                        mask[rows].rearrange("p n s -> p (n s)")[:, bass.ds(s * (ST * SEQ), ST * SEQ)].rearrange("p (n s) -> p n s", n=ST),
                        ALU.mult, ALU.add).then_inc(masked, 1)
                dve.wait_ge(masked, s * 2 + 2)
                nc.vector.tensor_reduce(mx[:], s_[:], AX.X, ALU.max).then_inc(max_done, 1)
                dve.wait_ge(max_done, s + 1)
                nc.vector.tensor_tensor(s_[:], s_[:], bcast(mx[:], 2, SEQ), ALU.subtract).then_inc(sub_done, 1)
                dve.wait_ge(exp_done, s + 1)
                nc.vector.tensor_reduce(sm[:], s_[:], AX.X, ALU.add).then_inc(sum_done, 1)
                dve.wait_ge(sum_done, s + 1)
                nc.vector.reciprocal(rc[:], sm[:]).then_inc(rec_done, 1)
                dve.wait_ge(rec_done, s + 1)
                for b in range(2):
                    rows = slice(b * SEQ, (b + 1) * SEQ)
                    nc.vector.tensor_tensor(probs[rows, :, b * SEQ:(b + 1) * SEQ], s_[rows], bcast(rc[rows], 2, SEQ),
                                            ALU.mult).then_inc(probs_done, 1)
                take_steps(dve, steps, 2 if s > 0 else 0)
                for j in range(ST):
                    dve.wait_ge(o_done, s * 2 + j // 2 + 1)
                    nc.vector.scalar_tensor_tensor(tile(j), vo[j // 2][:, (j % 2) * E:(j % 2 + 1) * E], k["gate"][:, 0:1], tile(j),
                                                   ALU.mult, ALU.add).then_inc(x_done, 1)
            for step in steps:
                step(dve)

        @block.scalar
        def _(act):
            act.wait_ge(loaded, 7 * 16)
            for s in range(GROUPS):
                for c_ in range(KT):
                    act.wait_ge(turned, s * ST + ST)
                    nc.scalar.activation(xnT[:, c_, :], tp[c_][:], ACT.Copy).then_inc(xnT_done, 1)
                for n, (dst, bias) in enumerate(((qT, bq), (kT, bk))):
                    for f in range(KT):
                        act.wait_ge(qk_done, s * 4 + n * 2 + f + 1)
                        nc.scalar.activation(dst[:, f, :], qk[f][:], ACT.Identity, bias=bias[:, f:f + 1]).then_inc(qk_kept, 1)
                if s == 0:
                    for n in range(3):
                        tern.on_scalar(act, n)
                act.wait_ge(sub_done, s + 1)
                nc.scalar.activation(s_[:], s_[:], ACT.Exp).then_inc(exp_done, 1)
                act.wait_ge(pT_turned, s + 1)
                nc.scalar.activation(pT[:], tp[0][:].rearrange("p (n m) -> p n m", n=ST), ACT.Copy).then_inc(pT_kept, 1)

        @block.tensor
        def _(pe):
            pe.wait_ge(loaded, 7 * 16)
            for s in range(GROUPS):
                for j in range(ST):
                    pe.wait_ge(normed, s * ST + j + 1)
                    for c_ in range(KT):
                        last = nc.tensor.transpose(tp[c_][:, j * P:(j + 1) * P], xn[:, j, c_ * P:(c_ + 1) * P], k["ident"][:])
                    last.then_inc(turned, 1)
                pe.wait_ge(xnT_done, s * KT + KT)
                for n, w in enumerate((wq, wk)):
                    for f in range(KT):
                        if n == 1:
                            pe.wait_ge(qk_kept, s * 4 + f + 1)
                        for c_ in range(KT):
                            last = nc.tensor.matmul(qk[f][:], w[:, c_, f * P:(f + 1) * P], xnT[:, c_, :],
                                                    start=c_ == 0, stop=c_ == KT - 1)
                        last.then_inc(qk_done, 1)
                if s > 0:
                    pe.wait_ge(x_done, s * ST)
                for j in range(ST):
                    for c_ in range(KT):
                        last = nc.tensor.matmul(vo[j // 2][:, (j % 2) * E:(j % 2 + 1) * E], xnT[:, c_, j * P:(j + 1) * P],
                                                wv[:, c_, :], start=c_ == 0, stop=c_ == KT - 1)
                    if j % 2 == 1:
                        last.then_inc(v_done, 1)
                pe.wait_ge(qk_kept, s * 4 + 4)
                for j in range(ST):
                    for c_ in range(KT):
                        last = nc.tensor.matmul(sp_[:, j * P:(j + 1) * P], qT[:, c_, j * P:(j + 1) * P], kT[:, c_, j * P:(j + 1) * P],
                                                start=c_ == 0, stop=c_ == KT - 1)
                last.then_inc(sc_done, 1)
                if s == 0:
                    tern.on_tensor(pe, k)
                pe.wait_ge(probs_done, s * 2 + 2)
                for j in range(ST):
                    last = nc.tensor.transpose(tp[0][:, j * P:(j + 1) * P], probs[:, j, :], k["ident"][:])
                last.then_inc(pT_turned, 1)
                pe.wait_ge(pT_kept, s + 1)
                pe.wait_ge(v_kept, s * 2 + 2)
                for j in range(ST):
                    last = nc.tensor.matmul(vo[j // 2][:, (j % 2) * E:(j % 2 + 1) * E], pT[:, j, :], v[:, j, :],
                                            start=True, stop=True)
                    if j % 2 == 1:
                        last.then_inc(o_done, 1)


def bitnet(nc, t, k, tern, weights):
    with phase_semaphores(nc) as take, ExitStack() as c:
        def sb(name, shape, dt=F32):
            return c.enter_context(nc.sbuf_tensor("b_" + name, shape, dt))

        def ps(name, dt=F32):
            return c.enter_context(nc.psum_tensor("b_" + name, [P, 512 if dt == F32 else 1024], dt))

        def sem(name):
            return take("b_" + name)

        FC = INNER // P
        wg, wu = (w[:].rearrange("p (c f) -> p c f", c=KT) for w in tern.values[:2])
        wd = tern.values[2][:].rearrange("p (c f) -> p c f", c=FC)
        mean = tern.mean
        lnw = sb("lnw", [P, INNER])
        xn, rnd, xq = sb("xn", [P, ST, E]), sb("rnd", [P, ST, E]), sb("xq", [P, ST, E], BF16)
        am, inv, sx, dg, du = (sb(n, [P, ST]) for n in ("am", "inv", "sx", "dg", "du"))
        xqT = sb("xqT", [P, KT, ST * P], BF16)
        silu = sb("silu", [P, 2, 512])
        h = sb("h", [P, ST, INNER])
        junk = sb("junk", [P, INNER])
        ssq, ms, r, ah, hm, hinv, hs, od, one = (sb(n, [P, ST]) for n in ("ssq", "ms", "r", "ah", "hm", "hinv", "hs", "od", "rr"))
        hr = sb("hr", [P, 2, INNER])
        hq = sb("hq", [P, ST, INNER], BF16)
        hT = sb("hT", [P, 2, FC, P], BF16)
        ln = LayerNorm(nc, c, take, "b_ln", k)
        tpx = ps("tpx", BF16)
        gp = [ps("g0"), ps("g1")]
        up = [ps("u0"), ps("u1")]
        tph = ps("tph", BF16)
        yp = [ps("y0"), ps("y1")]
        names = ("loaded", "normed",
                 "am_done", "inv_done", "sx_done", "rnd_done", "xq_done", "turned", "xqT_done", "gu_done", "silu_done",
                 "h_done", "ssq_done", "ms_done", "r_done", "hw_done", "ah_done", "hm_done", "hinv_done", "hs_done",
                 "hr_done", "hq_done", "hturned", "hT_done", "y_done", "x_done", "d_done")
        q = {n: sem(n) for n in names}
        weights.begin(c, take)
        block = c.enter_context(nc.Block())

        @block.sync
        def _(sp):
            sp.dma_start(lnw[:], t["L0_lnw"].rearrange("(o n) -> o n", o=1).broadcast_to([P, INNER])).then_inc(q["loaded"], 16)
            weights.on_sync(sp, t)

        @block.gpsimd
        def _(pool):
            steps = weights.on_pool()
            for s in range(GROUPS):
                ln.on_pool(pool, s)
                take_steps(pool, steps, 4 if s == 0 else 1)
                pool.wait_ge(q["ms_done"], s + 1)
                nc.gpsimd.tensor_tensor(r[:], ms[:], k["half"][:, 0:ST], ALU.pow).then_inc(q["r_done"], 1)
                take_steps(pool, steps, 1 if s == 0 else 4)

        @block.vector
        def _(dve):
            V = nc.vector
            dve.wait_ge(q["loaded"], 16)
            steps = weights.on_vector()
            for s in range(GROUPS):
                def tile(j):
                    return k["x"][:].rearrange("p n e -> p (n e)")[:, bass.ds(s * (ST * E) + j * E, E)]

                ln.on_vector(dve, s, tile, lambda j: xn[:, j, :], q["normed"])
                dve.wait_ge(q["normed"], s * ST + ST)
                V.tensor_reduce(am[:], xn[:], AX.X, ALU.max, apply_absolute_value=True).then_inc(q["am_done"], 1)
                dve.wait_ge(q["am_done"], s + 1)
                V.tensor_scalar(am[:], am[:], QUANT_EPS, 1.0 / 127.0, ALU.max, ALU.mult).then_inc(q["inv_done"], 1)
                dve.wait_ge(q["inv_done"], s + 1)
                V.reciprocal(sx[:], am[:]).then_inc(q["sx_done"], 1)
                V.tensor_scalar(dg[:], am[:], mean[:, 0:1], None, ALU.mult).then_inc(q["d_done"], 1)
                V.tensor_scalar(du[:], am[:], mean[:, 1:2], None, ALU.mult).then_inc(q["d_done"], 1)
                dve.wait_ge(q["sx_done"], s + 1)
                for j in range(ST):
                    V.tensor_scalar(rnd[:, j, :], xn[:, j, :], sx[:, j:j + 1], MAGIC, ALU.mult, ALU.add).then_inc(q["rnd_done"], 1)
                dve.wait_ge(q["rnd_done"], s * ST + ST)
                V.tensor_scalar(xq[:], rnd[:], MAGIC, None, ALU.subtract).then_inc(q["xq_done"], 1)
                dve.wait_ge(q["d_done"], s * 2 + 2)
                take_steps(dve, steps, 3 if s == 0 else 2)
                for n in range(2 * ST):
                    j, f = n // 2, n % 2
                    dve.wait_ge(q["silu_done"], s * 2 * ST + n + 1)
                    V.scalar_tensor_tensor(h[:, j, f * 512:(f + 1) * 512], up[n % 2][:], du[:, j:j + 1], silu[:, n % 2, :],
                                           ALU.mult, ALU.mult).then_inc(q["h_done"], 1)
                    if f == 1:
                        take_steps(dve, steps, 1)
                for j in range(ST):
                    dve.wait_ge(q["ssq_done"], s * ST + j + 1)
                    V.tensor_tensor(h[:, j, :], h[:, j, :], lnw[:], ALU.mult).then_inc(q["hw_done"], 1)
                V.tensor_scalar(ms[:], ssq[:], 1.0 / INNER, RMS_EPS, ALU.mult, ALU.add).then_inc(q["ms_done"], 1)
                dve.wait_ge(q["hw_done"], s * ST + ST)
                V.tensor_reduce(ah[:], h[:], AX.X, ALU.max, apply_absolute_value=True).then_inc(q["ah_done"], 1)
                dve.wait_ge(q["ah_done"], s + 1)
                dve.wait_ge(q["r_done"], s + 1)
                V.tensor_tensor(hm[:], ah[:], r[:], ALU.mult).then_inc(q["hm_done"], 1)
                dve.wait_ge(q["hm_done"], s * 2 + 1)
                V.tensor_scalar(hm[:], hm[:], QUANT_EPS, 1.0 / 127.0, ALU.max, ALU.mult).then_inc(q["hm_done"], 1)
                dve.wait_ge(q["hm_done"], s * 2 + 2)
                V.reciprocal(hinv[:], hm[:]).then_inc(q["hinv_done"], 1)
                V.tensor_scalar(od[:], hm[:], mean[:, 2:3], k["gate"][:, 2:3], ALU.mult, ALU.mult).then_inc(q["hinv_done"], 1)
                dve.wait_ge(q["hinv_done"], s * 2 + 2)
                V.tensor_tensor(hs[:], hinv[:], r[:], ALU.mult).then_inc(q["hs_done"], 1)
                dve.wait_ge(q["hs_done"], s + 1)
                for j in range(ST):
                    V.tensor_scalar(hr[:, j % 2, :], h[:, j, :], hs[:, j:j + 1], MAGIC, ALU.mult, ALU.add).then_inc(q["hr_done"], 1)
                    dve.wait_ge(q["hr_done"], s * ST + j + 1)
                    V.tensor_scalar(hq[:, j, :], hr[:, j % 2, :], MAGIC, None, ALU.subtract).then_inc(q["hq_done"], 1)
                take_steps(dve, steps, 2 if s == 0 else 0)
                for j in range(ST):
                    dve.wait_ge(q["y_done"], s * ST + j + 1)
                    V.scalar_tensor_tensor(tile(j), yp[j % 2][:, 0:E], od[:, j:j + 1], tile(j),
                                           ALU.mult, ALU.add).then_inc(q["x_done"], 1)

        @block.scalar
        def _(act):
            steps = weights.on_scalar()
            for s in range(GROUPS):
                act.wait_ge(q["turned"], s + 1)
                nc.scalar.activation(xqT[:].rearrange("p c m -> p (c m)"), tpx[:], ACT.Copy).then_inc(q["xqT_done"], 1)
                act.wait_ge(q["d_done"], s * 2 + 2)
                take_steps(act, steps, 1 if s == 0 else 0)
                for n in range(2 * ST):
                    j, f = n // 2, n % 2
                    act.wait_ge(q["gu_done"], s * 2 * ST + n + 1)
                    if n >= 2:
                        act.wait_ge(q["h_done"], s * 2 * ST + n - 1)
                    nc.scalar.activation(silu[:, n % 2, :], gp[n % 2][:], ACT.Silu, scale=dg[:, j:j + 1]).then_inc(q["silu_done"], 1)
                    if n in ((0, 3, 6) if s == 0 else (0, 2, 4)):
                        take_steps(act, steps, 1)
                for j in range(ST):
                    act.wait_ge(q["h_done"], s * 2 * ST + 2 * j + 2)
                    if j > 0:
                        act.wait_ge(q["ssq_done"], s * ST + j)
                    nc.scalar.activation(junk[:], h[:, j, :], ACT.Square, accum_out=ssq[:, j:j + 1]).then_inc(q["ssq_done"], 1)
                take_steps(act, steps, 1 if s == 0 else 2)
                for j in range(ST):
                    act.wait_ge(q["hturned"], s * ST + j + 1)
                    if j >= 2:
                        act.wait_ge(q["y_done"], s * ST + j - 1)
                    nc.scalar.activation(hT[:, j % 2].rearrange("p c m -> p (c m)"), tph[:], ACT.Copy).then_inc(q["hT_done"], 1)
                take_steps(act, steps, 1 if s == 0 else 2)

        @block.tensor
        def _(pe):
            for s in range(GROUPS):
                pe.wait_ge(q["xq_done"], s + 1)
                for j in range(ST):
                    for c_ in range(KT):
                        last = nc.tensor.transpose(tpx[:, (c_ * ST + j) * P:(c_ * ST + j + 1) * P], xq[:, j, c_ * P:(c_ + 1) * P], k["identb"][:])
                last.then_inc(q["turned"], 1)
                pe.wait_ge(q["xqT_done"], s + 1)
                for n in range(2 * ST):
                    j, f = n // 2, n % 2
                    if n >= 2:
                        pe.wait_ge(q["h_done"], s * 2 * ST + n - 1)
                    for w, dst in ((wg, gp[n % 2]), (wu, up[n % 2])):
                        for c_ in range(KT):
                            last = nc.tensor.matmul(dst[:], xqT[:, c_, j * P:(j + 1) * P], w[:, c_, f * 512:(f + 1) * 512],
                                                    start=c_ == 0, stop=c_ == KT - 1)
                    last.then_inc(q["gu_done"], 1)

                def turn(j):
                    pe.wait_ge(q["hq_done"], s * ST + j + 1)
                    if j > 0:
                        pe.wait_ge(q["hT_done"], s * ST + j)
                    for c_ in range(FC):
                        last = nc.tensor.transpose(tph[:, c_ * P:(c_ + 1) * P], hq[:, j, c_ * P:(c_ + 1) * P], k["identb"][:])
                    last.then_inc(q["hturned"], 1)

                def down(j):
                    pe.wait_ge(q["hT_done"], s * ST + j + 1)
                    if j >= 2:
                        pe.wait_ge(q["x_done"], s * ST + j - 1)
                    for c_ in range(FC):
                        last = nc.tensor.matmul(yp[j % 2][:, 0:E], hT[:, j % 2, c_, :], wd[:, c_, :],
                                                start=c_ == 0, stop=c_ == FC - 1)
                    last.then_inc(q["y_done"], 1)

                turn(0)
                for j in range(1, ST):
                    turn(j)
                    down(j - 1)
                down(ST - 1)


def quantize_tokens(nc, t, k):
    with phase_semaphores(nc) as take, ExitStack() as c:
        def sb(name, shape, dt=F32):
            return c.enter_context(nc.sbuf_tensor("n_" + name, shape, dt))

        def sem(name):
            return take("n_" + name)

        N = ST * P
        lw, lb, ins, inv = sb("lw", [P, KT]), sb("lb", [P, KT]), sb("ins", [P, 4 * KT]), sb("inv", [P, 4 * KT])
        xn, xm, lnT = sb("xn", [P, ST, E]), sb("xm", [P, ST, E]), sb("lnT", [P, KT, N])
        yb, kb, big = sb("yb", [P, 2, N], BF16), sb("kb", [P, 2, N], BF16), sb("big", [P, 2, N])
        ln1, ln2 = LayerNorm(nc, c, take, "n_ln1", k), LayerNorm(nc, c, take, "n_ln2", k)
        tp = [c.enter_context(nc.psum_tensor(f"n_tp{i}", [P, N], F32)) for i in range(KT)]
        q = {n: sem(n) for n in ("loaded", "inv_done", "normed", "normed2", "turned", "lnT_done", "y_done", "clipped", "abs_done",
                                 "k_done", "big_done", "xq_done")}
        W = 4 * KT
        block = c.enter_context(nc.Block())

        @block.sync
        def _(sp):
            for dst, src in ((lw, "L1_ln_w"), (lb, "L1_ln_b")):
                sp.dma_start(dst[:], t[src]).then_inc(q["loaded"], 16)
            for n, src in enumerate(("L1_q_in_scale", "L1_k_in_scale", "L1_v_in_scale", "L1_qx_in_scale")):
                sp.dma_start(ins[:, n * KT:(n + 1) * KT], t[src]).then_inc(q["loaded"], 16)

        @block.gpsimd
        def _(pool):
            with pool.Fori(0, GROUPS) as s:
                ln1.on_pool(pool, s)
                ln2.on_pool(pool, s)
                for w in range(W):
                    pool.wait_ge(q["big_done"], s * W + w + 1)
                    out = k["xq"][:].rearrange("p v c n -> p (v c n)")[:, bass.ds(s * N + w * TOK, N)]
                    nc.gpsimd.tensor_tensor(out, big[:, w % 2, :], kb[:, w % 2, :], ALU.subtract).then_inc(q["xq_done"], 1)

        @block.vector
        def _(dve):
            V = nc.vector
            dve.wait_ge(q["loaded"], 96)
            V.reciprocal(inv[:], ins[:]).then_inc(q["inv_done"], 1)
            with dve.Fori(0, GROUPS) as s:
                def tile(j):
                    return k["x"][:].rearrange("p n e -> p (n e)")[:, bass.ds(s * (ST * E) + j * E, E)]

                ln1.on_vector(dve, s, tile, lambda j: xn[:, j, :], q["normed"])
                dve.wait_ge(q["normed"], s * ST + ST)
                ln2.on_vector(dve, s, lambda j: xn[:, j, :], lambda j: xm[:, j, :], q["normed2"])
                for w in range(W):
                    u = w % 2
                    dve.wait_ge(q["y_done"], s * W + w + 1)
                    V.tensor_scalar(yb[:, u, :], yb[:, u, :], FP8_MAX, -FP8_MAX, ALU.min, ALU.max).then_inc(q["clipped"], 1)
                    dve.wait_ge(q["clipped"], s * W + w + 1)
                    if w >= 2:
                        dve.wait_ge(q["xq_done"], s * W + w - 1)
                    V.tensor_scalar(kb[:, u, :].bitcast(U16), yb[:, u, :].bitcast(U16), 0x7FFF, None, ALU.bitwise_and).then_inc(q["abs_done"], 1)
                    dve.wait_ge(q["abs_done"], s * W + w + 1)
                    V.tensor_scalar(kb[:, u, :], kb[:, u, :], FP8_LEAST, FP8_SHIFT, ALU.max, ALU.mult).then_inc(q["k_done"], 1)
                    dve.wait_ge(q["k_done"], s * W + w + 1)
                    V.tensor_tensor(big[:, u, :], yb[:, u, :], kb[:, u, :], ALU.add).then_inc(q["big_done"], 1)
                dve.wait_ge(q["xq_done"], s * W + W)

        @block.scalar
        def _(act):
            act.wait_ge(q["loaded"], 96)
            act.wait_ge(q["inv_done"], 1)
            with act.Fori(0, GROUPS) as s:
                act.wait_ge(q["turned"], s + 1)
                for c_ in range(KT):
                    nc.scalar.activation(lnT[:, c_, :], tp[c_][:], ACT.Identity, bias=lb[:, c_:c_ + 1],
                                         scale=lw[:, c_:c_ + 1]).then_inc(q["lnT_done"], 1)
                act.wait_ge(q["lnT_done"], s * KT + KT)
                for w in range(W):
                    if w >= 2:
                        act.wait_ge(q["big_done"], s * W + w - 1)
                    nc.scalar.activation(yb[:, w % 2, :], lnT[:, w % KT, :], ACT.Copy, scale=inv[:, w:w + 1]).then_inc(q["y_done"], 1)

        @block.tensor
        def _(pe):
            with pe.Fori(0, GROUPS) as s:
                for j in range(ST):
                    pe.wait_ge(q["normed2"], s * ST + j + 1)
                    for c_ in range(KT):
                        last = nc.tensor.transpose(tp[c_][:, j * P:(j + 1) * P], xm[:, j, c_ * P:(c_ + 1) * P], k["ident"][:])
                last.then_inc(q["turned"], 1)


def gqa_pass(nc, t, k, weights):
    cross = weights.cross
    L = "x2" if cross else "c2"
    with phase_semaphores(nc) as take, ExitStack() as c:
        def sb(name, shape, dt=F32):
            return c.enter_context(nc.sbuf_tensor(f"{L}_{name}", shape, dt))

        def ps(name):
            return c.enter_context(nc.psum_tensor(f"{L}_{name}", [P, 512], F32))

        def sem(name):
            return take(f"{L}_{name}")

        CH = 512
        NQ, NK = HEADS * D // CH, KV * D // CH
        NN = NQ + NK
        NC = NN + NK
        NV = 1 if cross else 3
        GH = KV // 2
        w_hi, w_lo, w_ctx, p_hi, p_lo = weights.w_hi, weights.w_lo, weights.w_ctx, weights.p_hi, weights.p_lo
        ismooth, lnp, coef = weights.ismooth, weights.lnp, weights.coef
        qkT = sb("qkT", [P, 2, HEADS + KV, P])
        v = sb("v", [P, 2, KV * D])
        xqc = sb("xqc", [P, 2, NV * KT, P], F32R)
        ctxT = sb("ctxT", [P, KT, TOK]) if cross else None
        ctxc = sb("ctxc", [P, 2, KT, P]) if cross else None
        sq, ss = sb("sq", [P, 2, CH]), sb("ss", [P, 2, 4])
        ve, rs, qn = sb("ve", [P, 2, 4]), sb("rs", [P, 2, 4]), sb("qn", [P, 2, CH])
        ex = sb("ex", [P, 2, CH])
        mx, sm, rc = sb("mx", [P, 2, 8]), sb("sm", [P, 2, 8]), sb("rc", [P, 2, 8])
        pT = sb("pT", [P, 2, GH, P])
        yb, kb, big = sb("yb", [P, 2, 2 * CH], BF16), sb("kb", [P, 2, 2 * CH], BF16), sb("big", [P, 2, 2 * CH])
        cat = sb("cat", [P, 2, 2 * GH, P], F32R)
        proj = [ps("proj0"), ps("proj1"), ps("proj2")]
        turns = [ps("turn0"), ps("turn1")]
        sp_ = ps("scores")
        op = c.enter_context(nc.psum_tensor(f"{L}_op", [P, 2, CH], F32))
        CHUNKS = (("k", 0), ("q", 0), ("q", 1), ("k", 1), ("q", 2), ("q", 3), ("v", 0), ("v", 1))
        PROJ_BANK = (0, 1, 0, 1, 2, 0, 1, 2)
        OUT_BANK = 2
        TURN_BANK, PROBS_BANK = (0, 0, 1, 1, 0, 1), (1, 0)

        names = ("ctx_loaded", "xqc_done", "qkv_done", "turned", "sc_done", "pt_done", "pv_done", "y_done", "sq_done", "tev_done",
                 "vev_done", "exp_done", "ptev_done", "ss_done", "qn_done", "max_done", "sub_done", "sum_done", "rec_done",
                 "pn_done", "q1_done", "clipped", "abs_done", "k_done", "big_done", "cat_done", "x_done", "ve_done", "rs_done")
        q = {n: sem(n) for n in names}


        def run(eng, ahead, both, alone, last):
            ahead(0, 0, True)
            both(0, 0, True)
            both(1, 1, False)
            with eng.Fori(1, TILES // 2 - 1) as i:
                both(i * 2, 0, False)
                both(i * 2 + 1, 1, False)
            both(TILES - 2, 0, False)
            alone(TILES - 1, 1)
            last(TILES - 1)

        with nc.Block() as block:
            if cross:
                @block.sync
                def _(sp):
                    sp.dma_start(ctxT[:], t["ctxT"].rearrange("(c p) n -> p c n", p=P)).then_inc(q["ctx_loaded"], 16)

            @block.gpsimd
            def _(pool):
                G = nc.gpsimd

                def copy_tile(n, par, wait):
                    if wait:
                        pool.wait_ge(q["qkv_done"], n * NC - NC)
                    src = k["xq"][:, 3:4] if cross else k["xq"][:, 0:3]
                    last = G.tensor_copy(xqc[:, par], src.rearrange("p v c n -> p (v c) n")[:, :, bass.ds(n * P, P)])
                    if cross:
                        last = G.tensor_copy(ctxc[:, par], ctxT[:, :, bass.ds(n * P, P)])
                    last.then_inc(q["xqc_done"], 1)

                def rstd(n, i, first):
                    u = i % 2
                    if not (first and i < 2):
                        pool.wait_ge(q["qn_done"], n * NN + i - 1)
                    pool.wait_ge(q["ve_done"], n * NN + i + 1)
                    G.tensor_tensor(rs[:, u, :], ve[:, u, :], k["half"][:, 0:4], ALU.pow).then_inc(q["rs_done"], 1)

                def normalise(n, h):
                    e3 = ex[:, h, :].rearrange("p (g s) -> p g s", s=SEQ)
                    pool.wait_ge(q["rec_done"], n * 2 + h + 1)
                    G.tensor_tensor(e3, e3, bcast(rc[:, h, :], 2, SEQ), ALU.mult).then_inc(q["pn_done"], 1)

                def fp8(n, h):
                    pool.wait_ge(q["big_done"], n * 2 + h + 1)
                    if not (isinstance(n, int) and n == 0):
                        pool.wait_ge(q["y_done"], n)
                    G.tensor_tensor(cat[:, h].rearrange("p h (b s) -> p b h s", b=2), big[:, h, :].rearrange("p (b h s) -> p b h s", b=2, s=SEQ),
                                    kb[:, h, :].rearrange("p (b h s) -> p b h s", b=2, s=SEQ), ALU.subtract).then_inc(q["cat_done"], 1)

                def ahead(n, par, first):
                    if cross:
                        pool.wait_ge(q["ctx_loaded"], 16)
                    copy_tile(0, 0, False)
                    copy_tile(1, 1, False)
                    for i in range(NN):
                        rstd(n, i, first)

                def both(n, par, first):
                    rstd(n + 1, 0, False)
                    rstd(n + 1, 1, False)
                    if not (isinstance(n, int) and n == TILES - 2):
                        copy_tile(n + 2, par, True)
                    normalise(n, 0)
                    rstd(n + 1, 2, False)
                    rstd(n + 1, 3, False)
                    normalise(n, 1)
                    rstd(n + 1, 4, False)
                    rstd(n + 1, 5, False)
                    fp8(n, 0)
                    fp8(n, 1)

                def alone(n, par):
                    normalise(n, 0)
                    normalise(n, 1)
                    fp8(n, 0)
                    fp8(n, 1)

                run(pool, ahead, both, alone, lambda n: None)

            @block.vector
            def _(dve):
                V = nc.vector

                def sums(n, i):
                    dve.wait_ge(q["sq_done"], n * NN + i + 1)
                    V.tensor_reduce(ss[:, i % 2, :], sq[:, i % 2, :].rearrange("p (h d) -> p h d", d=D), AX.X, ALU.add).then_inc(q["ss_done"], 1)
                    dve.wait_ge(q["ss_done"], n * NN + i + 1)
                    V.tensor_scalar(ve[:, i % 2, :], ss[:, i % 2, :], 1.0 / D, LN_EPS, ALU.mult, ALU.add).then_inc(q["ve_done"], 1)

                def scale(n, i, first):
                    dve.wait_ge(q["rs_done"], n * NN + i + 1)
                    if not (first and i < 2):
                        dve.wait_ge(q["turned"], n * NN + i - 1)
                    V.tensor_tensor(qn[:, i % 2, :].rearrange("p (h d) -> p h d", d=D), proj[PROJ_BANK[i]][:].rearrange("p (h d) -> p h d", d=D),
                                    bcast(rs[:, i % 2, :], 2, D), ALU.mult).then_inc(q["qn_done"], 1)

                def less_max(n, h, first):
                    dve.wait_ge(q["sc_done"], n * 2 + h + 1)
                    s3 = sp_[:].rearrange("p (g s) -> p g s", s=SEQ)
                    V.tensor_reduce(mx[:, h, :], s3, AX.X, ALU.max).then_inc(q["max_done"], 1)
                    dve.wait_ge(q["max_done"], n * 2 + h + 1)
                    if not first:
                        dve.wait_ge(q["pt_done"], n * 2 + h - 1)
                    V.tensor_tensor(ex[:, h, :].rearrange("p (g s) -> p g s", s=SEQ), s3, bcast(mx[:, h, :], 2, SEQ),
                                    ALU.subtract).then_inc(q["sub_done"], 1)

                def total(n, h, first):
                    e3 = ex[:, h, :].rearrange("p (g s) -> p g s", s=SEQ)
                    dve.wait_ge(q["exp_done"], n * 2 + h + 1)
                    V.tensor_reduce(sm[:, h, :], e3, AX.X, ALU.add).then_inc(q["sum_done"], 1)
                    dve.wait_ge(q["sum_done"], n * 2 + h + 1)
                    if not first:
                        dve.wait_ge(q["pn_done"], n * 2 + h - 1)
                    V.reciprocal(rc[:, h, :], sm[:, h, :]).then_inc(q["rec_done"], 1)

                def unload(n, h, first):
                    dve.wait_ge(q["pv_done"], n * 2 + h + 1)
                    if not first:
                        dve.wait_ge(q["big_done"], n * 2 + h - 1)
                    V.tensor_tensor(yb[:, h, :].rearrange("p (b h s) -> p b h s", b=2, s=SEQ),
                                    op[:].rearrange("p b (h s) -> p b h s", s=SEQ),
                                    bcast(bcast(ismooth[:, 2 * GH * h:2 * GH * (h + 1)], 1, 2), 3, SEQ), ALU.mult).then_inc(q["q1_done"], 1)

                def rounding(n, h, first):
                    dve.wait_ge(q["q1_done"], n * 2 + h + 1)
                    V.tensor_scalar(yb[:, h, :], yb[:, h, :], FP8_MAX, -FP8_MAX, ALU.min, ALU.max).then_inc(q["clipped"], 1)
                    if not first:
                        dve.wait_ge(q["cat_done"], n * 2 + h - 1)
                    dve.wait_ge(q["clipped"], n * 2 + h + 1)
                    V.tensor_scalar(kb[:, h, :].bitcast(U16), yb[:, h, :].bitcast(U16), 0x7FFF, None, ALU.bitwise_and).then_inc(q["abs_done"], 1)
                    dve.wait_ge(q["abs_done"], n * 2 + h + 1)
                    V.tensor_scalar(kb[:, h, :], kb[:, h, :], FP8_LEAST, FP8_SHIFT, ALU.max, ALU.mult).then_inc(q["k_done"], 1)
                    dve.wait_ge(q["k_done"], n * 2 + h + 1)
                    V.tensor_tensor(big[:, h, :], yb[:, h, :], kb[:, h, :], ALU.add).then_inc(q["big_done"], 1)

                def add_x(n):
                    tile = k["x"][:].rearrange("p n e -> p (n e)")[:, bass.ds(n * E, E)]
                    dve.wait_ge(q["y_done"], n + 1)
                    V.scalar_tensor_tensor(tile, proj[OUT_BANK][:, 0:E], coef[:, 1:2], tile, ALU.mult, ALU.add).then_inc(q["x_done"], 1)

                def ahead(n, par, first):
                    sums(n, 0)
                    for i in range(1, NN):
                        sums(n, i)
                        scale(n, i - 1, first)
                    scale(n, NN - 1, first)

                def both(n, par, first):
                    m = n + 1
                    less_max(n, 0, first)
                    sums(m, 0)
                    sums(m, 1)
                    less_max(n, 1, first)
                    scale(m, 0, False)
                    total(n, 0, first)
                    scale(m, 1, False)
                    total(n, 1, first)
                    if not first:
                        add_x(n - 1)
                    sums(m, 2)
                    sums(m, 3)
                    scale(m, 2, False)
                    sums(m, 4)
                    scale(m, 3, False)
                    unload(n, 0, first)
                    sums(m, 5)
                    scale(m, 4, False)
                    rounding(n, 0, first)
                    scale(m, 5, False)
                    unload(n, 1, first)
                    rounding(n, 1, first)

                def alone(n, par):
                    less_max(n, 0, False)
                    total(n, 0, False)
                    less_max(n, 1, False)
                    total(n, 1, False)
                    add_x(n - 1)
                    for h in range(2):
                        unload(n, h, False)
                        rounding(n, h, False)

                run(dve, ahead, both, alone, add_x)

            @block.scalar
            def _(act):
                A = nc.scalar

                def square(n, i, first):
                    act.wait_ge(q["qkv_done"], n * NC + i + 1)
                    if not (first and i < 2):
                        act.wait_ge(q["ss_done"], n * NN + i - 1)
                    A.activation(sq[:, i % 2, :], proj[PROJ_BANK[i]][:], ACT.Square).then_inc(q["sq_done"], 1)

                def keep_qk(n, i, par):
                    act.wait_ge(q["turned"], n * NN + i + 1)
                    kind, at = CHUNKS[i]
                    w, at = (0, 4 * at) if kind == "q" else (2, HEADS + 4 * at)
                    A.activation(qkT[:, par, at:at + 4, :], turns[TURN_BANK[i]][:].rearrange("p (h m) -> p h m", h=4), ACT.Identity,
                                 bias=lnp[:, w + 1:w + 2], scale=lnp[:, w:w + 1]).then_inc(q["tev_done"], 1)

                def keep_v(n, i, par):
                    act.wait_ge(q["qkv_done"], n * NC + NN + i + 1)
                    A.activation(v[:, par, i * CH:(i + 1) * CH], proj[PROJ_BANK[NN + i]][:], ACT.Copy).then_inc(q["vev_done"], 1)

                def exponent(n, h):
                    act.wait_ge(q["sub_done"], n * 2 + h + 1)
                    A.activation(ex[:, h, :], ex[:, h, :], ACT.Exp, scale=D ** -0.5).then_inc(q["exp_done"], 1)

                def keep_pT(n, h):
                    act.wait_ge(q["pt_done"], n * 2 + h + 1)
                    A.activation(pT[:, h], turns[PROBS_BANK[h]][:].rearrange("p (g m) -> p g m", g=GH), ACT.Copy).then_inc(q["ptev_done"], 1)

                def ahead(n, par, first):
                    square(n, 0, first)
                    square(n, 1, first)
                    for i in range(2, NN):
                        keep_qk(n, i - 2, par)
                        square(n, i, first)
                    keep_v(n, 0, par)
                    keep_qk(n, NN - 2, par)
                    keep_v(n, 1, par)
                    keep_qk(n, NN - 1, par)

                def both(n, par, first):
                    m, mp = n + 1, 1 - par
                    square(m, 0, False)
                    exponent(n, 0)
                    square(m, 1, False)
                    exponent(n, 1)
                    square(m, 2, False)
                    keep_qk(m, 0, mp)
                    square(m, 3, False)
                    keep_pT(n, 0)
                    square(m, 4, False)
                    keep_qk(m, 1, mp)
                    square(m, 5, False)
                    keep_pT(n, 1)
                    keep_v(m, 0, mp)
                    keep_qk(m, 2, mp)
                    keep_qk(m, 3, mp)
                    keep_v(m, 1, mp)
                    keep_qk(m, 4, mp)
                    keep_qk(m, 5, mp)

                def alone(n, par):
                    exponent(n, 0)
                    exponent(n, 1)
                    keep_pT(n, 0)
                    keep_pT(n, 1)

                run(act, ahead, both, alone, lambda n: None)

            @block.tensor
            def _(pe):
                T = nc.tensor

                def project(n, i, par, first):
                    if i == 0:
                        pe.wait_ge(q["xqc_done"], n + 1)
                    if i == 0 and not first:
                        pe.wait_ge(q["qn_done"], n * NN)
                    if i == 1 and not first:
                        pe.wait_ge(q["vev_done"], n * NK - 1)
                    if i in (2, 3):
                        pe.wait_ge(q["qn_done"], n * NN + i - 1)
                    if i == 4 and not first and not (isinstance(n, int) and n == 1):
                        pe.wait_ge(q["x_done"], n - 1)
                    if i > 4:
                        pe.wait_ge(q["qn_done"], n * NN + i - 2)
                    bank = proj[PROJ_BANK[i]][:]
                    kind, at = CHUNKS[i]
                    if kind == "q" or not cross:
                        v_, at = {"q": (0, at), "k": (1, NQ + at), "v": (2, NN + at)}[kind]
                        for c_ in range(KT):
                            for part in range(2):
                                last = T.matmul(bank, xqc[:, par, v_ * KT + c_, :], (w_hi, w_lo)[part][:, at, c_, :],
                                                start=c_ == 0 and part == 0, stop=c_ == KT - 1 and part == 1)
                    else:
                        at += 0 if kind == "k" else NK
                        for c_ in range(KT):
                            last = T.matmul(bank, ctxc[:, par, c_, :], w_ctx[:, at, c_, :], start=c_ == 0, stop=c_ == KT - 1)
                    last.then_inc(q["qkv_done"], 1)

                def turn(n, i, first):
                    pe.wait_ge(q["qn_done"], n * NN + i + 1)
                    if i == 0 and not first:
                        pe.wait_ge(q["tev_done"], n * NN - 1)
                    if i in (1, 3):
                        pe.wait_ge(q["tev_done"], n * NN + i)
                    if i == 2 and not first:
                        pe.wait_ge(q["ptev_done"], n * 2 - 1)
                    if i == 4:
                        pe.wait_ge(q["tev_done"], n * NN + 2)
                        if not first:
                            pe.wait_ge(q["ptev_done"], n * 2)
                    if i == 5:
                        pe.wait_ge(q["tev_done"], n * NN + 4)
                    bank = turns[TURN_BANK[i]]
                    for h in range(4):
                        out = bank[:, h * P:(h + 1) * P]
                        if CHUNKS[i][0] == "q":
                            out = bank[:].rearrange("p (g b h s) -> p g h b s", g=2, b=2, h=2)[:, h // 2, h % 2]
                        last = T.transpose(out, qn[:, i % 2, h * D:(h + 1) * D], k["ident"][:])
                    last.then_inc(q["turned"], 1)

                def scores(n, h, par, first):
                    pe.wait_ge(q["tev_done"], n * NN + (h + 1) * NN // 2)
                    if not (first and h == 0):
                        pe.wait_ge(q["sub_done"], n * 2 + h)
                    for g in range(GH):
                        kv = h * GH + g
                        for b in range(2):
                            rows = slice(b * SEQ, (b + 1) * SEQ)
                            last = T.matmul(sp_[:, (g * 2 + b) * SEQ:(g * 2 + b + 1) * SEQ], qkT[:, par, 2 * kv + b, :],
                                            qkT[:, par, HEADS + kv, rows], start=True, stop=True)
                    last.then_inc(q["sc_done"], 1)

                def turn_p(n, h, alone):
                    pe.wait_ge(q["pn_done"], n * 2 + h + 1)
                    if h == 0 or alone:
                        pe.wait_ge(q["tev_done"], n * NN + NN)
                    else:
                        pe.wait_ge(q["tev_done"], n * NN + NN + 2)
                    for g in range(GH):
                        last = T.transpose(turns[PROBS_BANK[h]][:, g * P:(g + 1) * P], ex[:, h, g * P:(g + 1) * P], k["ident"][:])
                    last.then_inc(q["pt_done"], 1)

                def attend(n, h, par, first):
                    pe.wait_ge(q["ptev_done"], n * 2 + h + 1)
                    pe.wait_ge(q["vev_done"], n * NK + NK)
                    if not (first and h == 0):
                        pe.wait_ge(q["q1_done"], n * 2 + h)
                    for g in range(GH):
                        kv = h * GH + g
                        for b in range(2):
                            rows = slice(b * SEQ, (b + 1) * SEQ)
                            last = T.matmul(op[:, b, g * P:(g + 1) * P], v[rows, par, kv * D:(kv + 1) * D], pT[rows, h, g, :],
                                            start=True, stop=True)
                    last.then_inc(q["pv_done"], 1)

                def output(n):
                    pe.wait_ge(q["cat_done"], n * 2 + 2)
                    pe.wait_ge(q["vev_done"], n * NK + 2 * NK if not (isinstance(n, int) and n == TILES - 1) else TILES * NK)
                    for hd in range(HEADS):
                        for part in range(2):
                            last = T.matmul(proj[OUT_BANK][:, 0:E], cat[:, hd // (2 * GH), hd % (2 * GH), :], (p_hi, p_lo)[part][:, hd, :],
                                            start=hd == 0 and part == 0, stop=hd == HEADS - 1 and part == 1)
                    last.then_inc(q["y_done"], 1)

                def ahead(n, par, first):
                    project(n, 0, par, first)
                    project(n, 1, par, first)
                    for i in range(2, NC):
                        turn(n, i - 2, first)
                        project(n, i, par, first)

                def both(n, par, first):
                    m, mp = n + 1, 1 - par
                    scores(n, 0, par, first)
                    project(m, 0, mp, False)
                    project(m, 1, mp, False)
                    scores(n, 1, par, first)
                    if not first:
                        output(n - 1)
                    project(m, 2, mp, False)
                    turn(m, 0, False)
                    project(m, 3, mp, False)
                    turn_p(n, 0, False)
                    project(m, 4, mp, False)
                    turn(m, 1, False)
                    attend(n, 0, par, first)
                    project(m, 5, mp, False)
                    turn(m, 2, False)
                    turn_p(n, 1, False)
                    project(m, 6, mp, False)
                    attend(n, 1, par, first)
                    turn(m, 3, False)
                    project(m, 7, mp, False)
                    turn(m, 4, False)
                    turn(m, 5, False)

                def alone(n, par):
                    scores(n, 0, par, False)
                    output(n - 1)
                    scores(n, 1, par, False)
                    turn_p(n, 0, True)
                    attend(n, 0, par, False)
                    turn_p(n, 1, True)
                    attend(n, 1, par, False)

                run(pe, ahead, both, alone, output)


def moe(nc, t, k):
    with phase_semaphores(nc) as take, ExitStack() as c:
        def sb(name, shape, dt=F32):
            return c.enter_context(nc.sbuf_tensor("m_" + name, shape, dt))

        def ps(name):
            return c.enter_context(nc.psum_tensor("m_" + name, [P, 512], F32))

        def sem(name):
            return take("m_" + name)

        N, NE, X = ST * P, EXPERTS + 1, EXPERTS
        w1, wg, w2 = sb("w1", [P, 2, KT, E]), sb("wg", [P, 2, KT, E]), sb("w2", [P, 2, KT, E])
        gw, gb, eb = sb("gw", [P, KT, X]), sb("gb", [P, X]), sb("eb", [P, X])
        earlier = sb("earlier", [P, X, X])
        xn, xnT = sb("xn", [P, ST, E]), sb("xnT", [P, KT, TOK])
        lg, pr, bp = sb("lg", [P, ST, X]), sb("pr", [P, ST, X]), sb("bp", [P, ST, X])
        mx, sm = sb("mx", [P, ST]), sb("sm", [P, ST])
        gt, eq = sb("gt", [P, ST, X * X]), sb("eq", [P, ST, X * X])
        rank = sb("rank", [P, ST, X])
        we = sb("we", [P, GROUPS * ST, NE])
        silu, h = sb("silu", [P, 2, N]), sb("h", [P, 2, KT, N])
        ln = LayerNorm(nc, c, take, "m_ln", k)
        ap_, gp = [ps("a0"), ps("a1")], [ps("g0"), ps("g1")]
        yp = [ps("y0"), ps("y1")]
        tp = ap_
        lp = gp[0]
        names = ("loaded", "w_loaded0", "w_loaded1", "normed", "turned", "xnT_done", "lg_done", "lb_done", "mx_done", "sub_done",
                 "exp_done", "sm_done", "rec_done", "pr_done", "bp_done", "gt_done", "eq_done", "eqm_done", "sum_done", "rank_done",
                 "sel_done", "ws_done", "wr_done", "wg_done", "we_done", "ag_done", "silu_done", "h_done", "y_done", "x_done", "ones_done",
                 "earlier_done")
        q = {n: sem(n) for n in names}
        w_loaded = [q["w_loaded0"], q["w_loaded1"]]
        UNITS = NE * GROUPS

        with nc.Block() as block:
            @block.sync
            def _(sp):
                sp.dma_start(gw[:], t["L1_gate_w"].rearrange("(c p) x -> p c x", p=P)).then_inc(q["loaded"], 16)
                for dst, src in ((gb, "L1_gate_b"), (eb, "L1_biases")):
                    sp.dma_start(dst[:], t[src].rearrange("(o n) -> o n", o=1).broadcast_to([P, X])).then_inc(q["loaded"], 16)

            @block.gpsimd
            def _(pool):
                nc.gpsimd.memset(earlier[:], 1.0).then_inc(q["ones_done"], 1)
                pool.wait_ge(q["ones_done"], 1)
                nc.gpsimd.affine_select(out=earlier[:], in_=earlier[:], compare_op=ALU.is_gt, fill=0.0, base=0,
                                        pattern=[[1, X], [-1, X]], channel_multiplier=0).then_inc(q["earlier_done"], 1)
                with pool.Fori(0, GROUPS) as s:
                    ln.on_pool(pool, s)

            @block.vector
            def _(dve):
                V = nc.vector
                dve.wait_ge(q["loaded"], 48)
                dve.wait_ge(q["earlier_done"], 1)
                with dve.Fori(0, GROUPS) as s:
                    def tile(j):
                        return k["x"][:].rearrange("p n e -> p (n e)")[:, bass.ds(s * (ST * E) + j * E, E)]

                    ln.on_vector(dve, s, tile, lambda j: xn[:, j, :], q["normed"])
                    dve.wait_ge(q["lg_done"], s + 1)
                    V.tensor_tensor(lg[:], lp[:, 0:ST * X].rearrange("p (j x) -> p j x", x=X), bcast(gb[:], 1, ST), ALU.add).then_inc(q["lb_done"], 1)
                    dve.wait_ge(q["lb_done"], s + 1)
                    V.tensor_reduce(mx[:], lg[:], AX.X, ALU.max).then_inc(q["mx_done"], 1)
                    dve.wait_ge(q["mx_done"], s + 1)
                    V.tensor_tensor(lg[:], lg[:], bcast(mx[:], 2, X), ALU.subtract).then_inc(q["sub_done"], 1)
                    dve.wait_ge(q["exp_done"], s + 1)
                    V.tensor_reduce(sm[:], lg[:], AX.X, ALU.add).then_inc(q["sm_done"], 1)
                    dve.wait_ge(q["sm_done"], s + 1)
                    V.reciprocal(sm[:], sm[:]).then_inc(q["rec_done"], 1)
                    dve.wait_ge(q["rec_done"], s + 1)
                    V.tensor_tensor(pr[:], lg[:], bcast(sm[:], 2, X), ALU.mult).then_inc(q["pr_done"], 1)
                    dve.wait_ge(q["pr_done"], s + 1)
                    V.tensor_tensor(bp[:], pr[:], bcast(eb[:], 1, ST), ALU.add).then_inc(q["bp_done"], 1)
                    dve.wait_ge(q["bp_done"], s + 1)
                    for j in range(ST):
                        other, own = bcast(bp[:, j, :], 1, X), bcast(bp[:, j, :], 2, X)
                        V.tensor_tensor(gt[:, j, :].rearrange("p (e o) -> p e o", o=X), other, own, ALU.is_gt).then_inc(q["gt_done"], 1)
                        V.tensor_tensor(eq[:, j, :].rearrange("p (e o) -> p e o", o=X), other, own, ALU.is_equal).then_inc(q["eq_done"], 1)
                    dve.wait_ge(q["eq_done"], s * ST + ST)
                    V.tensor_tensor(eq[:], eq[:], bcast(earlier[:].rearrange("p e o -> p (e o)"), 1, ST), ALU.mult).then_inc(q["eqm_done"], 1)
                    dve.wait_ge(q["eqm_done"], s + 1)
                    dve.wait_ge(q["gt_done"], s * ST + ST)
                    V.tensor_tensor(gt[:], gt[:], eq[:], ALU.add).then_inc(q["sum_done"], 1)
                    dve.wait_ge(q["sum_done"], s + 1)
                    V.tensor_reduce(rank[:].rearrange("p j x -> p (j x)"), gt[:].rearrange("p j (e o) -> p (j e) o", o=X), AX.X, ALU.add).then_inc(q["rank_done"], 1)
                    dve.wait_ge(q["rank_done"], s + 1)
                    V.scalar_tensor_tensor(rank[:], rank[:], TOP_K - 0.5, pr[:], ALU.is_lt, ALU.mult).then_inc(q["sel_done"], 1)
                    dve.wait_ge(q["sel_done"], s + 1)
                    V.tensor_reduce(sm[:], rank[:], AX.X, ALU.add).then_inc(q["ws_done"], 1)
                    dve.wait_ge(q["ws_done"], s + 1)
                    V.reciprocal(sm[:], sm[:]).then_inc(q["wr_done"], 1)
                    dve.wait_ge(q["wr_done"], s + 1)
                    V.tensor_scalar(sm[:], sm[:], k["gate"][:, 3:4], None, ALU.mult).then_inc(q["wg_done"], 1)
                    dve.wait_ge(q["wg_done"], s + 1)
                    table = we[:].rearrange("p n x -> p (n x)")[:, bass.ds(s * (ST * NE), ST * NE)].rearrange("p (n x) -> p n x", x=NE)
                    V.tensor_tensor(table[:, :, 1:NE], rank[:], bcast(sm[:], 2, X), ALU.mult).then_inc(q["we_done"], 1)
                V.tensor_scalar(we[:, :, 0], k["ones"][:, 0:GROUPS * ST], k["gate"][:, 3:4], None, ALU.mult)

            @block.scalar
            def _(act):
                with act.Fori(0, GROUPS) as s:
                    act.wait_ge(q["turned"], s + 1)
                    for c_ in range(KT):
                        nc.scalar.activation(xnT[:].rearrange("p c n -> p (c n)")[:, bass.ds(s * N + c_ * TOK, N)], tp[c_][:],
                                             ACT.Copy).then_inc(q["xnT_done"], 1)
                    act.wait_ge(q["sub_done"], s + 1)
                    nc.scalar.activation(lg[:], lg[:], ACT.Exp).then_inc(q["exp_done"], 1)

            @block.tensor
            def _(pe):
                for s in range(GROUPS):
                    if s > 0:
                        pe.wait_ge(q["xnT_done"], s * KT)
                    for j in range(ST):
                        pe.wait_ge(q["normed"], s * ST + j + 1)
                        for c_ in range(KT):
                            last = nc.tensor.transpose(tp[c_][:, j * P:(j + 1) * P], xn[:, j, c_ * P:(c_ + 1) * P], k["ident"][:])
                    last.then_inc(q["turned"], 1)
                    pe.wait_ge(q["xnT_done"], (s + 1) * KT)
                    if s > 0:
                        pe.wait_ge(q["lb_done"], s)
                    for j in range(ST):
                        for c_ in range(KT):
                            at = s * N + j * P
                            last = nc.tensor.matmul(lp[:, j * X:(j + 1) * X], xnT[:, c_, at:at + P], gw[:, c_, :],
                                                    start=c_ == 0, stop=c_ == KT - 1)
                    last.then_inc(q["lg_done"], 1)

        def run(eng, first_product, second_product):
            first_product(0, 0, True)
            for n in range(1, 4):
                first_product(n, n, True)
                second_product(n - 1, n - 1, True)
            with eng.Fori(1, UNITS // 4) as i:
                for u in range(4):
                    first_product(i * 4 + u, u, False)
                    second_product(i * 4 + (u - 1), (u - 1) % 4, u == 0 and None)
            second_product(UNITS - 1, 3, False)

        with nc.Block() as block:
            @block.sync
            def _(sp):
                def load(e, par):
                    for w, src in ((w1, "L1_W1"), (wg, "L1_Wg"), (w2, "L1_W2")):
                        flat = t[src].rearrange("x k f -> (x k) f")[bass.ds(e * E, E), :]
                        sp.dma_start(w[:, par], flat.rearrange("(c p) f -> p c f", p=P)).then_inc(w_loaded[par], 16)

                load(0, 0)
                load(1, 1)
                with sp.Fori(1, NE // 2) as i:
                    sp.wait_ge(q["y_done"], i * 4 - 2)
                    load(i * 2, 0)
                    sp.wait_ge(q["y_done"], i * 4)
                    load(i * 2 + 1, 1)

            @block.scalar
            def _(act):
                def silus(n, u, first):
                    for f in range(KT):
                        act.wait_ge(q["ag_done"], n * KT + f + 1)
                        if not (first and u == 0):
                            act.wait_ge(q["h_done"], n * KT + f - 1)
                        nc.scalar.activation(silu[:, f, :], ap_[f][:], ACT.Silu).then_inc(q["silu_done"], 1)

                run(act, silus, lambda n, u, first: None)

            @block.vector
            def _(dve):
                def product(n, u, first):
                    for f in range(KT):
                        dve.wait_ge(q["silu_done"], n * KT + f + 1)
                        nc.vector.tensor_tensor(h[:, u % 2, f, :], silu[:, f, :], gp[f][:], ALU.mult).then_inc(q["h_done"], 1)

                def add_x(n, u, first):
                    e_off = n // 2 if isinstance(n, int) else None
                    for j in range(ST):
                        dve.wait_ge(q["y_done"], n + 1) if j == 0 else None
                        row = (u % 2) * ST + j
                        tile = k["x"][:, row, :]
                        if e_off is None:
                            at = we[:].rearrange("p n x -> p (n x)")[:, bass.ds((n - u % 2) // 2 + row * NE, 1)]
                        else:
                            at = we[:, row, e_off:e_off + 1]
                        nc.vector.scalar_tensor_tensor(tile, yp[j // 2][:, (j % 2) * E:(j % 2 + 1) * E], at, tile,
                                                       ALU.mult, ALU.add).then_inc(q["x_done"], 1)

                run(dve, product, add_x)

            @block.tensor
            def _(pe):
                def first_products(n, u, first):
                    s, par = u % 2, u // 2
                    if s == 0:
                        e3 = (n // 4 + 1) if isinstance(n, int) else (n - u) // 4 + 1
                        pe.wait_ge(w_loaded[par], e3 * 48)
                    for f in range(KT):
                        if not (first and u == 0):
                            pe.wait_ge(q["h_done"], n * KT + f - 1)
                        for w, dst in ((w1, ap_[f]), (wg, gp[f])):
                            for c_ in range(KT):
                                last = nc.tensor.matmul(dst[:], w[:, par, c_, f * P:(f + 1) * P], xnT[:, c_, s * N:(s + 1) * N],
                                                        start=c_ == 0, stop=c_ == KT - 1)
                        last.then_inc(q["ag_done"], 1)

                def second_product(n, u, first):
                    par = u // 2
                    pe.wait_ge(q["h_done"], n * KT + KT)
                    if not (isinstance(n, int) and n == 0):
                        pe.wait_ge(q["x_done"], n * ST)
                    for j in range(ST):
                        for f in range(KT):
                            last = nc.tensor.matmul(yp[j // 2][:, (j % 2) * E:(j % 2 + 1) * E], h[:, u % 2, f, j * P:(j + 1) * P],
                                                    w2[:, par, f, :], start=f == 0, stop=f == KT - 1)
                    last.then_inc(q["y_done"], 1)

                run(pe, first_products, second_product)


def kernel(**a):
    import numpy as np
    import concourse.bacc as bacc
    from concourse.bass_utils import run_bass_kernel_spmd

    def arr(name):
        return np.ascontiguousarray(a[name])

    def columns(name):
        return np.ascontiguousarray(np.asarray(a[name]).reshape(-1, P).T)

    def turned(name):
        return np.ascontiguousarray(np.asarray(a[name]).T)

    ins = {
        "x": arr("x").reshape(TOK, E),
        "ctxT": np.ascontiguousarray(arr("ctx_2048").reshape(TOK, E).T),
        "mask": arr("mask_BxSxS2_ff0").reshape(TOK, SEQ),
        "g_xattn": arr("g_xattn"), "g_ffn": arr("g_ffn"),
        "L0_WqT": turned("L0_xattn_Wq"), "L0_WkT": turned("L0_xattn_Wk"), "L0_WvT": turned("L0_xattn_Wv"),
        "L0_bq": columns("L0_xattn_bq"), "L0_bk": columns("L0_xattn_bk"), "L0_bv": arr("L0_xattn_bv"),
        "L0_gateT": turned("L0_ffn_w_gate"), "L0_upT": turned("L0_ffn_w_up"), "L0_downT": turned("L0_ffn_w_down"),
        "L0_lnw": arr("L0_ffn_ln_weight"),
        "L1_wqT": turned("L1_xattn_wq"), "L1_wkT": turned("L1_xattn_wk"), "L1_wvT": turned("L1_xattn_wv"),
        "L1_wqxT": turned("L1_xattn_wqx"), "L1_wkvxT": turned("L1_xattn_w_kv_x"), "L1_wprojT": turned("L1_xattn_wproj"),
        "L1_smoothT": np.ascontiguousarray(arr("L1_xattn_proj_smooth").reshape(2 * HEADS, D).T),
        "L1_gate_w": arr("L1_ffn_gate_w"), "L1_gate_b": arr("L1_ffn_gate_b"), "L1_biases": arr("L1_ffn_biases"),
        "L1_W1": np.concatenate([arr("L1_ffn_Ws1")[None], arr("L1_ffn_W1")]),
        "L1_Wg": np.concatenate([arr("L1_ffn_Wsg")[None], arr("L1_ffn_Wg")]),
        "L1_W2": np.concatenate([arr("L1_ffn_Ws2")[None], arr("L1_ffn_W2")]),
    }
    for n in ("ln_w", "ln_b", "q_in_scale", "k_in_scale", "v_in_scale", "qx_in_scale"):
        ins["L1_" + n] = columns("L1_xattn_" + n)
    for n in ("qln_w", "qln_b", "kln_w", "kln_b",
              "qxln_w", "qxln_b", "kxln_w", "kxln_b"):
        ins["L1_" + n] = arr("L1_xattn_" + n)
    for n in ("wq_scale", "wk_scale", "wv_scale", "wqx_scale", "proj_in_scale", "proj_w_scale"):
        ins["L1_" + n] = arr("L1_xattn_" + n).reshape(1)

    nc = bacc.Bacc("TRN2", target_bir_lowering=False, num_devices=1)
    t = {n: nc.dram_tensor("in_" + n, v.shape, mybir.dt.from_np(v.dtype), kind="ExternalInput").ap() for n, v in ins.items()}
    t["out"] = nc.dram_tensor("out_x", (TOK, E), F32, kind="ExternalOutput").ap()
    flamingo_program(nc, t)
    r = run_bass_kernel_spmd(nc, [{"in_" + n: v for n, v in ins.items()}], core_ids=[0])
    return np.asarray(r.results[0]["out_x"]).reshape(BATCH, SEQ, E)
```

```python
from contextlib import ExitStack, contextmanager
from itertools import islice

import concourse.bass as bass
from concourse import mybir

F32 = mybir.dt.float32
F32R = mybir.dt.float32r
BF16 = mybir.dt.bfloat16
U16 = mybir.dt.uint16
ALU = mybir.AluOpType
ACT = mybir.ActivationFunctionType
AX = mybir.AxisListType

P = 128
BATCH, SEQ, E = 16, 64, 256
TOK = BATCH * SEQ
TILES = TOK // P
KT = E // P
ST = 4
GROUPS = TILES // ST
INNER = 1024
HEADS, KV, D = 16, 8, 128
EXPERTS, TOP_K = 7, 3
MAGIC = 1.5 * 2.0 ** 23
FP8_MAX = 448.0
FP8_LEAST = 1.5 * 2.0 ** -6
FP8_SHIFT = 2.0 ** 20
LN_EPS, RMS_EPS, QUANT_EPS = 1e-5, 1e-6, 1e-5


def bcast(ap, axis, n):
    shape = list(ap.shape)
    shape.insert(axis, n)
    return ap.unsqueeze(axis).broadcast_to(shape)


@contextmanager
def phase_semaphores(nc):
    taken = []

    def take(name):
        taken.append(nc.alloc_semaphore(name=name))
        return taken[-1]

    yield take
    nc.clear_and_free_semaphores(taken)
    nc.all_engine_barrier()


def flamingo_program(nc, t):
    ctx = ExitStack()
    with ctx:
        def sb(name, shape, dt=F32):
            return ctx.enter_context(nc.sbuf_tensor(name, shape, dt))

        k = {
            "x": sb("x_res", [P, TILES, E]),
            "ident": sb("ident", [P, P]),
            "identb": sb("identb", [P, P], BF16),
            "ones": sb("ones", [P, P]),
            "half": sb("neg_half", [P, 32]),
            "gate": sb("gate", [P, 4]),
        }
        setup(nc, t, k)
        with ExitStack() as right, ExitStack() as left:
            over_tokens = PassWeights(nc, left, k)
            over_context = PassWeights(nc, left, k, over=over_tokens)
            with ExitStack() as c:
                tern = Ternary(nc, c)
                attention0(nc, t, k, tern)
                bitnet(nc, t, k, tern, over_tokens)
            k["xq"] = right.enter_context(nc.sbuf_tensor("xq_all", [P, 4, KT, TOK], BF16, side="right"))
            quantize_tokens(nc, t, k)
            with phase_semaphores(nc) as take:
                over_context.begin(left, take)
                gqa_pass(nc, t, k, over_tokens, following=over_context)
                gqa_pass(nc, t, k, over_context)
        moe(nc, t, k)
        with nc.semaphore("stored") as stored, nc.Block() as block:
            @block.sync
            def _(sp):
                sp.dma_start(t["out"].rearrange("(n p) e -> p n e", p=P), k["x"][:]).then_inc(stored, 16)
                sp.wait_ge(stored, 16)


def setup(nc, t, k):
    with phase_semaphores(nc) as take, ExitStack() as c:
        loaded = take("setup_loaded")
        filled = take("setup_filled")
        made = take("setup_made")
        raw = c.enter_context(nc.sbuf_tensor("gate_raw", [P, 4], F32))
        block = c.enter_context(nc.Block())

        @block.sync
        def _(sp):
            sp.dma_start(k["x"][:], t["x"].rearrange("(n p) e -> p n e", p=P)).then_inc(loaded, 16)
            sp.dma_start(raw[:, 0:2], t["g_xattn"].rearrange("(o n) -> o n", o=1).broadcast_to([P, 2])).then_inc(loaded, 16)
            sp.dma_start(raw[:, 2:4], t["g_ffn"].rearrange("(o n) -> o n", o=1).broadcast_to([P, 2])).then_inc(loaded, 16)

        @block.gpsimd
        def _(pool):
            nc.gpsimd.memset(k["ident"][:], 0.0).then_inc(filled, 1)
            nc.gpsimd.memset(k["ones"][:], 1.0)
            nc.gpsimd.memset(k["half"][:], -0.5)
            pool.wait_ge(filled, 1)
            nc.gpsimd.affine_select(out=k["ident"][:], in_=k["ident"][:], compare_op=ALU.not_equal, fill=1.0,
                                    base=0, pattern=[[-1, P]], channel_multiplier=1).then_inc(made, 1)
            pool.wait_ge(made, 1)
            nc.gpsimd.tensor_copy(k["identb"][:], k["ident"][:]).then_inc(made, 1)
            pool.wait_ge(made, 2)

        @block.scalar
        def _(act):
            act.wait_ge(loaded, 48)
            nc.scalar.activation(k["gate"][:], raw[:], ACT.Tanh)


class LayerNorm:

    def __init__(self, nc, c, take, name, k):
        self.nc, self.k = nc, k
        self.stats = c.enter_context(nc.sbuf_tensor(name + "_stats", [P, ST, 6], F32))
        self.mv = c.enter_context(nc.sbuf_tensor(name + "_mv", [P, ST, 2], F32))
        self.ve = c.enter_context(nc.sbuf_tensor(name + "_ve", [P, ST], F32))
        self.rstd = c.enter_context(nc.sbuf_tensor(name + "_rstd", [P, ST], F32))
        self.stats_done = take(name + "_stats_done")
        self.mv_done = take(name + "_mv_done")
        self.ve_done = take(name + "_ve_done")
        self.rstd_done = take(name + "_rstd_done")

    def on_vector(self, dve, s, source, out, normed):
        for j in range(ST):
            self.nc.vector.bn_stats(self.stats[:, j, :], source(j)).then_inc(self.stats_done, 1)
        dve.wait_ge(self.stats_done, (s + 1) * ST)
        self.nc.vector.memset(self.ve[:, 0:1], 0.0)
        for j in range(ST):
            self.nc.vector.bn_aggr(self.mv[:, j, :], self.stats[:, j, :]).then_inc(self.mv_done, 1)
        dve.wait_ge(self.mv_done, (s + 1) * ST)
        self.nc.vector.tensor_scalar(self.ve[:], self.mv[:, :, 1], 1.0, LN_EPS, ALU.mult, ALU.add).then_inc(self.ve_done, 1)
        dve.wait_ge(self.rstd_done, s + 1)
        for j in range(ST):
            self.nc.vector.tensor_scalar(out(j), source(j), self.mv[:, j, 0:1], self.rstd[:, j:j + 1],
                                         ALU.subtract, ALU.mult).then_inc(normed, 1)

    def on_pool(self, pool, s):
        pool.wait_ge(self.ve_done, s + 1)
        self.nc.gpsimd.tensor_tensor(self.rstd[:], self.ve[:], self.k["half"][:, 0:ST], ALU.pow).then_inc(self.rstd_done, 1)


def take_steps(eng, steps, n):
    for step in islice(steps, n):
        step(eng)


class Ternary:

    def __init__(self, nc, c):
        def sb(name, shape, dt=F32):
            return c.enter_context(nc.sbuf_tensor("tern_" + name, shape, dt, side="right"))

        self.nc = nc
        self.values = [sb(n, [P, KT * INNER], BF16) for n in ("gate", "up", "down")]
        self.mean = sb("mean", [P, 3])

    def begin(self, c, take):
        self.raw = [c.enter_context(self.nc.sbuf_tensor("tern_raw_" + n, [P, KT * INNER], F32)) for n in ("gate", "up", "down")]
        self.colsum = c.enter_context(self.nc.sbuf_tensor("tern_colsum", [P, 3], F32))
        self.inverse = c.enter_context(self.nc.sbuf_tensor("tern_inverse", [P, 3], F32))
        self.wsum = c.enter_context(self.nc.psum_tensor("tern_wsum", [P, 512], F32))
        self.loaded = [take(f"tern_loaded{n}") for n in range(3)]
        self.colsum_done, self.wsum_done, self.mean_done = take("tern_colsum_done"), take("tern_wsum_done"), take("tern_mean_done")
        self.inverse_done, self.scaled, self.clipped = take("tern_inverse_done"), take("tern_scaled"), take("tern_clipped")

    def on_sync(self, sp, t):
        for n, (src, slices) in enumerate((("L0_gateT", KT), ("L0_upT", KT), ("L0_downT", INNER // P))):
            sp.dma_start(self.raw[n][:].rearrange("p (c f) -> p c f", c=slices),
                         t[src].rearrange("(c p) f -> p c f", p=P)).then_inc(self.loaded[n], 16)

    def on_scalar(self, act, n):
        act.wait_ge(self.loaded[n], 16)
        self.nc.scalar.activation(self.values[n][:], self.raw[n][:], ACT.Abs, accum_out=self.colsum[:, n:n + 1]).then_inc(self.colsum_done, 1)

    def on_tensor(self, pe, k):
        pe.wait_ge(self.colsum_done, 3)
        self.nc.tensor.matmul(self.wsum[:, 0:3], k["ones"][:], self.colsum[:], start=True, stop=True).then_inc(self.wsum_done, 1)

    def means(self, dve):
        dve.wait_ge(self.wsum_done, 1)
        self.nc.vector.tensor_scalar(self.mean[:], self.wsum[:, 0:3], 1.0 / (E * INNER), QUANT_EPS, ALU.mult, ALU.max).then_inc(self.mean_done, 1)
        dve.wait_ge(self.mean_done, 1)
        self.nc.vector.reciprocal(self.inverse[:], self.mean[:]).then_inc(self.inverse_done, 1)
        dve.wait_ge(self.inverse_done, 1)

    def scaling(self, dve, n):
        self.nc.vector.tensor_scalar(self.raw[n][:], self.raw[n][:], self.inverse[:, n:n + 1], 1.0, ALU.mult, ALU.min).then_inc(self.scaled, 1)

    def clipping(self, dve, n):
        dve.wait_ge(self.scaled, n + 1)
        self.nc.vector.tensor_scalar(self.raw[n][:], self.raw[n][:], -1.0, MAGIC, ALU.max, ALU.add).then_inc(self.clipped, 1)

    def rounding(self, dve, n):
        dve.wait_ge(self.clipped, n + 1)
        self.nc.vector.tensor_scalar(self.values[n][:], self.raw[n][:], MAGIC, None, ALU.subtract)

    def on_vector(self):
        yield self.means
        for step in (self.scaling, self.clipping, self.rounding):
            for n in range(3):
                yield lambda dve, step=step, n=n: step(dve, n)


class PassWeights:

    CH = 512
    NQ, NK = HEADS * D // 512, KV * D // 512

    def __init__(self, nc, c, k, over=None):
        cross = over is not None
        L = "x" if cross else "c"

        def sb(name, shape, dt=F32):
            return c.enter_context(nc.sbuf_tensor(f"{L}_{name}", shape, dt))

        self.nc, self.k, self.cross, self.L = nc, k, cross, L
        if cross:
            self.w_hi, self.w_lo, self.p_hi, self.p_lo = over.w_hi, over.w_lo, over.p_hi, over.p_lo
            self.w_ctx, self.staging = sb("w_ctx", [P, 2 * self.NK, KT, self.CH]), sb("staging", [P, 2 * self.NK, KT * self.CH])
        self.smooth, self.ismooth = sb("smooth", [P, HEADS]), sb("ismooth", [P, HEADS])
        self.insc, self.wsc, self.sc = sb("insc", [P, 3, KT]), sb("wsc", [P, 3]), sb("sc", [P, 3, KT])
        self.lnp, self.pscale, self.coef = sb("lnp", [P, 4]), sb("pscale", [P, 2]), sb("coef", [P, 2])
        if cross:
            self.kinds = [("k", 0), ("q", 0), ("q", 1), ("k", 1), ("q", 2), ("q", 3)]
        else:
            self.kinds = [("q", i) for i in range(self.NQ)] + [(kind, i) for kind in "kv" for i in range(self.NK)]
        self.kinds += [("p", i) for i in range(4)]
        if not cross:
            self.p_hi, self.p_lo = sb("p_hi", [P, HEADS, E], F32R), sb("p_lo", [P, HEADS, E], F32R)
            kept = sb("q_hi", [P, self.NQ, KT, self.CH], F32R), sb("q_lo", [P, self.NQ, KT, self.CH], F32R)
            with ExitStack() as given_up:
                passing = [given_up.enter_context(nc.sbuf_tensor(f"{L}_kv_{part}", [P, 2 * self.NK, KT, self.CH], F32R)) for part in ("hi", "lo")]
            self.w_hi, self.w_lo = ([q_[:, i] for i in range(self.NQ)] + [kv[:, i] for i in range(2 * self.NK)]
                                    for q_, kv in zip(kept, passing))
        self.split = [not cross or kind in "qp" for kind, _ in self.kinds]

    def count(self, n, what):
        return sum(what(m) for m in range(n + 1))

    def centred_count(self, n):
        return self.count(n, lambda m: self.kinds[m][0] in "qk")

    def hi_count(self, n):
        return self.count(n, lambda m: self.split[m])

    def vector_lo_count(self, n):
        return self.count(n, lambda m: self.split[m] and self.kinds[m][0] != "p")

    def pool_lo_count(self, n):
        return self.count(n, lambda m: self.kinds[m][0] == "p")

    def begin(self, c, take):
        L, nc = self.L, self.nc
        if self.cross:
            self.STAGES = 2 * self.NK
            self.stage = [self.staging[:, i, :] for i in range(self.STAGES)]
        else:
            self.STAGES = 3
            self.stage = [c.enter_context(nc.sbuf_tensor(f"{L}_stage{i}", [P, KT * self.CH], F32)) for i in range(self.STAGES)]
        self.sums = c.enter_context(nc.sbuf_tensor(f"{L}_sums", [P, self.STAGES, 8], F32))
        self.small_count = 16 * (2 * (1 if self.cross else 3) + 7)
        self.small, self.scales = take(f"{L}_small"), take(f"{L}_scales")
        self.loaded = [take(f"{L}_loaded{i}") for i in range(self.STAGES)]
        self.sum_done, self.mean_done, self.centred = take(f"{L}_wsum_done"), take(f"{L}_wmean_done"), take(f"{L}_centred")
        self.hi_done, self.lo_done, self.plo_done = take(f"{L}_hi_done"), take(f"{L}_lo_done"), take(f"{L}_plo_done")
        self.rest_loaded = take(f"{L}_rest_loaded")

    def slot(self, n):
        kind, i = self.kinds[n]
        return i + {"q": 0, "k": self.NQ, "v": self.NQ + self.NK, "p": 0}[kind]

    def load_small(self, eng, t):
        x_ = "x" if self.cross else ""
        kinds = ("q",) if self.cross else ("q", "k", "v")
        small = [(self.insc[:, n, :], t[f"L1_{m}{x_}_in_scale"]) for n, m in enumerate(kinds)]
        small += [(self.wsc[:, n:n + 1], t[f"L1_w{m}{x_}_scale"].rearrange("(o n) -> o n", o=1).broadcast_to([P, 1])) for n, m in enumerate(kinds)]
        small += [(self.smooth[:], t["L1_smoothT"][:, HEADS * self.cross:HEADS * (self.cross + 1)])]
        small += [(self.lnp[:, n:n + 1], t[f"L1_{m}"].rearrange("(d o) -> d o", o=1))
                  for n, m in enumerate((f"q{x_}ln_w", f"q{x_}ln_b", f"k{x_}ln_w", f"k{x_}ln_b"))]
        small += [(self.pscale[:, n:n + 1], t[m].rearrange("(o n) -> o n", o=1).broadcast_to([P, 1]))
                  for n, m in enumerate(("L1_proj_in_scale", "L1_proj_w_scale"))]
        assert len(small) * 16 == self.small_count
        for dst, src in small:
            eng.dma_start(dst, src).then_inc(self.small, 16)

    def load(self, sp, t, chunks):
        source = {"q": "L1_wqxT" if self.cross else "L1_wqT", "k": "L1_wkvxT" if self.cross else "L1_wkT", "v": "L1_wvT"}
        half = HEADS * D if self.cross else 0
        for n in chunks:
            kind, i = self.kinds[n]
            stage = self.stage[n % self.STAGES]
            if n >= self.STAGES:
                self.ready(sp, n - self.STAGES)
            if kind == "p":
                dst = stage[:].rearrange("p (h f) -> p h f", h=4)
                src = t["L1_wprojT"][half + i * self.CH:half + (i + 1) * self.CH, :].rearrange("(h d) f -> d h f", d=D)
            else:
                dst = stage[:].rearrange("p (c f) -> p c f", c=KT)
                src = t[source[kind]][:, i * self.CH:(i + 1) * self.CH].rearrange("(c p) f -> p c f", p=P)
            sp.dma_start(dst, src).then_inc(self.loaded[n % self.STAGES], 16)

    def load_rest(self, sp, t):
        for i in range(self.NK):
            lo = KV * D + i * self.CH
            sp.dma_start(self.w_ctx[:, self.NK + i], t["L1_wkvxT"][:, lo:lo + self.CH].rearrange("(c p) f -> p c f", p=P)).then_inc(self.rest_loaded, 16)

    def ready(self, eng, n):
        if self.kinds[n][0] == "p":
            eng.wait_ge(self.plo_done, self.pool_lo_count(n))
        elif self.split[n]:
            eng.wait_ge(self.lo_done, self.vector_lo_count(n))
        else:
            eng.wait_ge(self.centred, self.centred_count(n))

    def arrived(self, eng, n):
        eng.wait_ge(self.loaded[n % self.STAGES], 16 * (n // self.STAGES + 1))

    def scale(self, dve):
        V = self.nc.vector
        dve.wait_ge(self.small, self.small_count)
        for n in range(1 if self.cross else 3):
            V.tensor_scalar(self.sc[:, n, :], self.insc[:, n, :], self.wsc[:, n:n + 1], None, ALU.mult).then_inc(self.scales, 1)
        V.reciprocal(self.ismooth[:], self.smooth[:]).then_inc(self.scales, 1)
        V.tensor_tensor(self.coef[:, 0:1], self.pscale[:, 0:1], self.pscale[:, 1:2], ALU.mult).then_inc(self.scales, 1)
        dve.wait_ge(self.scales, 3 if self.cross else 5)
        V.tensor_tensor(self.coef[:, 1:2], self.coef[:, 0:1], self.k["gate"][:, 1:2], ALU.mult).then_inc(self.scales, 1)

    def mean(self, dve, n):
        V, s = self.nc.vector, self.sums[:, n % self.STAGES, :]
        self.arrived(dve, n)
        V.tensor_reduce(s, self.stage[n % self.STAGES][:].rearrange("p (h d) -> p h d", d=D), AX.X, ALU.add).then_inc(self.sum_done, 1)
        dve.wait_ge(self.sum_done, self.centred_count(n))
        V.tensor_scalar(s, s, 1.0 / D, None, ALU.mult).then_inc(self.mean_done, 1)

    def low(self, dve, n):
        dve.wait_ge(self.hi_done, self.hi_count(n))
        kind, at = self.kinds[n][0], self.slot(n)
        for c_ in range(KT):
            last = self.nc.vector.scalar_tensor_tensor(
                self.w_lo[at][:, c_, :], self.stage[n % self.STAGES][:, c_ * self.CH:(c_ + 1) * self.CH],
                self.sc[:, "qkv".index(kind), c_:c_ + 1], self.w_hi[at][:, c_, :].bitcast(F32), ALU.mult, ALU.subtract)
        last.then_inc(self.lo_done, 1)

    def on_vector(self):
        yield self.scale
        for n in range(len(self.kinds) + 1):
            if n < len(self.kinds) and self.kinds[n][0] in "qk":
                yield lambda dve, n=n: self.mean(dve, n)
            if n > 0 and self.split[n - 1] and self.kinds[n - 1][0] != "p":
                yield lambda dve, n=n: self.low(dve, n - 1)

    def high(self, act, n):
        kind, at = self.kinds[n][0], self.slot(n)
        if kind in "qk":
            act.wait_ge(self.centred, self.centred_count(n))
        self.arrived(act, n)
        if kind == "p":
            last = self.nc.scalar.activation(self.p_hi[:, 4 * at:4 * at + 4, :].rearrange("p h f -> p (h f)"), self.stage[n % self.STAGES][:], ACT.Copy)
        else:
            for c_ in range(KT):
                last = self.nc.scalar.activation(self.w_hi[at][:, c_, :], self.stage[n % self.STAGES][:, c_ * self.CH:(c_ + 1) * self.CH],
                                                 ACT.Copy, scale=self.sc[:, "qkv".index(kind), c_:c_ + 1])
        last.then_inc(self.hi_done, 1)

    def on_scalar(self):
        yield lambda act: act.wait_ge(self.scales, 4 if self.cross else 6)
        for n in range(len(self.kinds)):
            if self.split[n]:
                yield lambda act, n=n: self.high(act, n)

    def centre(self, pool, n):
        pool.wait_ge(self.mean_done, self.centred_count(n))
        heads = self.stage[n % self.STAGES][:].rearrange("p (h d) -> p h d", d=D)
        out = heads if self.split[n] else self.w_ctx[:, self.kinds[n][1]].rearrange("p c (h d) -> p (c h) d", d=D)
        self.nc.gpsimd.tensor_tensor(out, heads, bcast(self.sums[:, n % self.STAGES, :], 2, D), ALU.subtract).then_inc(self.centred, 1)

    def low_output(self, pool, n):
        at = slice(4 * self.kinds[n][1], 4 * self.kinds[n][1] + 4)
        pool.wait_ge(self.hi_done, self.hi_count(n))
        self.nc.gpsimd.tensor_tensor(self.p_lo[:, at, :].rearrange("p h f -> p (h f)"), self.stage[n % self.STAGES][:],
                                     self.p_hi[:, at, :].rearrange("p h f -> p (h f)").bitcast(F32), ALU.subtract).then_inc(self.plo_done, 1)

    def on_pool(self):
        for n, (kind, _) in enumerate(self.kinds):
            if kind in "qk":
                yield lambda pool, n=n: self.centre(pool, n)
            if kind == "p":
                yield lambda pool, n=n: self.low_output(pool, n)


def attention0(nc, t, k, tern):
    with phase_semaphores(nc) as take, ExitStack() as c:
        def sb(name, shape, dt=F32):
            return c.enter_context(nc.sbuf_tensor("a_" + name, shape, dt))

        def ps(name):
            return c.enter_context(nc.psum_tensor("a_" + name, [P, 512], F32))

        def sem(name):
            return take("a_" + name)

        wq, wk, wv = sb("wq", [P, KT, E]), sb("wk", [P, KT, E]), sb("wv", [P, KT, E])
        bq, bk, bv = sb("bq", [P, KT]), sb("bk", [P, KT]), sb("bv", [P, E])
        mask = sb("mask", [P, TILES, SEQ])
        xn, xnT = sb("xn", [P, GROUPS, ST, E]), sb("xnT", [P, GROUPS, KT, ST * P])
        qT, kT = sb("qT", [P, GROUPS, KT, ST * P]), sb("kT", [P, GROUPS, KT, ST * P])
        v = sb("v", [P, GROUPS, ST, E])
        s_ = sb("s", [P, GROUPS, ST, SEQ])
        mx, sm, rc = sb("mx", [P, GROUPS, ST]), sb("sm", [P, GROUPS, ST]), sb("rc", [P, GROUPS, ST])
        probs = sb("probs", [P, GROUPS, ST, P])
        pT = sb("pT", [P, GROUPS, ST, P])
        ln = LayerNorm(nc, c, take, "a_ln", k)
        tp = [ps("tp0"), ps("tp1")]
        qk = [ps("qk0"), ps("qk1")]
        vo = [ps("vo0"), ps("vo1")]
        sp_ = ps("scores")
        loaded, normed, turned, xnT_done = sem("loaded"), sem("normed"), sem("turned"), sem("xnT_done")
        qk_done, qk_kept, v_done, v_kept = sem("qk_done"), sem("qk_kept"), sem("v_done"), sem("v_kept")
        sc_done, masked, max_done, sub_done = sem("sc_done"), sem("masked"), sem("max_done"), sem("sub_done")
        exp_done, sum_done, rec_done, probs_done = sem("exp_done"), sem("sum_done"), sem("rec_done"), sem("probs_done")
        pT_turned, pT_kept, o_done, x_done, zeroed = (sem("pT_turned"), sem("pT_kept"), sem("o_done"), sem("x_done"),
                                                      sem("zeroed"))
        tern.begin(c, take)
        block = c.enter_context(nc.Block())

        @block.sync
        def _(sp):
            for dst, src in ((wq, "L0_WqT"), (wk, "L0_WkT"), (wv, "L0_WvT")):
                sp.dma_start(dst[:], t[src].rearrange("(c p) f -> p c f", p=P)).then_inc(loaded, 16)
            for dst, src in ((bq, "L0_bq"), (bk, "L0_bk")):
                sp.dma_start(dst[:], t[src]).then_inc(loaded, 16)
            sp.dma_start(bv[:], t["L0_bv"].rearrange("(o n) -> o n", o=1).broadcast_to([P, E])).then_inc(loaded, 16)
            sp.dma_start(mask[:], t["mask"].rearrange("(n p) s -> p n s", p=P)).then_inc(loaded, 16)
            tern.on_sync(sp, t)

        @block.gpsimd
        def _(pool):
            nc.gpsimd.memset(probs[:], 0.0).then_inc(zeroed, 1)
            for s in range(GROUPS):
                ln.on_pool(pool, s)

        @block.vector
        def _(dve):
            V = nc.vector
            steps = tern.on_vector()

            def norm(s):
                ln.on_vector(dve, s, lambda j: k["x"][:, s * ST + j, :], lambda j: xn[:, s, j, :], normed)

            def keep_values(s):
                for h in range(2):
                    dve.wait_ge(v_done, s * 2 + h + 1)
                    V.tensor_tensor(v[:, s, 2 * h:2 * h + 2, :], vo[h][:].rearrange("p (n e) -> p n e", n=2),
                                    bcast(bv[:], 1, 2), ALU.add).then_inc(v_kept, 1)

            def less_max(s):
                dve.wait_ge(sc_done, s + 1)
                for b in range(2):
                    rows = slice(b * SEQ, (b + 1) * SEQ)
                    V.scalar_tensor_tensor(
                        s_[rows, s], sp_[rows].rearrange("p (n m) -> p n m", n=ST)[:, :, b * SEQ:(b + 1) * SEQ], E ** -0.5,
                        mask[rows, s * ST:(s + 1) * ST, :], ALU.mult, ALU.add).then_inc(masked, 1)
                dve.wait_ge(masked, s * 2 + 2)
                V.tensor_reduce(mx[:, s], s_[:, s], AX.X, ALU.max).then_inc(max_done, 1)
                dve.wait_ge(max_done, s + 1)
                V.tensor_tensor(s_[:, s], s_[:, s], bcast(mx[:, s], 2, SEQ), ALU.subtract).then_inc(sub_done, 1)

            def normalise(s):
                dve.wait_ge(exp_done, s + 1)
                V.tensor_reduce(sm[:, s], s_[:, s], AX.X, ALU.add).then_inc(sum_done, 1)
                dve.wait_ge(sum_done, s + 1)
                V.reciprocal(rc[:, s], sm[:, s]).then_inc(rec_done, 1)
                dve.wait_ge(rec_done, s + 1)
                for b in range(2):
                    rows = slice(b * SEQ, (b + 1) * SEQ)
                    V.tensor_tensor(probs[rows, s, :, b * SEQ:(b + 1) * SEQ], s_[rows, s], bcast(rc[rows, s], 2, SEQ),
                                    ALU.mult).then_inc(probs_done, 1)

            def add_x(s):
                for j in range(ST):
                    tile = k["x"][:, s * ST + j, :]
                    dve.wait_ge(o_done, s * 2 + j // 2 + 1)
                    V.scalar_tensor_tensor(tile, vo[j // 2][:, (j % 2) * E:(j % 2 + 1) * E], k["gate"][:, 0:1], tile,
                                           ALU.mult, ALU.add).then_inc(x_done, 1)

            norm(0)
            norm(1)
            dve.wait_ge(loaded, 7 * 16)
            dve.wait_ge(zeroed, 1)
            keep_values(0)
            less_max(0)
            take_steps(dve, steps, 2)
            normalise(0)
            take_steps(dve, steps, 2)
            keep_values(1)
            take_steps(dve, steps, 1)
            less_max(1)
            take_steps(dve, steps, 1)
            normalise(1)
            add_x(0)
            take_steps(dve, steps, 1)
            add_x(1)
            for step in steps:
                step(dve)

        @block.scalar
        def _(act):
            def turned_tokens(s):
                for c_ in range(KT):
                    act.wait_ge(turned, s * ST + ST)
                    nc.scalar.activation(xnT[:, s, c_, :], tp[c_][:], ACT.Copy).then_inc(xnT_done, 1)

            def keep(s, n):
                dst, bias = ((qT, bq), (kT, bk))[n]
                for f in range(KT):
                    act.wait_ge(qk_done, s * 4 + n * 2 + f + 1)
                    nc.scalar.activation(dst[:, s, f, :], qk[f][:], ACT.Identity, bias=bias[:, f:f + 1]).then_inc(qk_kept, 1)

            def exponent(s):
                act.wait_ge(sub_done, s + 1)
                nc.scalar.activation(s_[:, s], s_[:, s], ACT.Exp).then_inc(exp_done, 1)

            def turned_probs(s):
                act.wait_ge(pT_turned, s + 1)
                nc.scalar.activation(pT[:, s], tp[0][:].rearrange("p (n m) -> p n m", n=ST), ACT.Copy).then_inc(pT_kept, 1)

            turned_tokens(0)
            act.wait_ge(loaded, 7 * 16)
            keep(0, 0)
            keep(0, 1)
            turned_tokens(1)
            tern.on_scalar(act, 0)
            tern.on_scalar(act, 1)
            tern.on_scalar(act, 2)
            exponent(0)
            keep(1, 0)
            keep(1, 1)
            turned_probs(0)
            exponent(1)
            turned_probs(1)

        @block.tensor
        def _(pe):
            def turn(s):
                for j in range(ST):
                    pe.wait_ge(normed, s * ST + j + 1)
                    if s > 0 and j == 0:
                        pe.wait_ge(xnT_done, s * KT)
                    for c_ in range(KT):
                        last = nc.tensor.transpose(tp[c_][:, j * P:(j + 1) * P], xn[:, s, j, c_ * P:(c_ + 1) * P], k["ident"][:])
                    last.then_inc(turned, 1)

            def project_qk(s):
                pe.wait_ge(xnT_done, s * KT + KT)
                for n, w in enumerate((wq, wk)):
                    for f in range(KT):
                        if n == 1 or s > 0:
                            pe.wait_ge(qk_kept, s * 4 + n * 2 + f - 1)
                        for c_ in range(KT):
                            last = nc.tensor.matmul(qk[f][:], w[:, c_, f * P:(f + 1) * P], xnT[:, s, c_, :],
                                                    start=c_ == 0, stop=c_ == KT - 1)
                        last.then_inc(qk_done, 1)

            def project_v(s):
                if s > 0:
                    pe.wait_ge(v_kept, s * 2)
                for j in range(ST):
                    for c_ in range(KT):
                        last = nc.tensor.matmul(vo[j // 2][:, (j % 2) * E:(j % 2 + 1) * E], xnT[:, s, c_, j * P:(j + 1) * P],
                                                wv[:, c_, :], start=c_ == 0, stop=c_ == KT - 1)
                    if j % 2 == 1:
                        last.then_inc(v_done, 1)

            def scores(s):
                pe.wait_ge(qk_kept, s * 4 + 4)
                if s > 0:
                    pe.wait_ge(masked, s * 2)
                for j in range(ST):
                    at = slice(j * P, (j + 1) * P)
                    for c_ in range(KT):
                        last = nc.tensor.matmul(sp_[:, at], qT[:, s, c_, at], kT[:, s, c_, at], start=c_ == 0, stop=c_ == KT - 1)
                last.then_inc(sc_done, 1)

            def turn_probs(s):
                pe.wait_ge(probs_done, s * 2 + 2)
                if s > 0:
                    pe.wait_ge(pT_kept, s)
                for j in range(ST):
                    last = nc.tensor.transpose(tp[0][:, j * P:(j + 1) * P], probs[:, s, j, :], k["ident"][:])
                last.then_inc(pT_turned, 1)

            def attend(s):
                pe.wait_ge(pT_kept, s + 1)
                pe.wait_ge(v_kept, GROUPS * 2)
                for j in range(ST):
                    if s > 0 and j % 2 == 0:
                        pe.wait_ge(x_done, (s - 1) * ST + j + 2)
                    last = nc.tensor.matmul(vo[j // 2][:, (j % 2) * E:(j % 2 + 1) * E], pT[:, s, j, :], v[:, s, j, :],
                                            start=True, stop=True)
                    if j % 2 == 1:
                        last.then_inc(o_done, 1)

            turn(0)
            pe.wait_ge(loaded, 7 * 16)
            project_qk(0)
            turn(1)
            project_v(0)
            scores(0)
            tern.on_tensor(pe, k)
            project_qk(1)
            project_v(1)
            scores(1)
            turn_probs(0)
            attend(0)
            turn_probs(1)
            attend(1)


def bitnet(nc, t, k, tern, weights):
    with phase_semaphores(nc) as take, ExitStack() as c:
        def sb(name, shape, dt=F32):
            return c.enter_context(nc.sbuf_tensor("b_" + name, shape, dt))

        def ps(name, dt=F32):
            return c.enter_context(nc.psum_tensor("b_" + name, [P, 512 if dt == F32 else 1024], dt))

        def sem(name):
            return take("b_" + name)

        FC = INNER // P
        wg, wu = (w[:].rearrange("p (c f) -> p c f", c=KT) for w in tern.values[:2])
        wd = tern.values[2][:].rearrange("p (c f) -> p c f", c=FC)
        mean = tern.mean
        lnw = sb("lnw", [P, INNER])
        xn, rnd, xq = sb("xn", [P, ST, E]), sb("rnd", [P, ST, E]), sb("xq", [P, ST, E], BF16)
        am, inv, sx, dg, du = (sb(n, [P, ST]) for n in ("am", "inv", "sx", "dg", "du"))
        xqT = sb("xqT", [P, KT, ST * P], BF16)
        silu = sb("silu", [P, 2, 512])
        h = sb("h", [P, ST, INNER])
        junk = sb("junk", [P, INNER])
        ssq, ms, r, ah, hm, hinv, hs, od, one = (sb(n, [P, ST]) for n in ("ssq", "ms", "r", "ah", "hm", "hinv", "hs", "od", "rr"))
        hr = sb("hr", [P, 2, INNER])
        hq = sb("hq", [P, ST, INNER], BF16)
        hT = sb("hT", [P, 2, FC, P], BF16)
        ln = LayerNorm(nc, c, take, "b_ln", k)
        tpx = ps("tpx", BF16)
        gp = [ps("g0"), ps("g1")]
        up = [ps("u0"), ps("u1")]
        tph = ps("tph", BF16)
        yp = [ps("y0"), ps("y1")]
        names = ("loaded", "normed",
                 "am_done", "inv_done", "sx_done", "rnd_done", "xq_done", "turned", "xqT_done", "gu_done", "silu_done",
                 "h_done", "ssq_done", "ms_done", "r_done", "hw_done", "hw_last_done", "ah_done", "hm_done", "hinv_done", "hs_done",
                 "hr_done", "hq_done", "hturned", "hT_done", "y_done", "x_done", "d_done")
        q = {n: sem(n) for n in names}
        weights.begin(c, take)
        block = c.enter_context(nc.Block())

        @block.sync
        def _(sp):
            sp.dma_start(lnw[:], t["L0_lnw"].rearrange("(o n) -> o n", o=1).broadcast_to([P, INNER])).then_inc(q["loaded"], 16)
            weights.load_small(sp, t)
            weights.load(sp, t, range(len(weights.kinds)))

        @block.gpsimd
        def _(pool):
            steps = weights.on_pool()
            pool.wait_ge(q["loaded"], 16)
            for s in range(GROUPS):
                ln.on_pool(pool, s)
                take_steps(pool, steps, 3 if s == 0 else 1)
                for j in range(ST - 1):
                    pool.wait_ge(q["ssq_done"], s * ST + j + 1)
                    nc.gpsimd.tensor_tensor(h[:, j, :], h[:, j, :], lnw[:], ALU.mult).then_inc(q["hw_done"], 1)
                pool.wait_ge(q["ms_done"], s + 1)
                nc.gpsimd.tensor_tensor(r[:], ms[:], k["half"][:, 0:ST], ALU.pow).then_inc(q["r_done"], 1)
                take_steps(pool, steps, 2 if s == 0 else 4)

        @block.vector
        def _(dve):
            V = nc.vector
            steps = weights.on_vector()
            for s in range(GROUPS):
                def tile(j):
                    return k["x"][:].rearrange("p n e -> p (n e)")[:, bass.ds(s * (ST * E) + j * E, E)]

                ln.on_vector(dve, s, tile, lambda j: xn[:, j, :], q["normed"])
                dve.wait_ge(q["normed"], s * ST + ST)
                V.tensor_reduce(am[:], xn[:], AX.X, ALU.max, apply_absolute_value=True).then_inc(q["am_done"], 1)
                dve.wait_ge(q["am_done"], s + 1)
                V.tensor_scalar(am[:], am[:], QUANT_EPS, 1.0 / 127.0, ALU.max, ALU.mult).then_inc(q["inv_done"], 1)
                dve.wait_ge(q["inv_done"], s + 1)
                V.reciprocal(sx[:], am[:]).then_inc(q["sx_done"], 1)
                V.tensor_scalar(dg[:], am[:], mean[:, 0:1], None, ALU.mult).then_inc(q["d_done"], 1)
                V.tensor_scalar(du[:], am[:], mean[:, 1:2], None, ALU.mult).then_inc(q["d_done"], 1)
                dve.wait_ge(q["sx_done"], s + 1)
                for j in range(ST):
                    V.tensor_scalar(rnd[:, j, :], xn[:, j, :], sx[:, j:j + 1], MAGIC, ALU.mult, ALU.add).then_inc(q["rnd_done"], 1)
                dve.wait_ge(q["rnd_done"], s * ST + ST)
                V.tensor_scalar(xq[:], rnd[:], MAGIC, None, ALU.subtract).then_inc(q["xq_done"], 1)
                dve.wait_ge(q["d_done"], s * 2 + 2)
                take_steps(dve, steps, 3 if s == 0 else 2)
                for n in range(2 * ST):
                    j, f = n // 2, n % 2
                    dve.wait_ge(q["silu_done"], s * 2 * ST + n + 1)
                    V.scalar_tensor_tensor(h[:, j, f * 512:(f + 1) * 512], up[n % 2][:], du[:, j:j + 1], silu[:, n % 2, :],
                                           ALU.mult, ALU.mult).then_inc(q["h_done"], 1)
                    if f == 1:
                        take_steps(dve, steps, 1)
                if s == 0:
                    dve.wait_ge(q["loaded"], 16)
                for j in range(ST):
                    if j < ST - 1:
                        dve.wait_ge(q["hw_done"], s * (ST - 1) + j + 1)
                    else:
                        dve.wait_ge(q["hw_last_done"], s + 1)
                    V.tensor_reduce(ah[:, j:j + 1], h[:, j, :], AX.X, ALU.max, apply_absolute_value=True).then_inc(q["ah_done"], 1)
                    if j == 0:
                        dve.wait_ge(q["ssq_done"], s * ST + ST)
                        V.tensor_scalar(ms[:], ssq[:], 1.0 / INNER, RMS_EPS, ALU.mult, ALU.add).then_inc(q["ms_done"], 1)
                        V.tensor_tensor(h[:, ST - 1, :], h[:, ST - 1, :], lnw[:], ALU.mult).then_inc(q["hw_last_done"], 1)
                dve.wait_ge(q["ah_done"], s * ST + ST)
                dve.wait_ge(q["r_done"], s + 1)
                V.tensor_tensor(hm[:], ah[:], r[:], ALU.mult).then_inc(q["hm_done"], 1)
                dve.wait_ge(q["hm_done"], s * 2 + 1)
                V.tensor_scalar(hm[:], hm[:], QUANT_EPS, 1.0 / 127.0, ALU.max, ALU.mult).then_inc(q["hm_done"], 1)
                dve.wait_ge(q["hm_done"], s * 2 + 2)
                V.reciprocal(hinv[:], hm[:]).then_inc(q["hinv_done"], 1)
                V.tensor_scalar(od[:], hm[:], mean[:, 2:3], k["gate"][:, 2:3], ALU.mult, ALU.mult).then_inc(q["hinv_done"], 1)
                dve.wait_ge(q["hinv_done"], s * 2 + 2)
                V.tensor_tensor(hs[:], hinv[:], r[:], ALU.mult).then_inc(q["hs_done"], 1)
                dve.wait_ge(q["hs_done"], s + 1)
                for j in range(ST):
                    V.tensor_scalar(hr[:, j % 2, :], h[:, j, :], hs[:, j:j + 1], MAGIC, ALU.mult, ALU.add).then_inc(q["hr_done"], 1)
                    dve.wait_ge(q["hr_done"], s * ST + j + 1)
                    V.tensor_scalar(hq[:, j, :], hr[:, j % 2, :], MAGIC, None, ALU.subtract).then_inc(q["hq_done"], 1)
                take_steps(dve, steps, 2 if s == 0 else 0)
                for j in range(ST):
                    dve.wait_ge(q["y_done"], s * ST + j + 1)
                    V.scalar_tensor_tensor(tile(j), yp[j % 2][:, 0:E], od[:, j:j + 1], tile(j),
                                           ALU.mult, ALU.add).then_inc(q["x_done"], 1)

        @block.scalar
        def _(act):
            steps = weights.on_scalar()
            for s in range(GROUPS):
                act.wait_ge(q["turned"], s + 1)
                nc.scalar.activation(xqT[:].rearrange("p c m -> p (c m)"), tpx[:], ACT.Copy).then_inc(q["xqT_done"], 1)
                act.wait_ge(q["d_done"], s * 2 + 2)
                take_steps(act, steps, 1 if s == 0 else 0)

                def square(j):
                    act.wait_ge(q["h_done"], s * 2 * ST + 2 * j + 2)
                    if j > 0:
                        act.wait_ge(q["ssq_done"], s * ST + j)
                    nc.scalar.activation(junk[:], h[:, j, :], ACT.Square, accum_out=ssq[:, j:j + 1]).then_inc(q["ssq_done"], 1)

                for n in range(2 * ST):
                    j, f = n // 2, n % 2
                    act.wait_ge(q["gu_done"], s * 2 * ST + n + 1)
                    if n >= 2:
                        act.wait_ge(q["h_done"], s * 2 * ST + n - 1)
                    nc.scalar.activation(silu[:, n % 2, :], gp[n % 2][:], ACT.Silu, scale=dg[:, j:j + 1]).then_inc(q["silu_done"], 1)
                    if n in ((0, 3, 6) if s == 0 else (0, 2, 4)):
                        take_steps(act, steps, 1)
                    if n % 2 == 1 and n > 1:
                        square(n // 2 - 1)
                square(ST - 1)
                take_steps(act, steps, 1 if s == 0 else 2)
                for j in range(ST):
                    act.wait_ge(q["hturned"], s * ST + j + 1)
                    if j >= 2:
                        act.wait_ge(q["y_done"], s * ST + j - 1)
                    nc.scalar.activation(hT[:, j % 2].rearrange("p c m -> p (c m)"), tph[:], ACT.Copy).then_inc(q["hT_done"], 1)
                take_steps(act, steps, 1 if s == 0 else 2)

        @block.tensor
        def _(pe):
            for s in range(GROUPS):
                pe.wait_ge(q["xq_done"], s + 1)
                for j in range(ST):
                    for c_ in range(KT):
                        last = nc.tensor.transpose(tpx[:, (c_ * ST + j) * P:(c_ * ST + j + 1) * P], xq[:, j, c_ * P:(c_ + 1) * P], k["identb"][:])
                last.then_inc(q["turned"], 1)
                pe.wait_ge(q["xqT_done"], s + 1)
                for n in range(2 * ST):
                    j, f = n // 2, n % 2
                    if n >= 2:
                        pe.wait_ge(q["h_done"], s * 2 * ST + n - 1)
                    for w, dst in ((wg, gp[n % 2]), (wu, up[n % 2])):
                        for c_ in range(KT):
                            last = nc.tensor.matmul(dst[:], xqT[:, c_, j * P:(j + 1) * P], w[:, c_, f * 512:(f + 1) * 512],
                                                    start=c_ == 0, stop=c_ == KT - 1)
                    last.then_inc(q["gu_done"], 1)

                def turn(j):
                    pe.wait_ge(q["hq_done"], s * ST + j + 1)
                    if j > 0:
                        pe.wait_ge(q["hT_done"], s * ST + j)
                    for c_ in range(FC):
                        last = nc.tensor.transpose(tph[:, c_ * P:(c_ + 1) * P], hq[:, j, c_ * P:(c_ + 1) * P], k["identb"][:])
                    last.then_inc(q["hturned"], 1)

                def down(j):
                    pe.wait_ge(q["hT_done"], s * ST + j + 1)
                    if j >= 2:
                        pe.wait_ge(q["x_done"], s * ST + j - 1)
                    for c_ in range(FC):
                        last = nc.tensor.matmul(yp[j % 2][:, 0:E], hT[:, j % 2, c_, :], wd[:, c_, :],
                                                start=c_ == 0, stop=c_ == FC - 1)
                    last.then_inc(q["y_done"], 1)

                turn(0)
                for j in range(1, ST):
                    turn(j)
                    down(j - 1)
                down(ST - 1)


def quantize_tokens(nc, t, k):
    with phase_semaphores(nc) as take, ExitStack() as c:
        def sb(name, shape, dt=F32):
            return c.enter_context(nc.sbuf_tensor("n_" + name, shape, dt))

        def sem(name):
            return take("n_" + name)

        N = ST * P
        W = 4 * KT
        UNITS = GROUPS * W
        lw, lb, ins, inv = sb("lw", [P, KT]), sb("lb", [P, KT]), sb("ins", [P, 4 * KT]), sb("inv", [P, 4 * KT])
        xn, xm, lnT = sb("xn", [P, GROUPS, ST, E]), sb("xm", [P, GROUPS, ST, E]), sb("lnT", [P, GROUPS, KT, N])
        yb, kb, big = sb("yb", [P, 4, N], BF16), sb("kb", [P, 4, N], BF16), sb("big", [P, 4, N])
        ln1, ln2 = LayerNorm(nc, c, take, "n_ln1", k), LayerNorm(nc, c, take, "n_ln2", k)
        tp = [c.enter_context(nc.psum_tensor(f"n_tp{i}", [P, N], F32)) for i in range(GROUPS * KT)]
        q = {n: sem(n) for n in ("loaded", "inv_done", "normed", "normed2", "turned", "lnT_done", "y_done", "clipped", "abs_done",
                                 "k_done", "big_done", "xq_done")}
        block = c.enter_context(nc.Block())

        @block.sync
        def _(sp):
            for dst, src in ((lw, "L1_ln_w"), (lb, "L1_ln_b")):
                sp.dma_start(dst[:], t[src]).then_inc(q["loaded"], 16)
            for n, src in enumerate(("L1_q_in_scale", "L1_k_in_scale", "L1_v_in_scale", "L1_qx_in_scale")):
                sp.dma_start(ins[:, n * KT:(n + 1) * KT], t[src]).then_inc(q["loaded"], 16)

        @block.gpsimd
        def _(pool):
            def subtract(u):
                s, w = u // W, u % W
                pool.wait_ge(q["big_done"], u + 1)
                nc.gpsimd.tensor_tensor(k["xq"][:, w // KT, w % KT, s * N:(s + 1) * N], big[:, u % 4, :], kb[:, u % 4, :],
                                        ALU.subtract).then_inc(q["xq_done"], 1)

            ln1.on_pool(pool, 0)
            ln2.on_pool(pool, 0)
            ln1.on_pool(pool, 1)
            subtract(0)
            subtract(1)
            ln2.on_pool(pool, 1)
            for u in range(2, UNITS):
                subtract(u)

        @block.vector
        def _(dve):
            V = nc.vector

            def first_norm(s):
                ln1.on_vector(dve, s, lambda j: k["x"][:, s * ST + j, :], lambda j: xn[:, s, j, :], q["normed"])

            def second_norm(s):
                dve.wait_ge(q["normed"], s * ST + ST)
                ln2.on_vector(dve, s, lambda j: xn[:, s, j, :], lambda j: xm[:, s, j, :], q["normed2"])

            def round_two(u0):
                two = (u0, u0 + 1)
                for u in two:
                    dve.wait_ge(q["y_done"], u + 1)
                    V.tensor_scalar(yb[:, u % 4, :], yb[:, u % 4, :], FP8_MAX, -FP8_MAX, ALU.min, ALU.max).then_inc(q["clipped"], 1)
                for u in two:
                    if u >= 4:
                        dve.wait_ge(q["xq_done"], u - 3)
                    dve.wait_ge(q["clipped"], u + 1)
                    V.tensor_scalar(kb[:, u % 4, :].bitcast(U16), yb[:, u % 4, :].bitcast(U16), 0x7FFF, None,
                                    ALU.bitwise_and).then_inc(q["abs_done"], 1)
                for u in two:
                    dve.wait_ge(q["abs_done"], u + 1)
                    V.tensor_scalar(kb[:, u % 4, :], kb[:, u % 4, :], FP8_LEAST, FP8_SHIFT, ALU.max, ALU.mult).then_inc(q["k_done"], 1)
                for u in two:
                    dve.wait_ge(q["k_done"], u + 1)
                    V.tensor_tensor(big[:, u % 4, :], yb[:, u % 4, :], kb[:, u % 4, :], ALU.add).then_inc(q["big_done"], 1)

            first_norm(0)
            dve.wait_ge(q["loaded"], 96)
            V.reciprocal(inv[:], ins[:]).then_inc(q["inv_done"], 1)
            second_norm(0)
            first_norm(1)
            round_two(0)
            second_norm(1)
            for u in range(2, UNITS, 2):
                round_two(u)

        @block.scalar
        def _(act):
            def turned(s):
                act.wait_ge(q["turned"], s + 1)
                for c_ in range(KT):
                    nc.scalar.activation(lnT[:, s, c_, :], tp[s * KT + c_][:], ACT.Identity, bias=lb[:, c_:c_ + 1],
                                         scale=lw[:, c_:c_ + 1]).then_inc(q["lnT_done"], 1)

            def over_scale(u):
                s, w = u // W, u % W
                act.wait_ge(q["lnT_done"], s * KT + w % KT + 1)
                if u >= 4:
                    act.wait_ge(q["big_done"], u - 3)
                nc.scalar.activation(yb[:, u % 4, :], lnT[:, s, w % KT, :], ACT.Copy, scale=inv[:, w:w + 1]).then_inc(q["y_done"], 1)

            act.wait_ge(q["loaded"], 96)
            act.wait_ge(q["inv_done"], 1)
            turned(0)
            for u in range(4):
                over_scale(u)
            turned(1)
            for u in range(4, UNITS):
                over_scale(u)

        @block.tensor
        def _(pe):
            for s in range(GROUPS):
                for j in range(ST):
                    pe.wait_ge(q["normed2"], s * ST + j + 1)
                    for c_ in range(KT):
                        last = nc.tensor.transpose(tp[s * KT + c_][:, j * P:(j + 1) * P], xm[:, s, j, c_ * P:(c_ + 1) * P], k["ident"][:])
                last.then_inc(q["turned"], 1)


def gqa_pass(nc, t, k, weights, following=None):
    cross = weights.cross
    L = "x2" if cross else "c2"
    with phase_semaphores(nc) as take, ExitStack() as c:
        def sb(name, shape, dt=F32):
            return c.enter_context(nc.sbuf_tensor(f"{L}_{name}", shape, dt))

        def ps(name):
            return c.enter_context(nc.psum_tensor(f"{L}_{name}", [P, 512], F32))

        def sem(name):
            return take(f"{L}_{name}")

        CH = 512
        NQ, NK = HEADS * D // CH, KV * D // CH
        NN = NQ + NK
        NC = NN + NK
        NV = 1 if cross else 3
        GH = KV // 2
        w_hi, w_lo, p_hi, p_lo = weights.w_hi, weights.w_lo, weights.p_hi, weights.p_lo
        w_ctx = weights.w_ctx if cross else None
        ismooth, lnp, coef = weights.ismooth, weights.lnp, weights.coef
        qkT = sb("qkT", [P, 2, HEADS + KV, P])
        v = sb("v", [P, 2, KV * D])
        xqc = sb("xqc", [P, 2, NV * KT, P], F32R)
        ctxT = sb("ctxT", [P, KT, TOK]) if cross else None
        ctxc = sb("ctxc", [P, 2, KT, P]) if cross else None
        sq, ss = sb("sq", [P, 2, CH]), sb("ss", [P, 2, 4])
        ve, rs, qn = sb("ve", [P, 2, 4]), sb("rs", [P, 2, 4]), sb("qn", [P, 2, CH])
        ex = sb("ex", [P, 2, CH])
        mx, sm, rc = sb("mx", [P, 2, 8]), sb("sm", [P, 2, 8]), sb("rc", [P, 2, 8])
        pT = sb("pT", [P, 2, GH, P])
        yb, kb, big = sb("yb", [P, 2, 2 * CH], BF16), sb("kb", [P, 2, 2 * CH], BF16), sb("big", [P, 2, 2 * CH])
        cat = sb("cat", [P, 2, 2 * GH, P], F32R)
        proj = [ps("proj0"), ps("proj1"), ps("proj2")]
        turns = [ps("turn0"), ps("turn1")]
        sp_ = ps("scores")
        op = c.enter_context(nc.psum_tensor(f"{L}_op", [P, 2, CH], F32))
        CHUNKS = (("k", 0), ("q", 0), ("q", 1), ("k", 1), ("q", 2), ("q", 3), ("v", 0), ("v", 1))
        PROJ_BANK = (0, 1, 0, 1, 2, 0, 1, 2)
        OUT_BANK = 2
        TURN_BANK, PROBS_BANK = (0, 0, 1, 1, 0, 1), (1, 0)

        names = ("ctx_loaded", "xqc_done", "ctxc_done", "qkv_done", "turned", "sc_done", "pt_done", "pv_done", "y_done", "sq_done", "tev_done",
                 "vev_done", "exp_done", "ptev_done", "ss_done", "qn_done", "max_done", "sub_done", "sum_done", "rec_done",
                 "pn_done", "q1_done", "clipped", "abs_done", "k_done", "big_done", "cat_done", "x_done", "ve_done", "rs_done")
        q = {n: sem(n) for n in names}


        def run(eng, ahead, both, alone, last):
            ahead(0, 0, True)
            both(0, 0, True)
            both(1, 1, False)
            with eng.Fori(1, TILES // 2 - 1) as i:
                both(i * 2, 0, False)
                both(i * 2 + 1, 1, False)
            both(TILES - 2, 0, False)
            alone(TILES - 1, 1)
            last(TILES - 1)

        with nc.Block() as block:
            @block.sync
            def _(sp):
                if cross:
                    source = t["ctxT"].rearrange("(c p) n -> p c n", p=P)
                    for tokens in (slice(0, 2 * P), slice(2 * P, TOK)):
                        sp.dma_start(ctxT[:, :, tokens], source[:, :, tokens]).then_inc(q["ctx_loaded"], 16)
                        if tokens.start == 0:
                            sp.wait_ge(q["ctx_loaded"], 16)
                    weights.load(sp, t, range(NN, len(weights.kinds)))
                if following:
                    following.load_small(sp, t)
                    sp.wait_ge(q["qkv_done"], TILES * NC)
                    following.load(sp, t, range(NN))
                    following.load_rest(sp, t)

            @block.gpsimd
            def _(pool):
                G = nc.gpsimd

                def copy_tile(n, par, wait):
                    if wait:
                        pool.wait_ge(q["qkv_done"], n * NC - NC)
                    src = k["xq"][:, 3:4] if cross else k["xq"][:, 0:3]
                    G.tensor_copy(xqc[:, par], src.rearrange("p v c n -> p (v c) n")[:, :, bass.ds(n * P, P)]).then_inc(q["xqc_done"], 1)

                def copy_context(n, par):
                    if cross:
                        G.tensor_copy(ctxc[:, par], ctxT[:, :, bass.ds(n * P, P)]).then_inc(q["ctxc_done"], 1)

                def rstd(n, i, first):
                    u = i % 2
                    if not (first and i < 2):
                        pool.wait_ge(q["qn_done"], n * NN + i - 1)
                    pool.wait_ge(q["ve_done"], n * NN + i + 1)
                    G.tensor_tensor(rs[:, u, :], ve[:, u, :], k["half"][:, 0:4], ALU.pow).then_inc(q["rs_done"], 1)

                def normalise(n, h):
                    e3 = ex[:, h, :].rearrange("p (g s) -> p g s", s=SEQ)
                    pool.wait_ge(q["rec_done"], n * 2 + h + 1)
                    G.tensor_tensor(e3, e3, bcast(rc[:, h, :], 2, SEQ), ALU.mult).then_inc(q["pn_done"], 1)

                def fp8(n, h):
                    pool.wait_ge(q["big_done"], n * 2 + h + 1)
                    if not (isinstance(n, int) and n == 0):
                        pool.wait_ge(q["y_done"], n)
                    G.tensor_tensor(cat[:, h].rearrange("p h (b s) -> p b h s", b=2), big[:, h, :].rearrange("p (b h s) -> p b h s", b=2, s=SEQ),
                                    kb[:, h, :].rearrange("p (b h s) -> p b h s", b=2, s=SEQ), ALU.subtract).then_inc(q["cat_done"], 1)

                def ahead(n, par, first):
                    copy_tile(0, 0, False)
                    copy_tile(1, 1, False)
                    if cross:
                        pool.wait_ge(q["ctx_loaded"], 16)
                    copy_context(0, 0)
                    copy_context(1, 1)
                    for i in range(NN):
                        rstd(n, i, first)
                    if cross:
                        pool.wait_ge(q["ctx_loaded"], 32)

                def both(n, par, first):
                    prepare = cross and first
                    rstd(n + 1, 0, False)
                    rstd(n + 1, 1, False)
                    if not (isinstance(n, int) and n == TILES - 2):
                        copy_tile(n + 2, par, True)
                        copy_context(n + 2, par)
                    normalise(n, 0)
                    if prepare:
                        weights.low_output(pool, NN)
                    rstd(n + 1, 2, False)
                    rstd(n + 1, 3, False)
                    normalise(n, 1)
                    if prepare:
                        weights.low_output(pool, NN + 1)
                    rstd(n + 1, 4, False)
                    rstd(n + 1, 5, False)
                    fp8(n, 0)
                    if prepare:
                        weights.low_output(pool, NN + 2)
                    fp8(n, 1)
                    if prepare:
                        weights.low_output(pool, NN + 3)

                def alone(n, par):
                    def centre(*chunks):
                        for m in chunks if following else ():
                            following.centre(pool, m)

                    normalise(n, 0)
                    centre(0)
                    normalise(n, 1)
                    centre(1, 2)
                    fp8(n, 0)
                    centre(3, 4)
                    fp8(n, 1)
                    centre(5)

                run(pool, ahead, both, alone, lambda n: None)

            @block.vector
            def _(dve):
                V = nc.vector

                def sums(n, i):
                    dve.wait_ge(q["sq_done"], n * NN + i + 1)
                    V.tensor_reduce(ss[:, i % 2, :], sq[:, i % 2, :].rearrange("p (h d) -> p h d", d=D), AX.X, ALU.add).then_inc(q["ss_done"], 1)
                    dve.wait_ge(q["ss_done"], n * NN + i + 1)
                    V.tensor_scalar(ve[:, i % 2, :], ss[:, i % 2, :], 1.0 / D, LN_EPS, ALU.mult, ALU.add).then_inc(q["ve_done"], 1)

                def scale(n, i, first):
                    dve.wait_ge(q["rs_done"], n * NN + i + 1)
                    if not (first and i < 2):
                        dve.wait_ge(q["turned"], n * NN + i - 1)
                    V.tensor_tensor(qn[:, i % 2, :].rearrange("p (h d) -> p h d", d=D), proj[PROJ_BANK[i]][:].rearrange("p (h d) -> p h d", d=D),
                                    bcast(rs[:, i % 2, :], 2, D), ALU.mult).then_inc(q["qn_done"], 1)

                def less_max(n, h, first):
                    dve.wait_ge(q["sc_done"], n * 2 + h + 1)
                    s3 = sp_[:].rearrange("p (g s) -> p g s", s=SEQ)
                    V.tensor_reduce(mx[:, h, :], s3, AX.X, ALU.max).then_inc(q["max_done"], 1)
                    dve.wait_ge(q["max_done"], n * 2 + h + 1)
                    if not first:
                        dve.wait_ge(q["pt_done"], n * 2 + h - 1)
                    V.tensor_tensor(ex[:, h, :].rearrange("p (g s) -> p g s", s=SEQ), s3, bcast(mx[:, h, :], 2, SEQ),
                                    ALU.subtract).then_inc(q["sub_done"], 1)

                def total(n, h, first):
                    e3 = ex[:, h, :].rearrange("p (g s) -> p g s", s=SEQ)
                    dve.wait_ge(q["exp_done"], n * 2 + h + 1)
                    V.tensor_reduce(sm[:, h, :], e3, AX.X, ALU.add).then_inc(q["sum_done"], 1)
                    dve.wait_ge(q["sum_done"], n * 2 + h + 1)
                    if not first:
                        dve.wait_ge(q["pn_done"], n * 2 + h - 1)
                    V.reciprocal(rc[:, h, :], sm[:, h, :]).then_inc(q["rec_done"], 1)

                def unload(n, h, first):
                    dve.wait_ge(q["pv_done"], n * 2 + h + 1)
                    if not first:
                        dve.wait_ge(q["big_done"], n * 2 + h - 1)
                    V.tensor_tensor(yb[:, h, :].rearrange("p (b h s) -> p b h s", b=2, s=SEQ),
                                    op[:].rearrange("p b (h s) -> p b h s", s=SEQ),
                                    bcast(bcast(ismooth[:, 2 * GH * h:2 * GH * (h + 1)], 1, 2), 3, SEQ), ALU.mult).then_inc(q["q1_done"], 1)

                def rounding(n, h, first):
                    dve.wait_ge(q["q1_done"], n * 2 + h + 1)
                    V.tensor_scalar(yb[:, h, :], yb[:, h, :], FP8_MAX, -FP8_MAX, ALU.min, ALU.max).then_inc(q["clipped"], 1)
                    if not first:
                        dve.wait_ge(q["cat_done"], n * 2 + h - 1)
                    dve.wait_ge(q["clipped"], n * 2 + h + 1)
                    V.tensor_scalar(kb[:, h, :].bitcast(U16), yb[:, h, :].bitcast(U16), 0x7FFF, None, ALU.bitwise_and).then_inc(q["abs_done"], 1)
                    dve.wait_ge(q["abs_done"], n * 2 + h + 1)
                    V.tensor_scalar(kb[:, h, :], kb[:, h, :], FP8_LEAST, FP8_SHIFT, ALU.max, ALU.mult).then_inc(q["k_done"], 1)
                    dve.wait_ge(q["k_done"], n * 2 + h + 1)
                    V.tensor_tensor(big[:, h, :], yb[:, h, :], kb[:, h, :], ALU.add).then_inc(q["big_done"], 1)

                def add_x(n):
                    tile = k["x"][:].rearrange("p n e -> p (n e)")[:, bass.ds(n * E, E)]
                    dve.wait_ge(q["y_done"], n + 1)
                    V.scalar_tensor_tensor(tile, proj[OUT_BANK][:, 0:E], coef[:, 1:2], tile, ALU.mult, ALU.add).then_inc(q["x_done"], 1)

                def ahead(n, par, first):
                    for i in range(0, NN, 2):
                        sums(n, i)
                        sums(n, i + 1)
                        scale(n, i, first)
                        scale(n, i + 1, first)

                def both(n, par, first):
                    m = n + 1
                    less_max(n, 0, first)
                    sums(m, 0)
                    sums(m, 1)
                    less_max(n, 1, first)
                    scale(m, 0, False)
                    total(n, 0, first)
                    scale(m, 1, False)
                    total(n, 1, first)
                    if not first:
                        add_x(n - 1)
                    sums(m, 2)
                    sums(m, 3)
                    scale(m, 2, False)
                    sums(m, 4)
                    scale(m, 3, False)
                    unload(n, 0, first)
                    sums(m, 5)
                    scale(m, 4, False)
                    rounding(n, 0, first)
                    scale(m, 5, False)
                    unload(n, 1, first)
                    rounding(n, 1, first)

                def alone(n, par):
                    def prepare(*steps):
                        for step, *m in steps if following else ():
                            {"scale": following.scale, "mean": following.mean, "low": following.low}[step](dve, *m)

                    less_max(n, 0, False)
                    prepare(("scale",))
                    total(n, 0, False)
                    less_max(n, 1, False)
                    prepare(("mean", 0))
                    total(n, 1, False)
                    add_x(n - 1)
                    prepare(("mean", 1), ("mean", 2))
                    unload(n, 0, False)
                    rounding(n, 0, False)
                    prepare(("low", 1), ("mean", 3), ("low", 2), ("mean", 4))
                    unload(n, 1, False)
                    rounding(n, 1, False)
                    prepare(("mean", 5), ("low", 4), ("low", 5))

                run(dve, ahead, both, alone, add_x)

            @block.scalar
            def _(act):
                A = nc.scalar

                def square(n, i, first):
                    act.wait_ge(q["qkv_done"], n * NC + i + 1)
                    if not (first and i < 2):
                        act.wait_ge(q["ss_done"], n * NN + i - 1)
                    A.activation(sq[:, i % 2, :], proj[PROJ_BANK[i]][:], ACT.Square).then_inc(q["sq_done"], 1)

                def keep_qk(n, i, par):
                    act.wait_ge(q["turned"], n * NN + i + 1)
                    kind, at = CHUNKS[i]
                    w, at = (0, 4 * at) if kind == "q" else (2, HEADS + 4 * at)
                    A.activation(qkT[:, par, at:at + 4, :], turns[TURN_BANK[i]][:].rearrange("p (h m) -> p h m", h=4), ACT.Identity,
                                 bias=lnp[:, w + 1:w + 2], scale=lnp[:, w:w + 1]).then_inc(q["tev_done"], 1)

                def keep_v(n, i, par):
                    act.wait_ge(q["qkv_done"], n * NC + NN + i + 1)
                    A.activation(v[:, par, i * CH:(i + 1) * CH], proj[PROJ_BANK[NN + i]][:], ACT.Copy).then_inc(q["vev_done"], 1)

                def exponent(n, h):
                    act.wait_ge(q["sub_done"], n * 2 + h + 1)
                    A.activation(ex[:, h, :], ex[:, h, :], ACT.Exp, scale=D ** -0.5).then_inc(q["exp_done"], 1)

                def keep_pT(n, h):
                    act.wait_ge(q["pt_done"], n * 2 + h + 1)
                    A.activation(pT[:, h], turns[PROBS_BANK[h]][:].rearrange("p (g m) -> p g m", g=GH), ACT.Copy).then_inc(q["ptev_done"], 1)

                def ahead(n, par, first):
                    square(n, 0, first)
                    square(n, 1, first)
                    for i in range(2, NN):
                        keep_qk(n, i - 2, par)
                        square(n, i, first)
                    keep_v(n, 0, par)
                    keep_qk(n, NN - 2, par)
                    keep_v(n, 1, par)
                    keep_qk(n, NN - 1, par)

                def both(n, par, first):
                    m, mp = n + 1, 1 - par
                    prepare = cross and first
                    square(m, 0, False)
                    exponent(n, 0)
                    square(m, 1, False)
                    exponent(n, 1)
                    if prepare:
                        weights.high(act, NN)
                    square(m, 2, False)
                    keep_qk(m, 0, mp)
                    if prepare:
                        weights.high(act, NN + 1)
                    square(m, 3, False)
                    keep_pT(n, 0)
                    if prepare:
                        weights.high(act, NN + 2)
                    square(m, 4, False)
                    keep_qk(m, 1, mp)
                    square(m, 5, False)
                    keep_pT(n, 1)
                    keep_v(m, 0, mp)
                    keep_qk(m, 2, mp)
                    keep_qk(m, 3, mp)
                    if prepare:
                        weights.high(act, NN + 3)
                    keep_v(m, 1, mp)
                    keep_qk(m, 4, mp)
                    keep_qk(m, 5, mp)

                def alone(n, par):
                    exponent(n, 0)
                    exponent(n, 1)
                    keep_pT(n, 0)
                    if following:
                        act.wait_ge(following.scales, 4)
                        following.high(act, 1)
                    keep_pT(n, 1)
                    if following:
                        for m in (2, 4, 5):
                            following.high(act, m)

                run(act, ahead, both, alone, lambda n: None)

            @block.tensor
            def _(pe):
                T = nc.tensor

                def project(n, i, par, first):
                    if i == 0:
                        pe.wait_ge(q["xqc_done"], n + 1)
                        if cross:
                            pe.wait_ge(q["ctxc_done"], n + 1)
                    if cross and first and i == NN:
                        pe.wait_ge(weights.rest_loaded, 16 * NK)
                    if i == 0 and not first:
                        pe.wait_ge(q["qn_done"], n * NN)
                    if i == 1 and not first:
                        pe.wait_ge(q["vev_done"], n * NK - 1)
                    if i in (2, 3):
                        pe.wait_ge(q["qn_done"], n * NN + i - 1)
                    if i == 4 and not first and not (isinstance(n, int) and n == 1):
                        pe.wait_ge(q["x_done"], n - 1)
                    if i > 4:
                        pe.wait_ge(q["qn_done"], n * NN + i - 2)
                    bank = proj[PROJ_BANK[i]][:]
                    kind, at = CHUNKS[i]
                    if kind == "q" or not cross:
                        v_, at = {"q": (0, at), "k": (1, NQ + at), "v": (2, NN + at)}[kind]
                        for c_ in range(KT):
                            for part in range(2):
                                last = T.matmul(bank, xqc[:, par, v_ * KT + c_, :], (w_hi, w_lo)[part][at][:, c_, :],
                                                start=c_ == 0 and part == 0, stop=c_ == KT - 1 and part == 1)
                    else:
                        at += 0 if kind == "k" else NK
                        for c_ in range(KT):
                            last = T.matmul(bank, ctxc[:, par, c_, :], w_ctx[:, at, c_, :], start=c_ == 0, stop=c_ == KT - 1)
                    last.then_inc(q["qkv_done"], 1)

                def turn(n, i, first):
                    pe.wait_ge(q["qn_done"], n * NN + i + 1)
                    if i == 0 and not first:
                        pe.wait_ge(q["tev_done"], n * NN - 1)
                    if i in (1, 3):
                        pe.wait_ge(q["tev_done"], n * NN + i)
                    if i == 2 and not first:
                        pe.wait_ge(q["ptev_done"], n * 2 - 1)
                    if i == 4:
                        pe.wait_ge(q["tev_done"], n * NN + 2)
                        if not first:
                            pe.wait_ge(q["ptev_done"], n * 2)
                    if i == 5:
                        pe.wait_ge(q["tev_done"], n * NN + 4)
                    bank = turns[TURN_BANK[i]]
                    for h in range(4):
                        out = bank[:, h * P:(h + 1) * P]
                        if CHUNKS[i][0] == "q":
                            out = bank[:].rearrange("p (g b h s) -> p g h b s", g=2, b=2, h=2)[:, h // 2, h % 2]
                        last = T.transpose(out, qn[:, i % 2, h * D:(h + 1) * D], k["ident"][:])
                    last.then_inc(q["turned"], 1)

                def scores(n, h, par, first):
                    pe.wait_ge(q["tev_done"], n * NN + (h + 1) * NN // 2)
                    if not (first and h == 0):
                        pe.wait_ge(q["sub_done"], n * 2 + h)
                    for g in range(GH):
                        kv = h * GH + g
                        for b in range(2):
                            rows = slice(b * SEQ, (b + 1) * SEQ)
                            last = T.matmul(sp_[:, (g * 2 + b) * SEQ:(g * 2 + b + 1) * SEQ], qkT[:, par, 2 * kv + b, :],
                                            qkT[:, par, HEADS + kv, rows], start=True, stop=True)
                    last.then_inc(q["sc_done"], 1)

                def turn_p(n, h, alone):
                    pe.wait_ge(q["pn_done"], n * 2 + h + 1)
                    if h == 0 or alone:
                        pe.wait_ge(q["tev_done"], n * NN + NN)
                    else:
                        pe.wait_ge(q["tev_done"], n * NN + NN + 2)
                    for g in range(GH):
                        last = T.transpose(turns[PROBS_BANK[h]][:, g * P:(g + 1) * P], ex[:, h, g * P:(g + 1) * P], k["ident"][:])
                    last.then_inc(q["pt_done"], 1)

                def attend(n, h, par, first):
                    pe.wait_ge(q["ptev_done"], n * 2 + h + 1)
                    pe.wait_ge(q["vev_done"], n * NK + NK)
                    if not (first and h == 0):
                        pe.wait_ge(q["q1_done"], n * 2 + h)
                    for g in range(GH):
                        kv = h * GH + g
                        for b in range(2):
                            rows = slice(b * SEQ, (b + 1) * SEQ)
                            last = T.matmul(op[:, b, g * P:(g + 1) * P], v[rows, par, kv * D:(kv + 1) * D], pT[rows, h, g, :],
                                            start=True, stop=True)
                    last.then_inc(q["pv_done"], 1)

                def output(n):
                    if cross and isinstance(n, int) and n == 0:
                        weights.ready(pe, NN + 3)
                    pe.wait_ge(q["cat_done"], n * 2 + 2)
                    pe.wait_ge(q["vev_done"], n * NK + 2 * NK if not (isinstance(n, int) and n == TILES - 1) else TILES * NK)
                    for hd in range(HEADS):
                        for part in range(2):
                            last = T.matmul(proj[OUT_BANK][:, 0:E], cat[:, hd // (2 * GH), hd % (2 * GH), :], (p_hi, p_lo)[part][:, hd, :],
                                            start=hd == 0 and part == 0, stop=hd == HEADS - 1 and part == 1)
                    last.then_inc(q["y_done"], 1)

                def ahead(n, par, first):
                    project(n, 0, par, first)
                    project(n, 1, par, first)
                    for i in range(2, NC):
                        turn(n, i - 2, first)
                        project(n, i, par, first)

                def both(n, par, first):
                    m, mp = n + 1, 1 - par
                    scores(n, 0, par, first)
                    project(m, 0, mp, False)
                    project(m, 1, mp, False)
                    scores(n, 1, par, first)
                    if not first:
                        output(n - 1)
                    project(m, 2, mp, False)
                    turn(m, 0, False)
                    project(m, 3, mp, False)
                    turn_p(n, 0, False)
                    project(m, 4, mp, False)
                    turn(m, 1, False)
                    attend(n, 0, par, first)
                    project(m, 5, mp, False)
                    turn(m, 2, False)
                    turn_p(n, 1, False)
                    project(m, 6, mp, False)
                    attend(n, 1, par, first)
                    turn(m, 3, False)
                    project(m, 7, mp, False)
                    turn(m, 4, False)
                    turn(m, 5, False)

                def alone(n, par):
                    scores(n, 0, par, False)
                    scores(n, 1, par, False)
                    output(n - 1)
                    turn_p(n, 0, True)
                    attend(n, 0, par, False)
                    turn_p(n, 1, True)
                    attend(n, 1, par, False)

                run(pe, ahead, both, alone, output)


def moe(nc, t, k):
    with phase_semaphores(nc) as take, ExitStack() as c:
        def sb(name, shape, dt=F32):
            return c.enter_context(nc.sbuf_tensor("m_" + name, shape, dt))

        def ps(name):
            return c.enter_context(nc.psum_tensor("m_" + name, [P, 512], F32))

        def sem(name):
            return take("m_" + name)

        N, NE, X = ST * P, EXPERTS + 1, EXPERTS
        UNITS = NE * GROUPS
        MATS = (("w1", "L1_W1"), ("wg", "L1_Wg"), ("w2", "L1_W2"))
        raw = sb("raw", [P, 2, len(MATS), KT * E])
        w_hi, w_lo = sb("w_hi", [P, 2, len(MATS), KT, E], F32R), sb("w_lo", [P, 2, len(MATS), KT, E], F32R)
        gw, gb, eb = sb("gw", [P, KT, X]), sb("gb", [P, X]), sb("eb", [P, X])
        earlier = sb("earlier", [P, X, X])
        xn, xnT = sb("xn", [P, GROUPS, ST, E]), sb("xnT", [P, KT, N])
        xT_hi, xT_lo = sb("xT_hi", [P, KT, TOK], F32R), sb("xT_lo", [P, KT, TOK], F32R)
        lg, pr, bp = sb("lg", [P, TILES, X]), sb("pr", [P, TILES, X]), sb("bp", [P, TILES, X])
        mx, sm = sb("mx", [P, TILES]), sb("sm", [P, TILES])
        gt, eq = sb("gt", [P, TILES, X * X]), sb("eq", [P, TILES, X * X])
        rank = sb("rank", [P, TILES, X])
        we = sb("we", [P, TILES, NE])
        silu, h = sb("silu", [P, 2, N]), sb("h", [P, KT, N])
        h_hi, h_lo = sb("h_hi", [P, 2, KT, N], F32R), sb("h_lo", [P, 2, KT, N], F32R)
        ln = LayerNorm(nc, c, take, "m_ln", k)
        ap_, gp = [ps("a0"), ps("a1")], [ps("g0"), ps("g1")]
        yp = [ps("y0"), ps("y1")]
        tp, lp = yp, ps("lp")
        names = ("loaded", "gates_loaded", "raw_loaded0", "raw_loaded1", "w_hi_done", "w_lo_done", "normed", "turned", "xnT_done",
                 "xhi_done", "xlo_done", "lg_done", "lb_done", "mx_done", "sub_done", "exp_done", "sm_done", "rec_done",
                 "pr_done", "bp_done", "gt_done", "eq_done", "eqm_done", "sum_done", "rank_done", "sel_done", "ws_done", "wr_done",
                 "wg_done", "we_done", "ag_done", "silu_done", "h_done", "hhi_done", "hlo_done", "y_done", "x_done",
                 "ones_done", "earlier_done")
        q = {n: sem(n) for n in names}
        raw_loaded = [q["raw_loaded0"], q["raw_loaded1"]]

        def run(eng, first_product, second_product):
            first_product(0, 0, True)
            for n in range(1, 4):
                first_product(n, n, True)
                second_product(n - 1, n - 1)
            with eng.Fori(1, UNITS // 4 - 1) as i:
                for u in range(4):
                    first_product(i * 4 + u, u, False)
                    second_product(i * 4 + (u - 1), (u - 1) % 4)
            for n in range(UNITS - 4, UNITS):
                first_product(n, n % 4, False)
                second_product(n - 1, (n - 1) % 4)
            second_product(UNITS - 1, 3)

        def splits_next(n, u, first):
            return u % 2 == 0 and not (first and u == 0) and not (isinstance(n, int) and n >= UNITS - GROUPS)

        with nc.Block() as block:
            @block.sync
            def _(sp):
                def load(e, par):
                    for m, (_, src) in enumerate(MATS):
                        flat = t[src].rearrange("x k f -> (x k) f")[bass.ds(e * E, E), :]
                        sp.dma_start(raw[:, par, m, :].rearrange("p (c f) -> p c f", c=KT),
                                     flat.rearrange("(c p) f -> p c f", p=P)).then_inc(raw_loaded[par], 16)

                load(0, 0)
                sp.dma_start(gw[:], t["L1_gate_w"].rearrange("(c p) x -> p c x", p=P)).then_inc(q["gates_loaded"], 16)
                for dst, src in ((gb, "L1_gate_b"), (eb, "L1_biases")):
                    sp.dma_start(dst[:], t[src].rearrange("(o n) -> o n", o=1).broadcast_to([P, X])).then_inc(q["loaded"], 16)
                load(1, 1)
                with sp.Fori(1, NE // 2) as i:
                    for par in range(2):
                        sp.wait_ge(q["w_lo_done"], (i * 2 + par - 1) * len(MATS))
                        load(i * 2 + par, par)

            @block.gpsimd
            def _(pool):
                def token_lows(s):
                    ln.on_pool(pool, s)
                    for c_ in range(KT):
                        pool.wait_ge(q["xhi_done"], s * KT + c_ + 1)
                        nc.gpsimd.tensor_tensor(xT_lo[:, c_, s * N:(s + 1) * N], xnT[:, c_, :],
                                                xT_hi[:, c_, s * N:(s + 1) * N].bitcast(F32), ALU.subtract).then_inc(q["xlo_done"], 1)

                def weight_lows(e, par):
                    for m in range(len(MATS)):
                        pool.wait_ge(q["w_hi_done"], e * len(MATS) + m + 1)
                        nc.gpsimd.tensor_tensor(w_lo[:, par, m].rearrange("p c f -> p (c f)"), raw[:, par, m, :],
                                                w_hi[:, par, m].rearrange("p c f -> p (c f)").bitcast(F32),
                                                ALU.subtract).then_inc(q["w_lo_done"], 1)

                def hidden_lows(n, u, first):
                    for f in range(KT):
                        pool.wait_ge(q["hhi_done"], n * KT + f + 1)
                        if f == 0 and not (first and u < 2):
                            pool.wait_ge(q["y_done"], n - 1)
                        nc.gpsimd.tensor_tensor(h_lo[:, u % 2, f, :], h[:, f, :], h_hi[:, u % 2, f, :].bitcast(F32),
                                                ALU.subtract).then_inc(q["hlo_done"], 1)
                    if splits_next(n, u, first):
                        weight_lows((n - u) // 2 + u // 2 + 1, (u // 2 + 1) % 2)

                nc.gpsimd.memset(earlier[:], 1.0).then_inc(q["ones_done"], 1)
                pool.wait_ge(q["ones_done"], 1)
                nc.gpsimd.affine_select(out=earlier[:], in_=earlier[:], compare_op=ALU.is_gt, fill=0.0, base=0,
                                        pattern=[[1, X], [-1, X]], channel_multiplier=0).then_inc(q["earlier_done"], 1)
                weight_lows(0, 0)
                token_lows(0)
                token_lows(1)
                weight_lows(1, 1)
                run(pool, hidden_lows, lambda n, u: None)

            @block.scalar
            def _(act):
                def tokens(s):
                    act.wait_ge(q["turned"], s + 1)
                    if s > 0:
                        act.wait_ge(q["lg_done"], s)
                        act.wait_ge(q["xlo_done"], s * KT)
                    for c_ in range(KT):
                        nc.scalar.activation(xnT[:, c_, :], tp[c_][:], ACT.Copy).then_inc(q["xnT_done"], 1)
                        nc.scalar.activation(xT_hi[:, c_, s * N:(s + 1) * N], tp[c_][:], ACT.Copy).then_inc(q["xhi_done"], 1)

                def weight_highs(e, par, first):
                    if first:
                        act.wait_ge(raw_loaded[par], 16 * len(MATS))
                    else:
                        act.wait_ge(raw_loaded[par], ((e - par) // 2 + 1) * (16 * len(MATS)))
                        act.wait_ge(q["y_done"], e * 2 - 2)
                    for m in range(len(MATS)):
                        nc.scalar.activation(w_hi[:, par, m].rearrange("p c f -> p (c f)"), raw[:, par, m, :],
                                             ACT.Copy).then_inc(q["w_hi_done"], 1)

                def silus(n, u, first):
                    for f in range(KT):
                        act.wait_ge(q["ag_done"], n * KT + f + 1)
                        if not (first and u == 0):
                            act.wait_ge(q["h_done"], n * KT + f - 1)
                        nc.scalar.activation(silu[:, f, :], ap_[f][:], ACT.Silu).then_inc(q["silu_done"], 1)
                    for f in range(KT):
                        act.wait_ge(q["h_done"], n * KT + f + 1)
                        if f == 0 and not (first and u < 2):
                            act.wait_ge(q["y_done"], n - 1)
                        nc.scalar.activation(h_hi[:, u % 2, f, :], h[:, f, :], ACT.Copy).then_inc(q["hhi_done"], 1)
                    if splits_next(n, u, first):
                        weight_highs((n - u) // 2 + u // 2 + 1, (u // 2 + 1) % 2, False)

                weight_highs(0, 0, True)
                tokens(0)
                tokens(1)
                weight_highs(1, 1, True)
                act.wait_ge(q["sub_done"], 1)
                nc.scalar.activation(lg[:], lg[:], ACT.Exp).then_inc(q["exp_done"], 1)
                run(act, silus, lambda n, u: None)

            @block.vector
            def _(dve):
                V = nc.vector

                def route():
                    dve.wait_ge(q["loaded"], 32)
                    dve.wait_ge(q["earlier_done"], 1)
                    dve.wait_ge(q["lg_done"], GROUPS)
                    V.tensor_tensor(lg[:], lp[:, 0:TILES * X].rearrange("p (j x) -> p j x", x=X), bcast(gb[:], 1, TILES), ALU.add).then_inc(q["lb_done"], 1)
                    dve.wait_ge(q["lb_done"], 1)
                    V.tensor_reduce(mx[:], lg[:], AX.X, ALU.max).then_inc(q["mx_done"], 1)
                    dve.wait_ge(q["mx_done"], 1)
                    V.tensor_tensor(lg[:], lg[:], bcast(mx[:], 2, X), ALU.subtract).then_inc(q["sub_done"], 1)
                    dve.wait_ge(q["exp_done"], 1)
                    V.tensor_reduce(sm[:], lg[:], AX.X, ALU.add).then_inc(q["sm_done"], 1)
                    dve.wait_ge(q["sm_done"], 1)
                    V.reciprocal(sm[:], sm[:]).then_inc(q["rec_done"], 1)
                    dve.wait_ge(q["rec_done"], 1)
                    V.tensor_tensor(pr[:], lg[:], bcast(sm[:], 2, X), ALU.mult).then_inc(q["pr_done"], 1)
                    dve.wait_ge(q["pr_done"], 1)
                    V.tensor_tensor(bp[:], pr[:], bcast(eb[:], 1, TILES), ALU.add).then_inc(q["bp_done"], 1)
                    dve.wait_ge(q["bp_done"], 1)
                    for j in range(TILES):
                        other, own = bcast(bp[:, j, :], 1, X), bcast(bp[:, j, :], 2, X)
                        V.tensor_tensor(gt[:, j, :].rearrange("p (e o) -> p e o", o=X), other, own, ALU.is_gt).then_inc(q["gt_done"], 1)
                        V.tensor_tensor(eq[:, j, :].rearrange("p (e o) -> p e o", o=X), other, own, ALU.is_equal).then_inc(q["eq_done"], 1)
                    dve.wait_ge(q["eq_done"], TILES)
                    V.tensor_tensor(eq[:], eq[:], bcast(earlier[:].rearrange("p e o -> p (e o)"), 1, TILES), ALU.mult).then_inc(q["eqm_done"], 1)
                    dve.wait_ge(q["eqm_done"], 1)
                    dve.wait_ge(q["gt_done"], TILES)
                    V.tensor_tensor(gt[:], gt[:], eq[:], ALU.add).then_inc(q["sum_done"], 1)
                    dve.wait_ge(q["sum_done"], 1)
                    V.tensor_reduce(rank[:].rearrange("p j x -> p (j x)"), gt[:].rearrange("p j (e o) -> p (j e) o", o=X), AX.X, ALU.add).then_inc(q["rank_done"], 1)
                    dve.wait_ge(q["rank_done"], 1)
                    V.scalar_tensor_tensor(rank[:], rank[:], TOP_K - 0.5, pr[:], ALU.is_lt, ALU.mult).then_inc(q["sel_done"], 1)
                    dve.wait_ge(q["sel_done"], 1)
                    V.tensor_reduce(sm[:], rank[:], AX.X, ALU.add).then_inc(q["ws_done"], 1)
                    dve.wait_ge(q["ws_done"], 1)
                    V.reciprocal(sm[:], sm[:]).then_inc(q["wr_done"], 1)
                    dve.wait_ge(q["wr_done"], 1)
                    V.tensor_scalar(sm[:], sm[:], k["gate"][:, 3:4], None, ALU.mult).then_inc(q["wg_done"], 1)
                    dve.wait_ge(q["wg_done"], 1)
                    V.tensor_scalar(we[:, :, 0], k["ones"][:, 0:TILES], k["gate"][:, 3:4], None, ALU.mult).then_inc(q["we_done"], 1)
                    V.tensor_tensor(we[:, :, 1:NE], rank[:], bcast(sm[:], 2, X), ALU.mult).then_inc(q["we_done"], 1)
                    dve.wait_ge(q["we_done"], 2)

                def product(n, u, first):
                    for f in range(KT):
                        dve.wait_ge(q["silu_done"], n * KT + f + 1)
                        if f == 0 and not (first and u == 0):
                            dve.wait_ge(q["hlo_done"], n * KT)
                        V.tensor_tensor(h[:, f, :], silu[:, f, :], gp[f][:], ALU.mult).then_inc(q["h_done"], 1)

                def add_x(n, u):
                    for j in range(ST):
                        if j == 0:
                            dve.wait_ge(q["y_done"], n + 1)
                        row = (u % 2) * ST + j
                        tile = k["x"][:, row, :]
                        at = we[:].rearrange("p n x -> p (n x)")[:, bass.ds((n - u % 2) // 2 + row * NE, 1)]
                        V.scalar_tensor_tensor(tile, yp[j // 2][:, (j % 2) * E:(j % 2 + 1) * E], at, tile,
                                               ALU.mult, ALU.add).then_inc(q["x_done"], 1)

                for s in range(GROUPS):
                    ln.on_vector(dve, s, lambda j: k["x"][:, s * ST + j, :], lambda j: xn[:, s, j, :], q["normed"])
                route()
                run(dve, product, add_x)

            @block.tensor
            def _(pe):
                def tokens(s):
                    for j in range(ST):
                        pe.wait_ge(q["normed"], s * ST + j + 1)
                        for c_ in range(KT):
                            if j == 0 and s > 0:
                                pe.wait_ge(q["xhi_done"], s * KT)
                            last = nc.tensor.transpose(tp[c_][:, j * P:(j + 1) * P], xn[:, s, j, c_ * P:(c_ + 1) * P], k["ident"][:])
                    last.then_inc(q["turned"], 1)

                def logits(s):
                    if s == 0:
                        pe.wait_ge(q["gates_loaded"], 16)
                    pe.wait_ge(q["xnT_done"], (s + 1) * KT)
                    for j in range(ST):
                        for c_ in range(KT):
                            row = s * ST + j
                            last = nc.tensor.matmul(lp[:, row * X:(row + 1) * X], xnT[:, c_, j * P:(j + 1) * P], gw[:, c_, :],
                                                    start=c_ == 0, stop=c_ == KT - 1)
                    last.then_inc(q["lg_done"], 1)

                def first_products(n, u, first):
                    s, par = u % 2, u // 2
                    if first and s == u:
                        pe.wait_ge(q["xlo_done"], (s + 1) * KT)
                    if s == 0:
                        pe.wait_ge(q["w_lo_done"], ((n - u) // 2 + par + 1) * len(MATS))
                    for f in range(KT):
                        if not (first and u == 0):
                            pe.wait_ge(q["h_done"], n * KT + f - 1)
                        for m, dst in enumerate((ap_[f], gp[f])):
                            for c_ in range(KT):
                                at = (slice(None), par, m, c_, slice(f * P, (f + 1) * P))
                                hi, lo = xT_hi[:, c_, s * N:(s + 1) * N], xT_lo[:, c_, s * N:(s + 1) * N]
                                nc.tensor.matmul(dst[:], w_hi[at], hi, start=c_ == 0, stop=False)
                                nc.tensor.matmul(dst[:], w_hi[at], lo, start=False, stop=False)
                                last = nc.tensor.matmul(dst[:], w_lo[at], hi, start=False, stop=c_ == KT - 1)
                        last.then_inc(q["ag_done"], 1)

                def second_product(n, u):
                    par = u // 2
                    pe.wait_ge(q["hlo_done"], n * KT + KT)
                    if not (isinstance(n, int) and n == 0):
                        pe.wait_ge(q["x_done"], n * ST)
                    for j in range(ST):
                        out = yp[j // 2][:, (j % 2) * E:(j % 2 + 1) * E]
                        for f in range(KT):
                            hi, lo = (part[:, u % 2, f, j * P:(j + 1) * P] for part in (h_hi, h_lo))
                            nc.tensor.matmul(out, hi, w_hi[:, par, 2, f, :], start=f == 0, stop=False)
                            nc.tensor.matmul(out, hi, w_lo[:, par, 2, f, :], start=False, stop=False)
                            last = nc.tensor.matmul(out, lo, w_hi[:, par, 2, f, :], start=False, stop=f == KT - 1)
                    last.then_inc(q["y_done"], 1)

                tokens(0)
                logits(0)
                tokens(1)
                logits(1)
                run(pe, first_products, second_product)


def kernel(**a):
    import numpy as np
    import concourse.bacc as bacc
    from concourse.bass_utils import run_bass_kernel_spmd

    def arr(name):
        return np.ascontiguousarray(a[name])

    def columns(name):
        return np.ascontiguousarray(np.asarray(a[name]).reshape(-1, P).T)

    def turned(name):
        return np.ascontiguousarray(np.asarray(a[name]).T)

    ins = {
        "x": arr("x").reshape(TOK, E),
        "ctxT": np.ascontiguousarray(arr("ctx_2048").reshape(TOK, E).T),
        "mask": arr("mask_BxSxS2_ff0").reshape(TOK, SEQ),
        "g_xattn": arr("g_xattn"), "g_ffn": arr("g_ffn"),
        "L0_WqT": turned("L0_xattn_Wq"), "L0_WkT": turned("L0_xattn_Wk"), "L0_WvT": turned("L0_xattn_Wv"),
        "L0_bq": columns("L0_xattn_bq"), "L0_bk": columns("L0_xattn_bk"), "L0_bv": arr("L0_xattn_bv"),
        "L0_gateT": turned("L0_ffn_w_gate"), "L0_upT": turned("L0_ffn_w_up"), "L0_downT": turned("L0_ffn_w_down"),
        "L0_lnw": arr("L0_ffn_ln_weight"),
        "L1_wqT": turned("L1_xattn_wq"), "L1_wkT": turned("L1_xattn_wk"), "L1_wvT": turned("L1_xattn_wv"),
        "L1_wqxT": turned("L1_xattn_wqx"), "L1_wkvxT": turned("L1_xattn_w_kv_x"), "L1_wprojT": turned("L1_xattn_wproj"),
        "L1_smoothT": np.ascontiguousarray(arr("L1_xattn_proj_smooth").reshape(2 * HEADS, D).T),
        "L1_gate_w": arr("L1_ffn_gate_w"), "L1_gate_b": arr("L1_ffn_gate_b"), "L1_biases": arr("L1_ffn_biases"),
        "L1_W1": np.concatenate([arr("L1_ffn_Ws1")[None], arr("L1_ffn_W1")]),
        "L1_Wg": np.concatenate([arr("L1_ffn_Wsg")[None], arr("L1_ffn_Wg")]),
        "L1_W2": np.concatenate([arr("L1_ffn_Ws2")[None], arr("L1_ffn_W2")]),
    }
    for n in ("ln_w", "ln_b", "q_in_scale", "k_in_scale", "v_in_scale", "qx_in_scale"):
        ins["L1_" + n] = columns("L1_xattn_" + n)
    for n in ("qln_w", "qln_b", "kln_w", "kln_b",
              "qxln_w", "qxln_b", "kxln_w", "kxln_b"):
        ins["L1_" + n] = arr("L1_xattn_" + n)
    for n in ("wq_scale", "wk_scale", "wv_scale", "wqx_scale", "proj_in_scale", "proj_w_scale"):
        ins["L1_" + n] = arr("L1_xattn_" + n).reshape(1)

    nc = bacc.Bacc("TRN2", target_bir_lowering=False, num_devices=1)
    t = {n: nc.dram_tensor("in_" + n, v.shape, mybir.dt.from_np(v.dtype), kind="ExternalInput").ap() for n, v in ins.items()}
    t["out"] = nc.dram_tensor("out_x", (TOK, E), F32, kind="ExternalOutput").ap()
    flamingo_program(nc, t)
    r = run_bass_kernel_spmd(nc, [{"in_" + n: v for n, v in ins.items()}], core_ids=[0])
    return np.asarray(r.results[0]["out_x"]).reshape(BATCH, SEQ, E)
```
